# Optimizing a Trainium2 kernel written in Bass

```python
import numpy as np
import jax
import jax.numpy as jnp

def _softmax(x, axis=-1):
    return jax.nn.softmax(x, axis=axis)

def _gelu(x):
    return jax.nn.gelu(x, approximate=True)

def _silu(x):
    return jax.nn.silu(x)

def _sigmoid(x):
    return jax.nn.sigmoid(x)

def _layernorm(x, axis=-1, eps=1e-05):
    m = jnp.mean(x, axis=axis, keepdims=True)
    v = jnp.var(x, axis=axis, keepdims=True)
    return (x - m) / jnp.sqrt(v + eps)

def _scatter_add(tgt, idx, src, axis=0):
    return tgt.at[idx].add(src)

def _segment_sum(src, seg, n):
    return jax.ops.segment_sum(src, seg, n)
kernel_name = 'mk_gnn_ffn_d2_gnn_r32_190703'

def setup_inputs(seed: int=0):
    np.random.seed(seed)
    _w = jnp.asarray

    def _rec_inputs():
        import jax
        import jax.numpy as jnp
        _gk = jax.random.key(seed)
        x = -0.0003713 + 1 * jax.random.normal(jax.random.fold_in(_gk, 1), (3125, 256), jnp.float32)
        src = jax.random.randint(jax.random.fold_in(_gk, 2), (50000,), 0, 3125, jnp.int32)
        dst = jax.random.randint(jax.random.fold_in(_gk, 3), (50000,), 0, 3125, jnp.int32)
        _o = jnp.argsort(dst, stable=True)
        src = src[_o]
        dst = dst[_o]
        return (x, src, dst)
    x, src, dst = _rec_inputs()

    def _L0_gnn_setup():
        import jax, jax.numpy as jnp
        import numpy as np
        N_NODES = 50000
        N_EDGES = 25000
        IN_DIM = 256
        OUT_DIM = 64
        HEADS = 4
        NEG_SLOPE = 0.2
        key = jax.random.key(seed)
        k_x, k_e, k_w, k_as, k_ad = jax.random.split(key, 5)
        x = jax.random.normal(k_x, (N_NODES, IN_DIM), dtype=jnp.float32)
        edge_index = jax.random.randint(k_e, (2, N_EDGES), 0, N_NODES, dtype=jnp.int64)
        W = jax.random.normal(k_w, (IN_DIM, HEADS * OUT_DIM), dtype=jnp.float32) / np.sqrt(IN_DIM)
        att_src = jax.random.normal(k_as, (HEADS, OUT_DIM), dtype=jnp.float32) / np.sqrt(OUT_DIM)
        att_dst = jax.random.normal(k_ad, (HEADS, OUT_DIM), dtype=jnp.float32) / np.sqrt(OUT_DIM)
        bias = jnp.zeros((HEADS * OUT_DIM,), dtype=jnp.float32)
        return {'x': x, 'edge_index': edge_index, 'W': W, 'att_src': att_src, 'att_dst': att_dst, 'bias': bias}
    _L0_gnn_all = _L0_gnn_setup()
    _L0_gnn_in = {k: v for k, v in _L0_gnn_all.items() if k in ('W', 'att_src', 'att_dst', 'bias')}
    del _L0_gnn_all

    def _L0_ffn_setup():
        import jax, jax.numpy as jnp
        import numpy as np
        C = 256
        HID = 1024
        E = 8
        TEMP = 1.0
        key = jax.random.key(seed)
        ks = jax.random.split(key, 7)
        x = jax.random.normal(ks[0], (8, 512, C), dtype=jnp.float32)
        W1 = jax.random.normal(ks[1], (C, HID), dtype=jnp.float32) * 0.02
        b1 = jnp.zeros((HID,), dtype=jnp.float32)
        Wg = jax.random.normal(ks[2], (HID, E), dtype=jnp.float32) * 0.02
        bg = jnp.zeros((E,), dtype=jnp.float32)
        Wd = jax.random.normal(ks[3], (E, HID, C), dtype=jnp.float32) * 0.02
        bd = jnp.zeros((E, C), dtype=jnp.float32)
        return {'x': x, 'W1': W1, 'b1': b1, 'Wg': Wg, 'bg': bg, 'Wd': Wd, 'bd': bd}
    _L0_ffn_all = _L0_ffn_setup()
    _L0_ffn_in = {k: v for k, v in _L0_ffn_all.items() if k in ('W1', 'b1', 'Wg', 'bg', 'Wd', 'bd')}
    del _L0_ffn_all

    def _L1_gnn_setup():
        import jax, jax.numpy as jnp
        import numpy as np
        N_NODES = 3125
        N_EDGES = 100000
        IN_FEAT = 256
        OUT_FEAT = 256
        EPS = 1e-12
        key = jax.random.key(seed)
        k1, k2, k3, k4, k5 = jax.random.split(key, 5)
        x = jax.random.normal(k1, (N_NODES, IN_FEAT), dtype=jnp.float32)
        W = jax.random.normal(k2, (IN_FEAT, OUT_FEAT), dtype=jnp.float32) / np.sqrt(IN_FEAT)
        b = jax.random.normal(k3, (OUT_FEAT,), dtype=jnp.float32) * 0.01
        src = jax.random.randint(k4, (N_EDGES,), 0, N_NODES, dtype=jnp.int32)
        dst = jax.random.randint(k5, (N_EDGES,), 0, N_NODES, dtype=jnp.int32)
        return {'x': x, 'W': W, 'b': b, 'src': src, 'dst': dst}
    _L1_gnn_all = _L1_gnn_setup()
    _L1_gnn_in = {k: v for k, v in _L1_gnn_all.items() if k in ('W', 'b')}
    del _L1_gnn_all

    def _L1_ffn_setup():
        import jax, jax.numpy as jnp
        import numpy as np
        BN_EPS = 0.001

        def _bn(h, g, b, m, v):
            return g * (h - m) * jax.lax.rsqrt(v + BN_EPS) + b
        key = jax.random.key(seed)
        ks = jax.random.split(key, 8)
        B, F, Df = (256, 64, 256)
        E, H, D = (8, 256, 256)
        s1 = 1.0 / np.sqrt(Df)
        s2 = 1.0 / np.sqrt(H)
        return {'x': jax.random.normal(ks[0], (B, F, Df), jnp.float32), 'Wr': jax.random.normal(ks[1], (Df, E), jnp.float32) * s1, 'br': jnp.zeros((E,), jnp.float32), 'W1': jax.random.normal(ks[2], (E, Df, H), jnp.float32) * s1, 'b1': jnp.zeros((E, H), jnp.float32), 'g1': jnp.ones((E, H), jnp.float32), 'be1': jnp.zeros((E, H), jnp.float32), 'm1': jnp.zeros((E, H), jnp.float32), 'v1': jnp.ones((E, H), jnp.float32), 'W2': jax.random.normal(ks[3], (E, H, H), jnp.float32) * s2, 'b2': jnp.zeros((E, H), jnp.float32), 'g2': jnp.ones((E, H), jnp.float32), 'be2': jnp.zeros((E, H), jnp.float32), 'm2': jnp.zeros((E, H), jnp.float32), 'v2': jnp.ones((E, H), jnp.float32), 'Wo': jax.random.normal(ks[4], (E, H, D), jnp.float32) * s2, 'bo': jnp.zeros((E, D), jnp.float32)}
    _L1_ffn_all = _L1_ffn_setup()
    _L1_ffn_in = {k: v for k, v in _L1_ffn_all.items() if k in ('Wr', 'br', 'W1', 'b1', 'g1', 'be1', 'm1', 'v1', 'W2', 'b2', 'g2', 'be2', 'm2', 'v2', 'Wo', 'bo')}
    del _L1_ffn_all
    return {'x': x, 'src': src, 'dst': dst, 'L0_gnn_W': _L0_gnn_in['W'], 'L0_gnn_att_src': _L0_gnn_in['att_src'], 'L0_gnn_att_dst': _L0_gnn_in['att_dst'], 'L0_gnn_bias': _L0_gnn_in['bias'], 'L0_ffn_W1': _L0_ffn_in['W1'], 'L0_ffn_b1': _L0_ffn_in['b1'], 'L0_ffn_Wg': _L0_ffn_in['Wg'], 'L0_ffn_bg': _L0_ffn_in['bg'], 'L0_ffn_Wd': _L0_ffn_in['Wd'], 'L0_ffn_bd': _L0_ffn_in['bd'], 'L1_gnn_W': _L1_gnn_in['W'], 'L1_gnn_b': _L1_gnn_in['b'], 'L1_ffn_Wr': _L1_ffn_in['Wr'], 'L1_ffn_br': _L1_ffn_in['br'], 'L1_ffn_W1': _L1_ffn_in['W1'], 'L1_ffn_b1': _L1_ffn_in['b1'], 'L1_ffn_g1': _L1_ffn_in['g1'], 'L1_ffn_be1': _L1_ffn_in['be1'], 'L1_ffn_m1': _L1_ffn_in['m1'], 'L1_ffn_v1': _L1_ffn_in['v1'], 'L1_ffn_W2': _L1_ffn_in['W2'], 'L1_ffn_b2': _L1_ffn_in['b2'], 'L1_ffn_g2': _L1_ffn_in['g2'], 'L1_ffn_be2': _L1_ffn_in['be2'], 'L1_ffn_m2': _L1_ffn_in['m2'], 'L1_ffn_v2': _L1_ffn_in['v2'], 'L1_ffn_Wo': _L1_ffn_in['Wo'], 'L1_ffn_bo': _L1_ffn_in['bo']}

def reference(x, src, dst, L0_gnn_W, L0_gnn_att_src, L0_gnn_att_dst, L0_gnn_bias, L0_ffn_W1, L0_ffn_b1, L0_ffn_Wg, L0_ffn_bg, L0_ffn_Wd, L0_ffn_bd, L1_gnn_W, L1_gnn_b, L1_ffn_Wr, L1_ffn_br, L1_ffn_W1, L1_ffn_b1, L1_ffn_g1, L1_ffn_be1, L1_ffn_m1, L1_ffn_v1, L1_ffn_W2, L1_ffn_b2, L1_ffn_g2, L1_ffn_be2, L1_ffn_m2, L1_ffn_v2, L1_ffn_Wo, L1_ffn_bo):
    import jax
    import jax.numpy as jnp

    def _L0_gnn_ref(x, edge_index, W, att_src, att_dst, bias):
        import jax, jax.numpy as jnp
        import numpy as np
        N_NODES = 50000
        N_EDGES = 25000
        IN_DIM = 256
        OUT_DIM = 64
        HEADS = 4
        NEG_SLOPE = 0.2
        N = x.shape[0]
        H, C = att_src.shape
        loop = jnp.arange(N, dtype=edge_index.dtype)
        src = jnp.concatenate([edge_index[0], loop])
        dst = jnp.concatenate([edge_index[1], loop])
        xh = (x @ W).reshape(N, H, C)
        a_src = jnp.einsum('nhc,hc->nh', xh, att_src)
        a_dst = jnp.einsum('nhc,hc->nh', xh, att_dst)
        logits = jax.nn.leaky_relu(a_src[src] + a_dst[dst], NEG_SLOPE)
        seg_max = jax.ops.segment_max(logits, dst, num_segments=N)
        e = jnp.exp(logits - seg_max[dst])
        seg_sum = jax.ops.segment_sum(e, dst, num_segments=N)
        alpha = e / seg_sum[dst]
        msgs = alpha[:, :, None] * xh[src]
        out = jax.ops.segment_sum(msgs, dst, num_segments=N)
        out = out.reshape(N, H * C) + bias
        return out

    def _L0_ffn_ref(x, W1, b1, Wg, bg, Wd, bd):
        import jax, jax.numpy as jnp
        import numpy as np
        C = 256
        HID = 1024
        E = 8
        TEMP = 1.0
        orig_shape = x.shape
        xf = x.reshape(-1, orig_shape[-1])
        H = jax.nn.gelu(xf @ W1 + b1, approximate=False)
        probs = jax.nn.softmax((H @ Wg + bg) / TEMP, axis=-1)
        assign = jnp.argmax(probs, axis=-1)
        out = jnp.zeros_like(xf)
        for e in range(Wd.shape[0]):
            y = H @ Wd[e] + bd[e]
            sel = (assign == e)[:, None]
            out = out + jnp.where(sel, probs[:, e:e + 1] * y, 0.0)
        return out.reshape(orig_shape)

    def _L1_gnn_ref(x, W, b, src, dst):
        import jax, jax.numpy as jnp
        import numpy as np
        N_NODES = 3125
        N_EDGES = 100000
        IN_FEAT = 256
        OUT_FEAT = 256
        EPS = 1e-12
        N = x.shape[0]
        ones = jnp.ones(src.shape[0], dtype=x.dtype)
        deg_out = jnp.maximum(jax.ops.segment_sum(ones, src, num_segments=N), 1.0)
        deg_in = jnp.maximum(jax.ops.segment_sum(ones, dst, num_segments=N), 1.0)
        h = x * jax.lax.rsqrt(deg_out)[:, None]
        agg = jax.ops.segment_sum(h[src], dst, num_segments=N)
        h = agg * jax.lax.rsqrt(deg_in)[:, None]
        h = h @ W + b
        h = jax.nn.relu(h)
        nrm = jnp.maximum(jnp.linalg.norm(h, axis=1, keepdims=True), EPS)
        return h / nrm

    def _L1_ffn_ref(x, Wr, br, W1, b1, g1, be1, m1, v1, W2, b2, g2, be2, m2, v2, Wo, bo):
        import jax, jax.numpy as jnp
        import numpy as np
        BN_EPS = 0.001

        def _bn(h, g, b, m, v):
            return g * (h - m) * jax.lax.rsqrt(v + BN_EPS) + b
        feat = jnp.mean(x, axis=0)
        w = jax.nn.softmax(feat @ Wr + br, axis=-1)
        h = jnp.einsum('bfd,edh->bfeh', x, W1) + b1
        h = jax.nn.relu(_bn(h, g1, be1, m1, v1))
        h = jnp.einsum('bfeh,ehk->bfek', h, W2) + b2
        h = jax.nn.relu(_bn(h, g2, be2, m2, v2))
        y = jnp.einsum('bfeh,ehd->bfed', h, Wo) + bo
        return jnp.einsum('bfed,fe->bfd', y, w)
    edge_index = jnp.stack([src, dst])
    x = x + _L0_gnn_ref(_layernorm(x, axis=-1), edge_index, L0_gnn_W, L0_gnn_att_src, L0_gnn_att_dst, L0_gnn_bias)
    x = x + _L0_ffn_ref(_layernorm(x, axis=-1)[None], L0_ffn_W1, L0_ffn_b1, L0_ffn_Wg, L0_ffn_bg, L0_ffn_Wd, L0_ffn_bd)[0]
    x = x + _L1_gnn_ref(_layernorm(x, axis=-1), L1_gnn_W, L1_gnn_b, src, dst)
    x = x + _L1_ffn_ref(_layernorm(x, axis=-1)[None], L1_ffn_Wr, L1_ffn_br, L1_ffn_W1, L1_ffn_b1, L1_ffn_g1, L1_ffn_be1, L1_ffn_m1, L1_ffn_v1, L1_ffn_W2, L1_ffn_b2, L1_ffn_g2, L1_ffn_be2, L1_ffn_m2, L1_ffn_v2, L1_ffn_Wo, L1_ffn_bo)[0]
    return x

_drawn_inputs = setup_inputs


def setup_inputs(seed=0):
    import zlib

    import numpy as np

    out = dict(_drawn_inputs(seed))
    spreads = {'L0_gnn_bias': (0.0, 0.1),
     'L0_ffn_b1': (0.0, 0.603),
     'L0_ffn_bg': (0.0, 0.404),
     'L0_ffn_bd': (0.0, 0.588),
     'L1_ffn_br': (0.0, 0.53),
     'L1_ffn_b1': (0.0, 0.325),
     'L1_ffn_g1': (1.0, 0.2),
     'L1_ffn_be1': (0.0, 0.353),
     'L1_ffn_m1': (0.0, 0.333),
     'L1_ffn_v1': (1.0, 0.6),
     'L1_ffn_b2': (0.0, 0.1),
     'L1_ffn_g2': (1.0, 0.2),
     'L1_ffn_be2': (0.0, 0.304),
     'L1_ffn_m2': (0.0, 0.1),
     'L1_ffn_v2': (1.0, 0.6),
     'L1_ffn_bo': (0.0, 0.1)}
    factors = {'L0_ffn_W1': 2.762, 'L0_ffn_Wg': 3.009, 'L0_ffn_Wd': 3.377, 'L1_gnn_b': 35.717}
    for name, (base, spread) in spreads.items():
        noise = np.random.default_rng([zlib.crc32(name.encode()), seed]).standard_normal(out[name].shape)
        drawn = base * np.exp(spread * noise) if base else spread * noise
        out[name] = jnp.asarray(drawn.astype(out[name].dtype))
    for name, factor in factors.items():
        out[name] = (out[name] * factor).astype(out[name].dtype)
    return out
```

```python
from contextlib import ExitStack

import concourse.bass as bass
from concourse import mybir

F32 = mybir.dt.float32
BF16 = mybir.dt.bfloat16
I32 = mybir.dt.int32
ALU = mybir.AluOpType
ACT = mybir.ActivationFunctionType
AX = mybir.AxisListType.X
RMAX = bass.bass_isa.ReduceOp.max

PT = 125
SLOTS = 17
CHUNKS = ((0, 6), (6, 12), (12, 17))
NCH = len(CHUNKS)
WIN = SLOTS * 128
BIG = 65536.0
MAGIC = 12582912.0
EPS_LN = 1e-5
EPS_BN = 1e-3
EPS_NORM = 1e-12
SLOPE = 0.2
NO_NODE = 1 << 20


class Chain:

    def __init__(self, eng, sem):
        self.eng, self.sem, self.n = eng, sem, 0

    def __call__(self, ins):
        self.n += 1
        ins.then_inc(self.sem, 1)
        self.eng.wait_ge(self.sem, self.n)

    def restart(self):
        self.eng.sem_clear(self.sem)
        self.n = 0


def one(ap, i, pat="p a c -> p (a c)"):
    return ap[:, bass.ds(i, 1)].rearrange(pat)


def two_block_gnn(nc, x, src, dst, g0_W, g0_as, g0_ad, g0_b, f0_W1, f0_b1, f0_Wg, f0_bg, f0_Wd, f0_bd,
                  g1_W, g1_b, f1_Wr, f1_br, f1_W1, f1_b1, f1_g1, f1_be1, f1_m1, f1_v1,
                  f1_W2, f1_b2, f1_g2, f1_be2, f1_m2, f1_v2, f1_Wo, f1_bo, out):
    N, C = x.shape
    E = src.shape[0]
    NT = N // PT
    HID = f0_W1.shape[1]
    NX = f0_Wd.shape[0]
    HEADS, HC = g0_as.shape
    KC = C // 128
    KH = HID // 128
    EC = E // PT
    EPT = EC // NT
    WA = C + 2 * HEADS
    TW = C + HEADS
    GW = TW + 4
    ROW = HID + C + 4
    REG = 26 * 128
    TMAX = 34
    UN = 5
    assert N % PT == 0 and E % PT == 0 and EC % NT == 0 and REG >= N + 128 and NT % UN == 0

    with ExitStack() as ctx:
        def sem(name, n=None):
            if n is None:
                return ctx.enter_context(nc.semaphore(name))
            return [ctx.enter_context(nc.semaphore(f"{name}{i}")) for i in range(n)]

        def allocator(c):
            return lambda name, shape, dt=F32: c.enter_context(nc.sbuf_tensor(name, shape, dt))

        def dram(name, shape, dt=F32):
            return nc.dram_tensor(name, shape, dt, kind="Internal").ap()

        sb = allocator(ctx)
        src_pad = dram("src_pad", (E + WIN,), I32)
        dst_pad = dram("dst_pad", (E + WIN,), I32)
        table0 = dram("table0", (N, TW))
        table1 = dram("table1", (N, C))
        x2_rows = dram("x2_rows", (N, C))
        rs_rows = dram("rs_rows", (N, 1))
        sorted_rows = dram("sorted_rows", (NX * REG + 128, ROW))

        ps = [ctx.enter_context(nc.psum_tensor(f"bank{i}", [128, 512], F32)) for i in range(8)]

        iota_c = sb("iota_c", [128, 128])
        iota_p = sb("iota_p", [128, 1])
        tile_lo = sb("tile_lo", [128, NT])
        ident = sb("ident", [128, 128])
        eps_ln = sb("eps_ln", [128, 1])
        eps_bn = sb("eps_bn", [128, 1])
        wtab = sb("wtab", [1, 2, NT + 1], I32)
        deg_in = sb("deg_in", [PT, NT])
        src_win = sb("src_win", [128, SLOTS], I32)
        idx = sb("idx", [128, SLOTS], I32)
        dst_win = sb("dst_win", [128, SLOTS], I32)
        dloc = sb("dloc", [128, SLOTS])
        OH = sb("OH", [128, SLOTS, PT])
        G = sb("G", [128, SLOTS, GW])
        st = sb("st", [128, 2, 6])
        mv = sb("mv", [128, 2, 2])
        std = sb("std", [128, 2])
        rstd = sb("rstd", [128, 2])
        xn = [sb(f"xn{i}", [128, C]) for i in range(2)]
        xT = [sb(f"xT{i}", [128, KC, 128]) for i in range(2)]
        cnt = sb("cnt", [128, NX])
        region8 = sb("region8", [128, NX])
        bn_rows = [sb("bn_rowsA", [128, 128]), sb("bn_rowsB", [32, 128])]

        v_chain = sem("v_chain")
        a_chain = sem("a_chain")
        p_chain = sem("p_chain")
        sink = sem("sink")

        def hold(eng, s, value):
            eng.wait_ge(s, value)
            eng.sem_inc(sink, 1)

        weights0 = ExitStack()
        sw = allocator(weights0)
        X = sw("X", [PT, NT, C])
        XH = sw("XH", [PT, NT, WA])
        node = sw("node", [PT, NT, 2 * HEADS])
        e_self = sw("e_self", [PT, NT, HEADS])
        tile_row = sw("tile_row", [128, NT])
        shi = sw("shi", [PT, EC])
        slo = sw("slo", [PT, EC])
        iota_b = sw("iota_b", [128, 128], BF16)
        before = sw("before", [128, 128], BF16)
        ones_b = sw("ones_b", [128, 128], BF16)
        zeros_b = sw("zeros_b", [128, 128], BF16)
        fW1 = sw("fW1", [128, KC, HID])
        fWg = sw("fWg", [128, KH, NX])
        bias0 = sw("bias0", [128, C])
        b1row = sw("b1row", [128, HID])
        bgrow = sw("bgrow", [128, NX])

        s_const = sem("s_const")
        loaded0 = sem("loaded0")
        edges_in = sem("edges_in")
        weights_in = sem("weights_in")
        padded = sem("padded")
        var_all = sem("var_all")
        std_all = sem("std_all")
        wm_ready = sem("wm_ready")
        wm_all = sem("wm_all")
        gm_ready = sem("gm_ready")
        gm_all = sem("gm_all")
        self_z = sem("self_z")
        self_e = sem("self_e")
        xn0 = sem("xn0")
        xT0_done = sem("xT0_done")
        xT0_copied = sem("xT0_copied")
        xh_done = sem("xh_done")
        xh_copied = sem("xh_copied")
        t0_written = sem("t0_written")

        def free_after(i, j):
            return i * UN + (j + 2 if j == 0 else j + 1)

        with ExitStack() as c0, nc.Block() as block:
            s0 = allocator(c0)
            W0 = s0("W0", [128, KC, WA])
            att = s0("att", [128, 2, C])
            wtmp = s0("wtmp", [128, C])
            iota_d = s0("iota_d", [128, NT])
            edge_no = s0("edge_no", [PT, EC])
            no_edge = s0("no_edge", [1, WIN], I32)
            stA = s0("stA", [PT, NT, 6])
            mvA = s0("mvA", [PT, NT, 2])
            stdA = s0("stdA", [PT, NT])
            rstdA = s0("rstdA", [PT, NT])
            srci = s0("srci", [PT, EC], I32)
            dsti = s0("dsti", [PT, EC], I32)
            tmpe = s0("tmpe", [PT, EC])
            dhi = s0("dhi", [PT, EC])
            other = s0("other", [PT, NT, EC], BF16)
            bound = s0("bound", [PT, NT, EC])
            wmm = s0("wmm", [PT, 2, NT])
            wall = s0("wall", [PT, 2, NT])
            wa = s0("wa", [PT, NT])
            wb = s0("wb", [PT, NT])
            wc = s0("wc", [PT, NT + 1])
            ones_t = s0("ones_t", [PT, NT])
            gmax = s0("gmax", [PT, HEADS])
            gall = s0("gall", [PT, HEADS])
            sh = s0("sh", [PT, NT, HEADS])

            @block.gpsimd
            def _(pool):
                def iota(ap, pattern, cm):
                    pool.iota(ap, pattern, base=0, channel_multiplier=cm,
                              allow_small_or_imprecise_dtypes=True).then_inc(s_const, 1)
                iota(iota_c[:, :], [[1, 128]], 0)
                iota(iota_p[:, :], [[1, 1]], 1)
                iota(iota_d[:, :], [[1, NT]], 0)
                iota(tile_lo[:, :], [[PT, NT]], 0)
                iota(tile_row[:, :], [[PT, NT]], 1)
                iota(region8[:, :], [[REG, NX]], 0)
                iota(edge_no[:, :], [[1, EC]], EC)
                pool.memset(no_edge[:, :], -1).then_inc(s_const, 1)
                pool.wait_ge(wm_ready, 1)
                nc.gpsimd.partition_all_reduce(wall[:, :, :].rearrange("p a t -> p (a t)"),
                                               wmm[:, :, :].rearrange("p a t -> p (a t)"), PT, RMAX).then_inc(wm_all, 1)
                pool.wait_ge(gm_ready, 1)
                nc.gpsimd.partition_all_reduce(gall[:, :], gmax[:, :], PT, RMAX).then_inc(gm_all, 1)

            @block.sync
            def _(sp):
                sp.dma_start(X[:, :, :], x.rearrange("(t p) c -> p t c", p=PT)).then_inc(loaded0, 16)
                sp.dma_start(W0[:, :, 0:C], g0_W.rearrange("(k p) n -> p k n", p=128)).then_inc(loaded0, 16)
                sp.dma_start(att[:, 0, :], g0_as.rearrange("h c -> (h c)").partition_broadcast(128)).then_inc(loaded0, 16)
                sp.dma_start(att[:, 1, :], g0_ad.rearrange("h c -> (h c)").partition_broadcast(128)).then_inc(loaded0, 16)
                sp.dma_start(dsti[:, :], dst.rearrange("(p j) -> p j", p=PT)).then_inc(edges_in, 16)
                sp.dma_start(srci[:, :], src.rearrange("(p j) -> p j", p=PT)).then_inc(edges_in, 16)
                sp.dma_start(src_pad[0:E], src).then_inc(padded, 16)
                sp.dma_start(dst_pad[0:E], dst).then_inc(padded, 16)
                sp.dma_start(src_pad[E:E + WIN], src[0:WIN]).then_inc(padded, 16)
                sp.dma_start(fW1[:, :, :], f0_W1.rearrange("(k p) n -> p k n", p=128)).then_inc(weights_in, 16)
                sp.dma_start(fWg[:, :, :], f0_Wg.rearrange("(k p) n -> p k n", p=128)).then_inc(weights_in, 16)
                for tile, vec in ((bias0[:, :], g0_b), (b1row[:, :], f0_b1), (bgrow[:, :], f0_bg)):
                    sp.dma_start(tile, vec.partition_broadcast(128)).then_inc(weights_in, 16)
                for i, vec in enumerate((f1_b1, f1_g1, f1_be1, f1_m1, f1_v1, f1_b2, f1_g2, f1_be2, f1_m2, f1_v2)):
                    at = i * NX * KC
                    sp.dma_start(bn_rows[at // 128][at % 128:at % 128 + NX * KC, :],
                                 vec.rearrange("e (k p) -> (e k) p", p=128)).then_inc(weights_in, 16)
                sp.wait_ge(s_const, 8)
                sp.dma_start(dst_pad[E:E + WIN].rearrange("(a n) -> a n", a=1), no_edge[:, :]).then_inc(padded, 16)
                with sp.Fori(0, NT) as t:
                    sp.wait_ge(xh_copied, t + 3)
                    sp.dma_start(table0.rearrange("(t p) n -> t p n", p=PT)[bass.ds(t, 1), :, :].rearrange("a p n -> (a p) n"),
                                 XH[:, bass.ds(t, 1), 0:TW].rearrange("p a n -> p (a n)")).then_inc(t0_written, 16)
                sp.wait_ge(t0_written, 16 * NT)
                sp.wait_ge(padded, 64)
                sp.wait_ge(weights_in, 16 * 15)

            @block.scalar
            def _(act):
                act.wait_ge(var_all, 1)
                act.activation(stdA[:, :], mvA[:, :, 1], ACT.Sqrt, bias=eps_ln[0:PT, :]).then_inc(std_all, 1)
                with act.Fori(0, NT // UN) as i:
                    for j in range(UN):
                        act.wait_ge(xT0_done, i * UN + (j + 3))
                        hold(act, xh_done, free_after(i, j))
                        act.activation(xT[j % 2][:, :, 0:PT],
                                       ps[j % 2][:, 0:KC * PT].rearrange("p (k n) -> p k n", k=KC),
                                       ACT.Copy).then_inc(xT0_copied, 1)
                act.wait_ge(self_z, 1)
                act.activation(e_self[:, :, :], sh[:, :, :], ACT.Exp).then_inc(self_e, 1)

            @block.tensor
            def _(pe):
                pe.sem_inc(xT0_done, 2)
                pe.sem_inc(xh_done, 2)
                with pe.Fori(0, NT // UN) as i:
                    for j in range(UN):
                        hold(pe, xn0, i * UN + (j + 1))
                        for k in range(KC):
                            m = pe.transpose(ps[j % 2][:, k * PT:(k + 1) * PT], xn[j % 2][0:PT, k * 128:(k + 1) * 128],
                                             ident[0:PT, 0:PT])
                        m.then_inc(xT0_done, 1)
                        hold(pe, xT0_copied, i * UN + (j + 1))
                        hold(pe, xh_copied, free_after(i, j))
                        for k in range(KC):
                            m = pe.matmul(ps[2 + j % 2][0:PT, 0:WA], xT[j % 2][:, k, 0:PT], W0[:, k, :],
                                          start=(k == 0), stop=(k == KC - 1))
                        m.then_inc(xh_done, 1)

            @block.vector
            def _(v):
                chain = Chain(v, v_chain)
                v.sem_inc(xh_copied, 2)
                v.memset(eps_ln[:, :], EPS_LN)
                v.memset(eps_bn[:, :], EPS_BN)
                v.memset(ones_b[:, :], 1.0)
                v.memset(zeros_b[:, :], 0.0)
                v.memset(ones_t[:, :], 1.0)
                v.memset(G[:, :, TW:GW], 1.0)
                chain(v.memset(cnt[:, :], 0.0))
                v.wait_ge(s_const, 8)
                v.tensor_scalar(ident[:, :], iota_c[:, :], iota_p[:, :], None, ALU.is_equal)
                v.tensor_copy(iota_b[:, :], iota_c[:, :])
                chain(v.tensor_scalar(before[:, :], iota_c[:, :], iota_p[:, :], None, ALU.is_gt))
                v.wait_ge(loaded0, 64)
                for t in range(NT):
                    chain(v.bn_stats(stA[:, t, :], X[:, t, :]))
                for t in range(NT):
                    ins = v.bn_aggr(mvA[:, t, :], stA[:, t, :])
                    if t < NT - 1:
                        chain(ins)
                ins.then_inc(var_all, 1)
                for a in range(2):
                    for k in range(KC):
                        chain(v.tensor_tensor(wtmp[:, :], W0[:, k, 0:C], att[:, a, :], ALU.mult))
                        chain(v.tensor_reduce(W0[:, k, C + a * HEADS:C + (a + 1) * HEADS],
                                              wtmp[:, :].rearrange("p (h c) -> p h c", h=HEADS), AX, ALU.add))
                v.wait_ge(std_all, 1)
                chain(v.reciprocal(rstdA[:, :], stdA[:, :]))
                with v.Fori(0, NT // UN) as i:
                    for j in range(UN):
                        hold(v, xT0_done, free_after(i, j))
                        v.tensor_scalar(xn[j % 2][0:PT, :], one(X, i * UN + j),
                                        one(mvA[:, :, 0:1], i * UN + j), rstdA[:, bass.ds(i * UN + j, 1)],
                                        ALU.subtract, ALU.mult).then_inc(xn0, 1)
                        hold(v, xh_done, i * UN + (j + 3))
                        v.tensor_copy(one(XH, i * UN + j), ps[2 + j % 2][0:PT, 0:WA]).then_inc(xh_copied, 1)
                chain.restart()
                v.wait_ge(xh_copied, NT + 2)
                v.tensor_reduce(gmax[:, :], XH[:, :, C:TW].rearrange("p t h -> p h t"), AX, ALU.max).then_inc(gm_ready, 1)
                v.wait_ge(edges_in, 32)
                for ends, hi in ((dsti, dhi), (srci, shi)):
                    chain(v.tensor_scalar(tmpe[:, :], ends[:, :], 1.0 / PT, -0.5 + 0.5 / PT, ALU.mult, ALU.add))
                    chain(v.tensor_scalar(tmpe[:, :], tmpe[:, :], MAGIC, None, ALU.add))
                    chain(v.tensor_scalar(hi[:, :], tmpe[:, :], -MAGIC, None, ALU.add))
                chain(v.tensor_scalar(tmpe[:, :], shi[:, :], -float(PT), None, ALU.mult))
                chain(v.tensor_tensor(slo[:, :], tmpe[:, :], srci[:, :], ALU.add))
                chain(v.tensor_tensor(other[:, :, :], dhi[:, :].unsqueeze(1).broadcast_to([PT, NT, EC]),
                                      iota_d[0:PT, :].unsqueeze(2).broadcast_to([PT, NT, EC]), ALU.not_equal))
                for side, s in enumerate((BIG, -BIG)):
                    chain(v.scalar_tensor_tensor(bound[:, :, :], other[:, :, :], s,
                                                 edge_no[:, :].unsqueeze(1).broadcast_to([PT, NT, EC]),
                                                 ALU.mult, ALU.add))
                    chain(v.tensor_reduce(wmm[:, side, :], bound[:, :, :], AX, ALU.min if side == 0 else ALU.max))
                v.tensor_scalar(wmm[:, 0, :], wmm[:, 0, :], -1.0, None, ALU.mult).then_inc(wm_ready, 1)
                v.wait_ge(gm_all, 1)
                v.wait_ge(wm_ready, 1)
                chain(v.tensor_copy(node[:, :, 0:HEADS], XH[:, :, TW:WA]))
                chain(v.tensor_tensor(sh[:, :, :], XH[:, :, TW:WA],
                                      gall[:, :].unsqueeze(1).broadcast_to([PT, NT, HEADS]), ALU.add))
                chain(v.scalar_tensor_tensor(node[:, :, HEADS:2 * HEADS], sh[:, :, :], SLOPE, sh[:, :, :],
                                             ALU.mult, ALU.max))
                chain(v.tensor_tensor(e_self[:, :, :], XH[:, :, C:TW], XH[:, :, TW:WA], ALU.add))
                chain(v.scalar_tensor_tensor(e_self[:, :, :], e_self[:, :, :], SLOPE, e_self[:, :, :],
                                             ALU.mult, ALU.max))
                v.tensor_tensor(sh[:, :, :], e_self[:, :, :], node[:, :, HEADS:2 * HEADS],
                                ALU.subtract).then_inc(self_z, 1)
                v.wait_ge(wm_all, 1)
                chain(v.tensor_scalar(wa[:, :], wall[:, 0, :], -1.0, float(E - 1), ALU.mult, ALU.min))
                chain(v.tensor_tensor(wb[:, :], wall[:, 1, :], wa[:, :], ALU.subtract))
                chain(v.tensor_scalar(wb[:, :], wb[:, :], 1.0, 1.0, ALU.add, ALU.max))
                chain(v.tensor_scalar(wb[:, :], wb[:, :], 1.0 / WIN, 0.5 - 0.5 / WIN, ALU.mult, ALU.add))
                chain(v.tensor_scalar(wb[:, :], wb[:, :], MAGIC, None, ALU.add))
                chain(v.tensor_scalar(wb[:, :], wb[:, :], -MAGIC, None, ALU.add))
                chain(v.memset(wc[:, 0:1], 0.0))
                chain(v.tensor_tensor_scan(wc[:, 1:NT + 1], ones_t[:, :], wb[:, :], 0.0, ALU.mult, ALU.add))
                chain(v.tensor_copy(wtab[0:1, 0, 0:NT], wa[0:1, :]))
                chain(v.tensor_copy(wtab[0:1, 1, :], wc[0:1, :]))
                v.wait_ge(self_e, 1)

        def window_passes(eng, d):
            first = eng.value_load(wtab[0:1, 1, bass.ds(d, 1)], min_val=0, max_val=NT * 23)
            last = eng.value_load(wtab[0:1, 1, bass.ds(d + 1, 1)], min_val=1, max_val=NT * 23)
            return first, last

        def load_windows(sp, taken_src, taken_dst, win_src, win_dst, row=None):
            with sp.Fori(0, NT) as d:
                first, last = window_passes(sp, d)
                start = sp.value_load(wtab[0:1, 0, bass.ds(d, 1)], min_val=0, max_val=E - 1)
                with sp.Fori(first, last) as q:
                    at = nc.s_assert_within((q - first) * WIN + start, 0, E, 
                                            skip_runtime_bounds_check_because="a pass starts inside its window")
                    sp.wait_ge(taken_src, q + 1)
                    sp.dma_start(src_win[:, :], src_pad[bass.ds(at, WIN)].rearrange("(p j) -> p j", p=128))\
                        .then_inc(win_src, 16)
                    sp.wait_ge(taken_dst, q + 1)
                    sp.dma_start(dst_win[:, :], dst_pad[bass.ds(at, WIN)].rearrange("(p j) -> p j", p=128))\
                        .then_inc(win_dst, 16)
                    if row is not None:
                        dst_row, win_row = row
                        sp.dma_start(dst_row[:, :], dst_pad[bass.ds(at, WIN)].partition_broadcast(PT))\
                            .then_inc(win_row, 16)

        def gather_tile(pool, d, table, width, win_src, taken_src, seg_done, idx_ready, got):
            first, last = window_passes(pool, d)
            with pool.Fori(first, last) as q:
                hold(pool, win_src, q * 16 + 16)
                for c, (j0, j1) in enumerate(CHUNKS):
                    hold(pool, seg_done, q * NCH + (c + 1))
                    pool.tensor_copy(idx[:, j0:j1], src_win[:, j0:j1]).then_inc(idx_ready, 1)
                    hold(pool, idx_ready, q * NCH + (c + 1))
                    if c == NCH - 1:
                        pool.sem_inc(taken_src, 1)
                    for j in range(j0, j1):
                        pool.indirect_dma_start(G[:, j, 0:width], None, table,
                                                bass.IndirectOffsetOnAxis(idx[:, j:j + 1], 0)).then_inc(got[j], 16)

        p1 = {n: sem("gat_" + n) for n in (
            "win_src", "win_dst", "win_row", "taken_src", "taken_dst", "idx_ready", "masks_ready", "adm_ready",
            "z_ready", "w_ready", "msgs_ready", "seg_done", "self_ready", "var_ready", "std_ready", "xn_ready",
            "xT_done", "xT_copied", "h_done", "hpre_ready", "gelu_done", "ht_done", "ht_a", "ht_v", "gate_done",
            "lmax_ready", "lexp_done", "sel_ready", "rank_done", "pos_ready", "scattered", "hist_ready", "hist_done",
            "pad_ready")}
        got1 = sem("gotA", SLOTS)
        with ExitStack() as c1, nc.Block() as block:
            s1 = allocator(c1)
            dst_row = s1("dst_row", [PT, WIN], I32)
            OHT = s1("OHT", [PT, WIN])
            lg4 = s1("lg4", [128, SLOTS, HEADS])
            selfm = s1("selfm", [PT, TW + 1])
            row = s1("row", [128, ROW])
            hpre = s1("hpre", [128, HID])
            HT = s1("HT", [128, KH, PT])
            r4 = s1("r4", [PT, HEADS])
            lg = s1("lg", [PT, NX])
            lex = s1("lex", [PT, NX])
            nmx = s1("nmx", [PT, 1])
            se = s1("se", [PT, 1])
            cand = s1("cand", [PT, NX])
            amin = s1("amin", [PT, 1])
            sel = s1("sel", [PT, NX])
            selb = s1("selb", [PT, NX], BF16)
            pos = s1("pos", [PT, NX])
            pos1 = s1("pos1", [PT, 1])
            posi = s1("posi", [PT, 1], I32)
            ohi = s1("ohi", [PT, EPT, NT], BF16)
            olo = s1("olo", [PT, EPT, PT], BF16)
            acc, hist, misc = ps[0], ps[2], ps[3]
            adm = (ps[1], ps[6], ps[7])
            gate_ps = misc[0:PT, 256:256 + NX]
            rank_ps = misc[0:PT, 272:272 + NX]
            all_ps = misc[0:PT, 288:288 + NX]

            @block.sync
            def _(sp):
                load_windows(sp, p1["taken_src"], p1["taken_dst"], p1["win_src"], p1["win_dst"],
                             (dst_row, p1["win_row"]))
                sp.wait_ge(p1["scattered"], 16 * (NT + 1))

            @block.gpsimd
            def _(pool):
                pool.sem_inc(p1["taken_src"], 1)
                pool.wait_ge(p1["pad_ready"], 1)
                pool.dma_start(sorted_rows[NX * REG:NX * REG + 128, :], row[:, :]).then_inc(p1["scattered"], 16)

                def scatter(d):
                    hold(pool, p1["pos_ready"], d + 1)
                    pool.indirect_dma_start(sorted_rows, bass.IndirectOffsetOnAxis(posi[:, :], 0),
                                            row[0:PT, :], None).then_inc(p1["scattered"], 16)

                def gathers(d):
                    gather_tile(pool, d, table0, TW, p1["win_src"], p1["taken_src"], p1["seg_done"],
                                p1["idx_ready"], got1)
                gathers(0)
                with pool.Fori(1, NT) as d:
                    gathers(d)
                    scatter(d - 1)
                scatter(NT - 1)

            @block.scalar
            def _(act):
                with act.Fori(0, NT) as d:
                    first, last = window_passes(act, d)
                    with act.Fori(first, last) as q:
                        for c, (j0, j1) in enumerate(CHUNKS):
                            act.wait_ge(p1["z_ready"], q * NCH + (c + 1))
                            act.activation(G[:, j0:j1, C:TW], lg4[:, j0:j1, :], ACT.Exp).then_inc(p1["w_ready"], 1)
                    act.wait_ge(p1["var_ready"], d + 1)
                    act.activation(std[0:PT, 0:1], mv[0:PT, 0, 1:2], ACT.Sqrt, bias=eps_ln[0:PT, :])\
                        .then_inc(p1["std_ready"], 1)
                    act.wait_ge(p1["xT_done"], d + 1)
                    act.activation(xT[0][:, :, 0:PT], misc[:, 0:KC * PT].rearrange("p (k n) -> p k n", k=KC),
                                   ACT.Copy).then_inc(p1["xT_copied"], 1)
                    for half in range(2):
                        act.wait_ge(p1["hpre_ready"], d * 2 + (half + 1))
                        act.activation(row[0:PT, half * 512:(half + 1) * 512], hpre[0:PT, half * 512:(half + 1) * 512],
                                       ACT.Gelu).then_inc(p1["gelu_done"], 1)
                    act.wait_ge(p1["ht_done"], d * 2 + 1)
                    act.activation(HT[:, 0:KH // 2, :], ps[6][:, 0:KH // 2 * PT].rearrange("p (k n) -> p k n", n=PT),
                                   ACT.Copy).then_inc(p1["ht_a"], 1)
                    act.wait_ge(p1["lmax_ready"], d + 1)
                    act.activation(lex[:, :], lg[:, :], ACT.Exp, bias=nmx[:, :], accum_out=se[:, :])\
                        .then_inc(p1["lexp_done"], 1)

            @block.tensor
            def _(pe):
                pe.matmul(hist[0:PT, 0:NT], zeros_b[0:PT, 0:PT], zeros_b[0:PT, 0:NT], start=True, stop=False,
                          skip_group_check=True)
                with pe.Fori(0, NT) as d:
                    hold(pe, p1["self_ready"], d + 1)
                    pe.matmul(acc[0:PT, 0:TW + 1], ident[0:PT, 0:PT], selfm[:, :], start=True, stop=False,
                              skip_group_check=True)
                    first, last = window_passes(pe, d)
                    with pe.Fori(first, last) as q:
                        for c, (j0, j1) in enumerate(CHUNKS):
                            hold(pe, p1["masks_ready"], q * NCH + (c + 1))
                            for j in range(j0, j1):
                                m = pe.matmul(adm[c][:, j * 8:(j + 1) * 8], OHT[:, j * 128:(j + 1) * 128],
                                              one(node, d), start=True, stop=True)
                            m.then_inc(p1["adm_ready"], 1)
                        for c, (j0, j1) in enumerate(CHUNKS):
                            hold(pe, p1["msgs_ready"], q * NCH + (c + 1))
                            for j in range(j0, j1):
                                m = pe.matmul(acc[0:PT, 0:TW + 1], OH[:, j, :], G[:, j, 0:TW + 1], start=False,
                                              stop=False, skip_group_check=True)
                            m.then_inc(p1["seg_done"], 1)
                    hold(pe, p1["hist_ready"], d + 1)
                    for j in range(EPT):
                        m = pe.matmul(hist[0:PT, 0:NT], olo[:, j, :], ohi[:, j, :], start=False, stop=False,
                                      skip_group_check=True)
                    m.then_inc(p1["hist_done"], 1)
                    hold(pe, p1["xn_ready"], d + 1)
                    for k in range(KC):
                        m = pe.transpose(misc[:, k * PT:(k + 1) * PT], xn[0][0:PT, k * 128:(k + 1) * 128],
                                         ident[0:PT, 0:PT])
                    m.then_inc(p1["xT_done"], 1)
                    hold(pe, p1["xT_copied"], d + 1)
                    for half in range(2):
                        for k in range(KC):
                            m = pe.matmul(ps[4 + half][0:PT, :], xT[0][:, k, 0:PT], fW1[:, k, half * 512:(half + 1) * 512],
                                          start=(k == 0), stop=(k == KC - 1))
                        m.then_inc(p1["h_done"], 1)
                    for half in range(2):
                        hold(pe, p1["gelu_done"], d * 2 + (half + 1))
                        for k in range(KH // 2):
                            kk = half * (KH // 2) + k
                            m = pe.transpose(ps[6 + half][:, k * PT:(k + 1) * PT], row[0:PT, kk * 128:(kk + 1) * 128],
                                             ident[0:PT, 0:PT])
                        m.then_inc(p1["ht_done"], 1)
                    hold(pe, p1["ht_a"], d + 1)
                    for k in range(KH):
                        if k == KH // 2:
                            hold(pe, p1["ht_v"], d + 1)
                        m = pe.matmul(gate_ps, HT[:, k, :], fWg[:, k, :], start=(k == 0), stop=(k == KH - 1))
                    m.then_inc(p1["gate_done"], 1)
                    hold(pe, p1["sel_ready"], d + 1)
                    pe.matmul(rank_ps, before[0:PT, 0:PT], selb[:, :], start=True, stop=True)
                    pe.matmul(all_ps, ones_b[0:PT, 0:PT], selb[:, :], start=True, stop=True).then_inc(p1["rank_done"], 1)

            @block.vector
            def _(v):
                chain = Chain(v, v_chain)
                v.sem_clear(v_chain)
                chain(v.memset(row[:, :], 0.0))
                v.memset(row[:, HID + C + 1:HID + C + 2].bitcast(I32), NO_NODE).then_inc(p1["pad_ready"], 1)
                v.sem_inc(p1["taken_dst"], 1)
                v.sem_inc(p1["seg_done"], NCH)
                with v.Fori(0, NT) as d:
                    chain.restart()
                    chain(v.tensor_tensor(selfm[:, 0:C].rearrange("p (h c) -> p h c", h=HEADS),
                                          XH[:, bass.ds(d, 1), 0:C].rearrange("p a (h c) -> p (a h) c", h=HEADS),
                                          one(e_self, d).unsqueeze(2).broadcast_to([PT, HEADS, HC]), ALU.mult))
                    chain(v.tensor_copy(selfm[:, C:TW], one(e_self, d)))
                    v.memset(selfm[:, TW:TW + 1], 0.0).then_inc(p1["self_ready"], 1)
                    chain(v.tensor_tensor(olo[:, :, :], iota_b[0:PT, 0:PT].unsqueeze(1).broadcast_to([PT, EPT, PT]),
                                          slo[:, bass.ds(d * EPT, EPT)].unsqueeze(2).broadcast_to([PT, EPT, PT]),
                                          ALU.is_equal))
                    v.tensor_tensor(ohi[:, :, :], iota_b[0:PT, 0:NT].unsqueeze(1).broadcast_to([PT, EPT, NT]),
                                    shi[:, bass.ds(d * EPT, EPT)].unsqueeze(2).broadcast_to([PT, EPT, NT]),
                                    ALU.is_equal).then_inc(p1["hist_ready"], 1)
                    first, last = window_passes(v, d)
                    with v.Fori(first, last) as q:
                        chain.restart()
                        hold(v, p1["win_dst"], q * 16 + 16)
                        chain(v.tensor_scalar(dloc[:, :], dst_win[:, :], tile_lo[:, bass.ds(d, 1)], None, ALU.subtract))
                        hold(v, p1["win_row"], q * 16 + 16)
                        for c, (j0, j1) in enumerate(CHUNKS):
                            chain(v.tensor_scalar(
                                OHT[:, j0 * 128:j1 * 128].rearrange("p (j e) -> p j e", e=128),
                                dst_row[:, :].rearrange("p (e j) -> p j e", j=SLOTS)[:, j0:j1, :],
                                tile_row[0:PT, bass.ds(d, 1)], None, ALU.is_equal))
                            hold(v, p1["seg_done"], q * NCH + (c + 1))
                            v.tensor_tensor(OH[:, j0:j1, :],
                                            iota_c[:, 0:PT].unsqueeze(1).broadcast_to([128, j1 - j0, PT]),
                                            dloc[:, j0:j1].unsqueeze(2).broadcast_to([128, j1 - j0, PT]),
                                            ALU.is_equal).then_inc(p1["masks_ready"], 1)
                        v.sem_inc(p1["taken_dst"], 1)

                        def logits(c):
                            j0, j1 = CHUNKS[c]
                            a = adm[c][:, j0 * 8:j1 * 8].rearrange("p (j n) -> p j n", n=8)
                            hold(v, p1["adm_ready"], q * NCH + (c + 1))
                            for j in range(j0, j1):
                                hold(v, got1[j], q * 16 + 16)
                            z = lg4[:, j0:j1, :]
                            chain(v.tensor_tensor(z, G[:, j0:j1, C:TW], a[:, :, 0:HEADS], ALU.add))
                            chain(v.scalar_tensor_tensor(z, z, SLOPE, z, ALU.mult, ALU.max))
                            chain(v.tensor_tensor(z, z, a[:, :, HEADS:2 * HEADS], ALU.subtract))
                            v.tensor_scalar(z, z, 0.0, None, ALU.min).then_inc(p1["z_ready"], 1)

                        def messages(c):
                            j0, j1 = CHUNKS[c]
                            hold(v, p1["w_ready"], q * NCH + (c + 1))
                            g4 = G[:, j0:j1, 0:C].rearrange("p j (h c) -> p j h c", h=HEADS)
                            v.tensor_tensor(g4, g4, G[:, j0:j1, C:TW].unsqueeze(3).broadcast_to([128, j1 - j0, HEADS, HC]),
                                            ALU.mult).then_inc(p1["msgs_ready"], 1)
                        logits(0)
                        logits(1)
                        messages(0)
                        logits(2)
                        messages(1)
                        messages(2)
                    chain.restart()
                    hold(v, p1["seg_done"], last * NCH + NCH)
                    hold(v, p1["scattered"], d * 16 + 16)
                    chain(v.reciprocal(r4[:, :], acc[0:PT, C:TW]))
                    x1 = row[0:PT, HID:HID + C]
                    chain(v.tensor_tensor(x1.rearrange("p (h c) -> p h c", h=HEADS),
                                          acc[0:PT, 0:C].rearrange("p (h c) -> p h c", h=HEADS),
                                          r4[:, :].unsqueeze(2).broadcast_to([PT, HEADS, HC]), ALU.mult))
                    chain(v.tensor_copy(deg_in[:, bass.ds(d, 1)], acc[0:PT, TW:TW + 1]))
                    chain(v.tensor_tensor(x1, x1, bias0[0:PT, :], ALU.add))
                    chain(v.tensor_tensor(x1, x1, one(X, d), ALU.add))
                    chain(v.bn_stats(st[0:PT, 0, :], x1))
                    v.bn_aggr(mv[0:PT, 0, :], st[0:PT, 0, :]).then_inc(p1["var_ready"], 1)
                    hold(v, p1["std_ready"], d + 1)
                    chain(v.reciprocal(rstd[0:PT, 0:1], std[0:PT, 0:1]))
                    v.tensor_scalar(xn[0][0:PT, :], x1, mv[0:PT, 0, 0:1], rstd[0:PT, 0:1], ALU.subtract,
                                    ALU.mult).then_inc(p1["xn_ready"], 1)
                    for half in range(2):
                        hold(v, p1["h_done"], d * 2 + (half + 1))
                        s = slice(half * 512, (half + 1) * 512)
                        v.tensor_tensor(hpre[0:PT, s], ps[4 + half][0:PT, :], b1row[0:PT, s], ALU.add)\
                            .then_inc(p1["hpre_ready"], 1)
                    hold(v, p1["ht_done"], d * 2 + 2)
                    v.tensor_copy(HT[:, KH // 2:KH, :], ps[7][:, 0:KH // 2 * PT].rearrange("p (k n) -> p k n", n=PT))\
                        .then_inc(p1["ht_v"], 1)
                    hold(v, p1["gate_done"], d + 1)
                    chain(v.tensor_tensor(lg[:, :], gate_ps, bgrow[0:PT, :], ALU.add))
                    chain(v.tensor_reduce(amin[:, :], lg[:, :], AX, ALU.max))
                    v.tensor_scalar(nmx[:, :], amin[:, :], -1.0, None, ALU.mult).then_inc(p1["lmax_ready"], 1)
                    chain(v.tensor_scalar(cand[:, :], lg[:, :], amin[:, :], BIG, ALU.is_lt, ALU.mult))
                    chain(v.tensor_tensor(cand[:, :], cand[:, :], iota_c[0:PT, 0:NX], ALU.add))
                    chain(v.tensor_reduce(amin[:, :], cand[:, :], AX, ALU.min))
                    chain(v.tensor_scalar(sel[:, :], iota_c[0:PT, 0:NX], amin[:, :], None, ALU.is_equal))
                    v.tensor_copy(selb[:, :], sel[:, :]).then_inc(p1["sel_ready"], 1)
                    hold(v, p1["lexp_done"], d + 1)
                    chain(v.reciprocal(row[0:PT, HID + C:HID + C + 1], se[:, :]))
                    chain(v.tensor_copy(row[0:PT, HID + C + 1:HID + C + 2].bitcast(I32), tile_row[0:PT, bass.ds(d, 1)]))
                    hold(v, p1["rank_done"], d + 1)
                    chain(v.tensor_tensor(pos[:, :], rank_ps, cnt[0:PT, :], ALU.add))
                    chain(v.tensor_tensor(pos[:, :], pos[:, :], region8[0:PT, :], ALU.add))
                    chain(v.tensor_tensor(pos[:, :], pos[:, :], sel[:, :], ALU.mult))
                    chain(v.tensor_reduce(pos1[:, :], pos[:, :], AX, ALU.add))
                    chain(v.tensor_tensor(cnt[0:PT, :], cnt[0:PT, :], all_ps, ALU.add))
                    v.tensor_copy(posi[:, :], pos1[:, :]).then_inc(p1["pos_ready"], 1)
                    hold(v, p1["hist_done"], d + 1)

        hist = ps[2]
        p2 = {n: sem("moe_" + n) for n in (
            "deg_ready", "sq_ready", "rs_ready", "tab_ready", "filled", "pads", "weights", "ht_done",
            "ht_a", "ht_v", "y_done", "var_ready", "std_ready", "ids_ready", "rs_got", "x2_ready", "h_ready",
            "bnt_done", "row_used")}
        rin = sem("rin", 2)
        sent = sem("sent", 2)
        weights0.close()
        w3 = ExitStack()
        s3w = allocator(w3)
        bnT = s3w("bnT", [128, 10, NX, KC])
        with ExitStack() as c2, nc.Block() as block:
            s2 = allocator(c2)
            Wd = s2("Wd", [128, NX, KH, C])
            bdrow = s2("bdrow", [128, NX, C])
            rbuf = [s2(f"rbuf{i}", [128, ROW]) for i in range(2)]
            HT = [s2(f"HTb{i}", [128, KH, 128]) for i in range(2)]
            pads = s2("pads", [128, ROW])
            degs = s2("degs", [PT, 2, NT])
            sqs = s2("sqs", [PT, 2, NT])
            rsq = s2("rsq", [PT, 2, NT])
            nt8 = s2("nt8", [128, NX])
            ct8 = s2("ct8", [128, NX])
            one8 = s2("one8", [128, NX])
            ge = s2("ge", [128, TMAX, NX])
            gn = s2("gn", [128, TMAX, NX])
            te = s2("te", [128, TMAX])
            ts_ = s2("ts_", [128, TMAX])
            tr = s2("tr", [128, TMAX])
            ttab = s2("ttab", [1, 2, TMAX], I32)
            ptab = s2("ptab", [1, NX + 1], I32)
            pf = s2("pf", [128, NX + 1])
            ids = [s2(f"ids{i}", [128, 1], I32) for i in range(2)]
            rsg = [s2(f"rsg{i}", [128, 1]) for i in range(2)]
            x2 = [s2(f"x2_{i}", [128, C]) for i in range(2)]
            hx = [s2(f"hx{i}", [128, C]) for i in range(2)]

            def pairs(eng):
                return eng.value_load(ptab[0:1, NX:NX + 1], min_val=1, max_val=TMAX // 2)

            @block.sync
            def _(sp):
                sp.dma_start(bdrow[:, :, :].rearrange("p e c -> p (e c)"),
                             f0_bd.rearrange("e c -> (e c)").partition_broadcast(128)).then_inc(p2["weights"], 16)
                for e in range(NX):
                    sp.dma_start(Wd[:, e, :, :], f0_Wd[e].rearrange("(k p) n -> p k n", p=128)).then_inc(p2["weights"], 16)
                sp.wait_ge(p2["tab_ready"], 2)
                for e in range(NX):
                    at = sp.value_load(ptab[0:1, e:e + 1], min_val=0, max_val=NX * REG)
                    sp.dma_start(sorted_rows[bass.ds(at, 128), :], pads[:, :]).then_inc(p2["pads"], 16)
                sp.wait_ge(p2["pads"], 16 * NX)
                n = pairs(sp)
                with sp.Fori(0, n) as u:
                    for b in range(2):
                        at = sp.value_load(ttab[0:1, 1, bass.ds(u * 2 + b, 1)], min_val=0, max_val=NX * REG)
                        sp.wait_ge(p2["row_used"], u * 2 + (b + 1))
                        sp.dma_start(rbuf[b][:, :], sorted_rows[bass.ds(at, 128), :]).then_inc(rin[b], 16)
                for b in range(2):
                    hold(sp, sent[b], n * 32 + 16)

            @block.gpsimd
            def _(pool):
                pool.wait_ge(p2["rs_ready"], 1)
                half = NT // 2
                with nc.allow_non_contiguous_dma(reason="one value a node, once"):
                    for b, (t0, t1) in enumerate(((0, half), (half, NT))):
                        pool.dma_start(rs_rows[t0 * PT:t1 * PT, :].rearrange("(t p) a -> p (t a)", p=PT),
                                       rsq[:, 0, t0:t1]).then_inc(sent[b], 16)
                for b in range(2):
                    pool.wait_ge(sent[b], 16)
                n = pairs_ready(pool, p2, ptab, NX, TMAX)
                with pool.Fori(0, n) as u:
                    for b in range(2):
                        hold(pool, p2["ids_ready"], u * 2 + (b + 1))
                        pool.indirect_dma_start(rsg[b][:, :], None, rs_rows, bass.IndirectOffsetOnAxis(ids[b][:, :], 0),
                                                bounds_check=N - 1, oob_is_err=False).then_inc(p2["rs_got"], 16)
                        hold(pool, p2["x2_ready"], u * 2 + (b + 1))
                        pool.indirect_dma_start(x2_rows, bass.IndirectOffsetOnAxis(ids[b][:, :], 0), x2[b][:, :], None,
                                                bounds_check=N - 1, oob_is_err=False).then_inc(sent[b], 16)
                        hold(pool, p2["h_ready"], u * 2 + (b + 1))
                        pool.indirect_dma_start(table1, bass.IndirectOffsetOnAxis(ids[b][:, :], 0), hx[b][:, :], None,
                                                bounds_check=N - 1, oob_is_err=False).then_inc(sent[b], 16)

            @block.scalar
            def _(act):
                act.wait_ge(p2["deg_ready"], 1)
                act.activation(sqs[:, :, :], degs[:, :, :], ACT.Sqrt).then_inc(p2["sq_ready"], 1)
                n = pairs_ready(act, p2, ptab, NX, TMAX)
                with act.Fori(0, n) as u:
                    for b in range(2):
                        hold(act, p2["y_done"], u * 2 + (b + 1))
                        act.wait_ge(p2["ht_done"], u * 4 + (2 * b + 1))
                        act.activation(HT[b][:, 0:KH // 2, :], ps[2 * b][:, :].rearrange("p (k n) -> p k n", n=128),
                                       ACT.Copy).then_inc(p2["ht_a"], 1)
                        act.wait_ge(p2["var_ready"], u * 2 + (b + 1))
                        act.activation(std[:, b:b + 1], mv[:, b, 1:2], ACT.Sqrt, bias=eps_ln[:, :])\
                            .then_inc(p2["std_ready"], 1)

            @block.tensor
            def _(pe):
                pe.transpose(ps[7][:, 0:128], bn_rows[0][:, :], ident[:, :])
                pe.transpose(ps[7][:, 128:160], bn_rows[1][:, :], ident[0:32, 0:32]).then_inc(p2["bnt_done"], 1)
                pe.sem_inc(p2["y_done"], 2)
                pe.wait_ge(p2["weights"], 16 * (NX + 1))
                n = pairs_ready(pe, p2, ptab, NX, TMAX)
                with pe.Fori(0, n) as u:
                    for b in range(2):
                        hold(pe, rin[b], u * 16 + 16)
                        for half in range(2):
                            for k in range(KH // 2):
                                kk = half * (KH // 2) + k
                                m = pe.transpose(ps[2 * b + half][:, k * 128:(k + 1) * 128],
                                                 rbuf[b][:, kk * 128:(kk + 1) * 128], ident[:, :])
                            m.then_inc(p2["ht_done"], 1)
                        e = pe.value_load(ttab[0:1, 0, bass.ds(u * 2 + b, 1)], min_val=0, max_val=NX - 1)
                        hold(pe, p2["ht_a"], u * 2 + (b + 1))
                        for k in range(KH):
                            if k == KH // 2:
                                hold(pe, p2["ht_v"], u * 2 + (b + 1))
                            m = pe.matmul(ps[4 + b][:, 0:C], HT[b][:, k, :],
                                          Wd[:, bass.ds(e, 1), k, :].rearrange("p a c -> p (a c)"),
                                          start=(k == 0), stop=(k == KH - 1))
                        m.then_inc(p2["y_done"], 1)

            @block.vector
            def _(v):
                chain = Chain(v, v_chain)
                chain.restart()
                v.sem_inc(p2["row_used"], 2)
                v.wait_ge(p2["bnt_done"], 1)
                chain(v.tensor_copy(bnT[:, :, :, :].rearrange("p i e k -> p (i e k)"), ps[7][:, 0:160]))
                chain(v.tensor_scalar(degs[:, 0, :], hist[0:PT, 0:NT], 1.0, None, ALU.max))
                v.tensor_scalar(degs[:, 1, :], deg_in[:, :], 1.0, None, ALU.max).then_inc(p2["deg_ready"], 1)
                v.wait_ge(p2["sq_ready"], 1)
                v.reciprocal(rsq[:, :, :], sqs[:, :, :]).then_inc(p2["rs_ready"], 1)
                v.wait_ge(p2["rs_ready"], 1)
                chain(v.tensor_copy(deg_in[:, :], rsq[:, 1, :]))
                v.memset(one8[:, :], 1.0)
                v.memset(rsg[0][:, :], 0.0)
                chain(v.memset(rsg[1][:, :], 0.0))
                chain(v.tensor_scalar(nt8[0:PT, :], cnt[0:PT, :], 1.0 / 128, 0.5 - 1.0 / 512, ALU.mult, ALU.add))
                chain(v.tensor_scalar(nt8[0:PT, :], nt8[0:PT, :], MAGIC, None, ALU.add))
                chain(v.tensor_scalar(nt8[0:PT, :], nt8[0:PT, :], -MAGIC, None, ALU.add))
                chain(v.tensor_tensor_scan(ct8[0:PT, :], one8[0:PT, :], nt8[0:PT, :], 0.0, ALU.mult, ALU.add))
                chain(v.tensor_tensor(ge[0:PT, :, :], iota_c[0:PT, 0:TMAX].unsqueeze(2).broadcast_to([PT, TMAX, NX]),
                                      ct8[0:PT, :].unsqueeze(1).broadcast_to([PT, TMAX, NX]), ALU.is_ge))
                chain(v.tensor_tensor(gn[0:PT, :, :], ge[0:PT, :, :],
                                      nt8[0:PT, :].unsqueeze(1).broadcast_to([PT, TMAX, NX]), ALU.mult))
                chain(v.tensor_reduce(te[0:PT, :], ge[0:PT, :, :], AX, ALU.add))
                chain(v.tensor_reduce(ts_[0:PT, :], gn[0:PT, :, :], AX, ALU.add))
                chain(v.tensor_tensor(tr[0:PT, :], iota_c[0:PT, 0:TMAX], ts_[0:PT, :], ALU.subtract))
                chain(v.tensor_scalar(ts_[0:PT, :], te[0:PT, :], REG / 128.0, None, ALU.mult))
                chain(v.tensor_tensor(tr[0:PT, :], tr[0:PT, :], ts_[0:PT, :], ALU.add))
                chain(v.tensor_scalar(tr[0:PT, :], tr[0:PT, :], 128.0, float(NX * REG), ALU.mult, ALU.min))
                chain(v.tensor_scalar(te[0:PT, :], te[0:PT, :], float(NX - 1), None, ALU.min))
                chain(v.tensor_tensor(pf[0:PT, 0:NX], region8[0:PT, :], cnt[0:PT, :], ALU.add))
                chain(v.tensor_scalar(pf[0:PT, NX:NX + 1], ct8[0:PT, NX - 1:NX], 0.5, 0.25, ALU.mult, ALU.add))
                chain(v.tensor_scalar(pf[0:PT, NX:NX + 1], pf[0:PT, NX:NX + 1], MAGIC, None, ALU.add))
                chain(v.tensor_scalar(pf[0:PT, NX:NX + 1], pf[0:PT, NX:NX + 1], -MAGIC, None, ALU.add))
                chain(v.tensor_copy(ttab[0:1, 0, :], te[0:1, :]))
                chain(v.tensor_copy(ttab[0:1, 1, :], tr[0:1, :]))
                v.tensor_copy(ptab[0:1, :], pf[0:1, :]).then_inc(p2["tab_ready"], 1)
                chain(v.memset(pads[:, :], 0.0))
                v.memset(pads[:, HID + C + 1:HID + C + 2].bitcast(I32), NO_NODE).then_inc(p2["tab_ready"], 1)
                v.wait_ge(p2["tab_ready"], 2)
                n = pairs(v)
                with v.Fori(0, n) as u:
                    chain.restart()
                    for b in range(2):
                        hold(v, rin[b], u * 16 + 16)
                        hold(v, sent[b], u * 32 + 16)
                        v.tensor_copy(ids[b][:, :], rbuf[b][:, HID + C + 1:HID + C + 2].bitcast(I32))\
                            .then_inc(p2["ids_ready"], 1)
                        hold(v, p2["y_done"], u * 2 + (b + 1))
                        hold(v, p2["ht_done"], u * 4 + (2 * b + 2))
                        v.tensor_copy(HT[b][:, KH // 2:KH, :], ps[2 * b + 1][:, :].rearrange("p (k n) -> p k n", n=128))\
                            .then_inc(p2["ht_v"], 1)
                        e = v.value_load(ttab[0:1, 0, bass.ds(u * 2 + b, 1)], min_val=0, max_val=NX - 1)
                        hold(v, p2["y_done"], u * 2 + (b + 3))
                        chain(v.tensor_tensor(x2[b][:, :], ps[4 + b][:, 0:C], one(bdrow, e), ALU.add))
                        chain(v.scalar_tensor_tensor(x2[b][:, :], x2[b][:, :], rbuf[b][:, HID + C:HID + C + 1],
                                                     rbuf[b][:, HID:HID + C], ALU.mult, ALU.add))
                        chain(v.bn_stats(st[:, b, :], x2[b][:, :]))
                        v.bn_aggr(mv[:, b, :], st[:, b, :]).then_inc(p2["var_ready"], 1)
                        v.sem_inc(p2["row_used"], 1)
                        v.sem_inc(p2["x2_ready"], 1)
                        hold(v, p2["std_ready"], u * 2 + (b + 1))
                        chain(v.reciprocal(rstd[:, b:b + 1], std[:, b:b + 1]))
                        hold(v, p2["rs_got"], u * 32 + (16 * b + 16))
                        chain(v.tensor_tensor(rstd[:, b:b + 1], rstd[:, b:b + 1], rsg[b][:, :], ALU.mult))
                        v.tensor_scalar(hx[b][:, :], x2[b][:, :], mv[:, b, 0:1], rstd[:, b:b + 1], ALU.subtract,
                                        ALU.mult).then_inc(p2["h_ready"], 1)

        p3 = {n: sem("gcn_" + n) for n in (
            "weights", "win_src", "win_dst", "taken_src", "taken_dst", "idx_ready", "masks_ready", "seg_done",
            "ag_ready", "agT_done", "agT_copied", "hw_done", "ss_ready", "nrm_ready", "var_ready", "std_ready",
            "xn_ready", "xT_done", "xT_copied", "gate_done", "lmax_ready", "lexp_done", "w_ready", "wT_done",
            "wT_copied", "bo_done", "h1_done", "h1_act", "h2_done", "h2_act", "y_done", "y_taken", "x2_in", "out_ready",
            "written", "sq_in", "sq_out", "zero_done")}
        got3 = sem("gotB", SLOTS)
        with ExitStack() as c3, nc.Block() as block:
            s3 = allocator(c3)
            L1 = s3("L1", [128, NX, KC, C])
            L2 = s3("L2", [128, NX, KC, C])
            L3 = s3("L3", [128, NX, KC, C])
            W1g = s3("W1g", [128, KC, C])
            b1g = s3("b1g", [128, C])
            Wr = s3("Wr", [128, KC, NX])
            brrow = s3("brrow", [128, NX])
            bo = s3("bo", [NX, C])
            bns = s3("bns", [128, 4, NX, KC])
            bsq = s3("bsq", [128, 2, NX, KC])
            x2t = s3("x2t", [PT, C])
            ag = s3("ag", [PT, C])
            agT = s3("agT", [128, KC, PT])
            hh = s3("hh", [PT, C])
            hsq = s3("hsq", [PT, C])
            ss = s3("ss", [PT, 1])
            nrm = s3("nrm", [PT, 1])
            x3 = s3("x3", [PT, C])
            lg = s3("lg3", [PT, NX])
            lex = s3("lex3", [PT, NX])
            lmx = s3("lmx", [PT, 1])
            nmx = s3("nmx3", [PT, 1])
            se = s3("se3", [PT, 1])
            rse = s3("rse", [PT, 1])
            wgt = s3("wgt", [PT, NX])
            wT = s3("wT", [NX, PT])
            h1 = [s3(f"h1_{i}", [128, KC, PT]) for i in range(2)]
            h2 = [s3(f"h2_{i}", [128, KC, PT]) for i in range(2)]
            ot = s3("ot", [PT, C])
            zero_b3 = s3("zero_b3", [128, 128])
            acc, misc = ps[0], ps[1]
            agT_ps = misc[:, 0:KC * PT].rearrange("p (k n) -> p k n", k=KC)
            hw_ps = ps[2][0:PT, 0:C]
            gate_ps = ps[2][0:PT, C:C + NX]
            y_ps = (ps[7][0:PT, 0:C], ps[1][0:PT, 0:C])
            wT_ps = ps[2][0:NX, C + 16:C + 16 + PT]

            @block.sync
            def _(sp):
                for tile, w in ((L1, f1_W1), (L2, f1_W2), (L3, f1_Wo)):
                    for e in range(NX):
                        sp.dma_start(tile[:, e, :, :], w[e].rearrange("(k p) n -> p k n", p=128)).then_inc(p3["weights"], 16)
                sp.dma_start(W1g[:, :, :], g1_W.rearrange("(k p) n -> p k n", p=128)).then_inc(p3["weights"], 16)
                sp.dma_start(Wr[:, :, :], f1_Wr.rearrange("(k p) n -> p k n", p=128)).then_inc(p3["weights"], 16)
                sp.dma_start(b1g[:, :], g1_b.partition_broadcast(128)).then_inc(p3["weights"], 16)
                sp.dma_start(brrow[:, :], f1_br.partition_broadcast(128)).then_inc(p3["weights"], 16)
                load_windows(sp, p3["taken_src"], p3["taken_dst"], p3["win_src"], p3["win_dst"])

            @block.gpsimd
            def _(pool):
                pool.sem_inc(p3["taken_src"], 1)
                with pool.Fori(0, NT) as d:
                    gather_tile(pool, d, table1, C, p3["win_src"], p3["taken_src"], p3["seg_done"],
                                p3["idx_ready"], got3)

            @block.scalar
            def _(act):
                act.wait_ge(p3["sq_in"], 1)
                act.activation(bsq[:, :, :, :], bsq[:, :, :, :], ACT.Sqrt, bias=eps_bn[:, :]).then_inc(p3["sq_out"], 1)
                x2v = x2_rows.rearrange("(t p) c -> t p c", p=PT)
                ov = out.rearrange("(t p) c -> t p c", p=PT)
                act.dma_start(bo[:, :], f1_bo).then_inc(p3["written"], 16)
                with act.Fori(0, NT) as d:
                    hold(act, p3["out_ready"], d + 1)
                    act.dma_start(x2t[:, :], x2v[bass.ds(d, 1), :, :].rearrange("a p c -> (a p) c")).then_inc(p3["x2_in"], 16)
                    act.wait_ge(p3["agT_done"], d + 1)
                    act.activation(agT[:, :, :], agT_ps, ACT.Copy).then_inc(p3["agT_copied"], 1)
                    act.wait_ge(p3["ss_ready"], d + 1)
                    act.activation(nrm[:, :], ss[:, :], ACT.Sqrt).then_inc(p3["nrm_ready"], 1)
                    act.wait_ge(p3["var_ready"], d + 1)
                    act.activation(std[0:PT, 0:1], mv[0:PT, 0, 1:2], ACT.Sqrt, bias=eps_ln[0:PT, :])\
                        .then_inc(p3["std_ready"], 1)
                    act.wait_ge(p3["xT_done"], d + 1)
                    act.activation(xT[0][:, :, 0:PT], agT_ps, ACT.Copy).then_inc(p3["xT_copied"], 1)
                    act.wait_ge(p3["lmax_ready"], d + 1)
                    act.activation(lex[:, :], lg[:, :], ACT.Exp, bias=nmx[:, :], accum_out=se[:, :])\
                        .then_inc(p3["lexp_done"], 1)
                    for i in range(NX + 1):
                        if i < NX:
                            act.wait_ge(p3["h1_done"], d * NX + (i + 1))
                            for k in range(KC):
                                m = act.activation(h1[i % 2][:, k, :], ps[3 + i % 2][:, k * PT:(k + 1) * PT], ACT.Relu,
                                                   bias=bns[:, 1, i, k:k + 1], scale=bns[:, 0, i, k:k + 1])
                            m.then_inc(p3["h1_act"], 1)
                        if i >= 1:
                            e = i - 1
                            act.wait_ge(p3["h2_done"], d * NX + (e + 1))
                            for k in range(KC):
                                m = act.activation(h2[e % 2][:, k, :], ps[5 + e % 2][:, k * PT:(k + 1) * PT], ACT.Relu,
                                                   bias=bns[:, 3, e, k:k + 1], scale=bns[:, 2, e, k:k + 1])
                            m.then_inc(p3["h2_act"], 1)
                    hold(act, p3["out_ready"], d + 2)
                    act.dma_start(ov[bass.ds(d, 1), :, :].rearrange("a p c -> (a p) c"), ot[:, :]).then_inc(p3["written"], 16)
                act.wait_ge(p3["written"], 16 * (NT + 1))

            @block.tensor
            def _(pe):
                pe.wait_ge(p3["weights"], 16 * (3 * NX + 4))
                pe.wait_ge(p3["zero_done"], 1)
                pe.wait_ge(p3["written"], 16)
                with pe.Fori(0, NT) as d:
                    pe.matmul(acc[0:PT, 0:C], zero_b3[0:PT, 0:PT], W1g[0:PT, 0, :], start=True, stop=False,
                              skip_group_check=True)
                    first, last = window_passes(pe, d)
                    with pe.Fori(first, last) as q:
                        for c, (j0, j1) in enumerate(CHUNKS):
                            hold(pe, p3["masks_ready"], q * NCH + (c + 1))
                            for j in range(j0, j1):
                                hold(pe, got3[j], q * 16 + 16)
                                m = pe.matmul(acc[0:PT, 0:C], OH[:, j, :], G[:, j, 0:C], start=False,
                                              stop=False, skip_group_check=True)
                            m.then_inc(p3["seg_done"], 1)
                    hold(pe, p3["ag_ready"], d + 1)
                    for k in range(KC):
                        m = pe.transpose(misc[:, k * PT:(k + 1) * PT], ag[:, k * 128:(k + 1) * 128], ident[0:PT, 0:PT])
                    m.then_inc(p3["agT_done"], 1)
                    hold(pe, p3["agT_copied"], d + 1)
                    for k in range(KC):
                        m = pe.matmul(hw_ps, agT[:, k, :], W1g[:, k, :], start=(k == 0), stop=(k == KC - 1))
                    m.then_inc(p3["hw_done"], 1)
                    hold(pe, p3["xn_ready"], d + 1)
                    for k in range(KC):
                        m = pe.transpose(misc[:, k * PT:(k + 1) * PT], xn[0][0:PT, k * 128:(k + 1) * 128],
                                         ident[0:PT, 0:PT])
                    m.then_inc(p3["xT_done"], 1)
                    hold(pe, p3["xT_copied"], d + 1)
                    for k in range(KC):
                        m = pe.matmul(gate_ps, xT[0][:, k, 0:PT], Wr[:, k, :], start=(k == 0), stop=(k == KC - 1))
                    m.then_inc(p3["gate_done"], 1)
                    for i in range(NX + 2):
                        if i < NX:
                            if i >= 2:
                                hold(pe, p3["h1_act"], d * NX + (i - 1))
                            for k in range(KC):
                                for kk in range(KC):
                                    m = pe.matmul(ps[3 + i % 2][:, k * PT:(k + 1) * PT],
                                                  L1[:, i, kk, k * 128:(k + 1) * 128], xT[0][:, kk, 0:PT],
                                                  start=(kk == 0), stop=(kk == KC - 1))
                            m.then_inc(p3["h1_done"], 1)
                        if 1 <= i <= NX:
                            e = i - 1
                            hold(pe, p3["h1_act"], d * NX + (e + 1))
                            if e >= 2:
                                hold(pe, p3["h2_act"], d * NX + (e - 1))
                            for k in range(KC):
                                for kk in range(KC):
                                    m = pe.matmul(ps[5 + e % 2][:, k * PT:(k + 1) * PT],
                                                  L2[:, e, kk, k * 128:(k + 1) * 128], h1[e % 2][:, kk, :],
                                                  start=(kk == 0), stop=(kk == KC - 1))
                            m.then_inc(p3["h2_done"], 1)
                        if i == 1:
                            hold(pe, p3["w_ready"], d + 1)
                            pe.transpose(wT_ps, wgt[:, :], ident[0:PT, 0:PT]).then_inc(p3["wT_done"], 1)
                            hold(pe, p3["wT_copied"], d + 1)
                            pe.matmul(hw_ps, wT[:, :], bo[:, :], start=True, stop=True).then_inc(p3["bo_done"], 1)
                        if i >= 2:
                            e = i - 2
                            hold(pe, p3["h2_act"], d * NX + (e + 1))
                            hold(pe, p3["y_taken"], d * NX + (e + 1))
                            for kk in range(KC):
                                m = pe.matmul(y_ps[e % 2], h2[e % 2][:, kk, :],
                                              L3[:, e, kk, :], start=(kk == 0), stop=(kk == KC - 1))
                            m.then_inc(p3["y_done"], 1)

            @block.vector
            def _(v):
                chain = Chain(v, v_chain)
                chain.restart()
                v.memset(zero_b3[:, :], 0.0).then_inc(p3["zero_done"], 1)
                v.sem_inc(p3["taken_dst"], 1)
                v.sem_inc(p3["seg_done"], NCH)
                v.sem_inc(p3["out_ready"], 1)
                v.sem_inc(p3["y_taken"], 2)
                for i in range(2):
                    ins = v.tensor_copy(bsq[:, i, :, :], bnT[:, 5 * i + 4, :, :])
                    if i == 0:
                        chain(ins)
                ins.then_inc(p3["sq_in"], 1)
                v.wait_ge(p3["sq_out"], 1)
                chain(v.reciprocal(bsq[:, :, :, :], bsq[:, :, :, :]))
                for i in range(2):
                    chain(v.tensor_tensor(bns[:, 2 * i, :, :], bsq[:, i, :, :], bnT[:, 5 * i + 1, :, :], ALU.mult))
                    chain(v.tensor_tensor(bns[:, 2 * i + 1, :, :], bnT[:, 5 * i, :, :], bnT[:, 5 * i + 3, :, :],
                                          ALU.subtract))
                    chain(v.tensor_tensor(bns[:, 2 * i + 1, :, :], bns[:, 2 * i + 1, :, :], bns[:, 2 * i, :, :], ALU.mult))
                    chain(v.tensor_tensor(bns[:, 2 * i + 1, :, :], bns[:, 2 * i + 1, :, :], bnT[:, 5 * i + 2, :, :],
                                          ALU.add))
                v.wait_ge(p3["weights"], 16 * (3 * NX + 4))
                with v.Fori(0, NT) as d:
                    first, last = window_passes(v, d)
                    with v.Fori(first, last) as q:
                        chain.restart()
                        hold(v, p3["win_dst"], q * 16 + 16)
                        chain(v.tensor_scalar(dloc[:, :], dst_win[:, :], tile_lo[:, bass.ds(d, 1)], None, ALU.subtract))
                        v.sem_inc(p3["taken_dst"], 1)
                        for c, (j0, j1) in enumerate(CHUNKS):
                            hold(v, p3["seg_done"], q * NCH + (c + 1))
                            v.tensor_tensor(OH[:, j0:j1, :],
                                            iota_c[:, 0:PT].unsqueeze(1).broadcast_to([128, j1 - j0, PT]),
                                            dloc[:, j0:j1].unsqueeze(2).broadcast_to([128, j1 - j0, PT]),
                                            ALU.is_equal).then_inc(p3["masks_ready"], 1)
                    chain.restart()
                    hold(v, p3["seg_done"], last * NCH + NCH)
                    v.tensor_scalar(ag[:, :], acc[0:PT, 0:C], deg_in[:, bass.ds(d, 1)], None, ALU.mult)\
                        .then_inc(p3["ag_ready"], 1)
                    hold(v, p3["hw_done"], d + 1)
                    chain(v.tensor_tensor(hh[:, :], hw_ps, b1g[0:PT, :], ALU.add))
                    chain(v.tensor_scalar(hh[:, :], hh[:, :], 0.0, None, ALU.max))
                    v.tensor_tensor_reduce(hsq[:, :], hh[:, :], hh[:, :], 1.0, 0.0, ALU.mult, ALU.add, ss[:, :])\
                        .then_inc(p3["ss_ready"], 1)
                    hold(v, p3["nrm_ready"], d + 1)
                    chain(v.tensor_scalar(nrm[:, :], nrm[:, :], EPS_NORM, None, ALU.max))
                    chain(v.reciprocal(nrm[:, :], nrm[:, :]))
                    hold(v, p3["x2_in"], d * 16 + 16)
                    chain(v.scalar_tensor_tensor(x3[:, :], hh[:, :], nrm[:, :], x2t[:, :], ALU.mult, ALU.add))
                    chain(v.bn_stats(st[0:PT, 0, :], x3[:, :]))
                    v.bn_aggr(mv[0:PT, 0, :], st[0:PT, 0, :]).then_inc(p3["var_ready"], 1)
                    hold(v, p3["std_ready"], d + 1)
                    chain(v.reciprocal(rstd[0:PT, 0:1], std[0:PT, 0:1]))
                    v.tensor_scalar(xn[0][0:PT, :], x3[:, :], mv[0:PT, 0, 0:1], rstd[0:PT, 0:1], ALU.subtract,
                                    ALU.mult).then_inc(p3["xn_ready"], 1)
                    hold(v, p3["gate_done"], d + 1)
                    chain(v.tensor_tensor(lg[:, :], gate_ps, brrow[0:PT, :], ALU.add))
                    chain(v.tensor_reduce(lmx[:, :], lg[:, :], AX, ALU.max))
                    v.tensor_scalar(nmx[:, :], lmx[:, :], -1.0, None, ALU.mult).then_inc(p3["lmax_ready"], 1)
                    hold(v, p3["lexp_done"], d + 1)
                    chain(v.reciprocal(rse[:, :], se[:, :]))
                    v.tensor_scalar(wgt[:, :], lex[:, :], rse[:, :], None, ALU.mult).then_inc(p3["w_ready"], 1)
                    hold(v, p3["wT_done"], d + 1)
                    v.tensor_copy(wT[:, :], wT_ps).then_inc(p3["wT_copied"], 1)
                    hold(v, p3["bo_done"], d + 1)
                    hold(v, p3["written"], d * 16 + 16)
                    chain(v.tensor_tensor(ot[:, :], x3[:, :], hw_ps, ALU.add))
                    for e in range(NX):
                        hold(v, p3["y_done"], d * NX + (e + 1))
                        if e:
                            v.wait_ge(v_chain, chain.n)
                        m = v.scalar_tensor_tensor(ot[:, :], y_ps[e % 2], wgt[:, e:e + 1],
                                                   ot[:, :], ALU.mult, ALU.add)
                        m.then_inc(p3["y_taken"], 1)
                        hold(v, p3["y_taken"], d * NX + (e + 3))
                    v.sem_inc(p3["out_ready"], 1)
        w3.close()


def pairs_ready(eng, p2, ptab, NX, TMAX):
    eng.wait_ge(p2["tab_ready"], 2)
    return eng.value_load(ptab[0:1, NX:NX + 1], min_val=1, max_val=TMAX // 2)


_INS = ['x', 'src', 'dst', 'L0_gnn_W', 'L0_gnn_att_src', 'L0_gnn_att_dst', 'L0_gnn_bias', 'L0_ffn_W1', 'L0_ffn_b1',
        'L0_ffn_Wg', 'L0_ffn_bg', 'L0_ffn_Wd', 'L0_ffn_bd', 'L1_gnn_W', 'L1_gnn_b', 'L1_ffn_Wr', 'L1_ffn_br',
        'L1_ffn_W1', 'L1_ffn_b1', 'L1_ffn_g1', 'L1_ffn_be1', 'L1_ffn_m1', 'L1_ffn_v1', 'L1_ffn_W2', 'L1_ffn_b2',
        'L1_ffn_g2', 'L1_ffn_be2', 'L1_ffn_m2', 'L1_ffn_v2', 'L1_ffn_Wo', 'L1_ffn_bo']
_OUTS = [((3125, 256), 'float32')]


def kernel(**inputs):
    import numpy as _np
    import concourse.bacc as _bacc
    from concourse import mybir as _mybir
    from concourse.bass_utils import run_bass_kernel_spmd as _run

    nc = _bacc.Bacc("TRN2", target_bir_lowering=False, num_devices=1)
    arrays, args = {}, []
    for name in _INS:
        a = _np.ascontiguousarray(inputs[name])
        arrays[f"in_{name}_dram"] = a
        args.append(nc.dram_tensor(f"in_{name}_dram", a.shape, _mybir.dt.from_np(a.dtype), kind="ExternalInput").ap())
    for i, (shape, dtype) in enumerate(_OUTS):
        dt = _mybir.dt.from_np(_np.dtype(dtype))
        args.append(nc.dram_tensor(f"out_{i}_dram", shape, dt, kind="ExternalOutput").ap())
    two_block_gnn(nc, *args)
    r = _run(nc, [arrays], core_ids=[0])
    got = tuple(r.results[0][f"out_{i}_dram"] for i in range(len(_OUTS)))
    return got[0]
```

```python
from contextlib import ExitStack

import concourse.bass as bass
from concourse import mybir

F32 = mybir.dt.float32
BF16 = mybir.dt.bfloat16
F16 = mybir.dt.float16
I32 = mybir.dt.int32
ALU = mybir.AluOpType
ACT = mybir.ActivationFunctionType
AX = mybir.AxisListType.X
RMAX = bass.bass_isa.ReduceOp.max

PT = 125
SLOTS = 17
CHUNKS = ((0, 6), (6, 12), (12, 17))
NCH = len(CHUNKS)
WIN = SLOTS * 128
BIG = 65536.0
MAGIC = 12582912.0
EPS_LN = 1e-5
EPS_BN = 1e-3
EPS_NORM = 1e-12
SLOPE = 0.2
NO_NODE = 1 << 20
LOW = 4096.0


class Chain:

    def __init__(self, eng, sem):
        self.eng, self.sem, self.n = eng, sem, 0

    def __call__(self, ins):
        self.n += 1
        ins.then_inc(self.sem, 1)
        self.eng.wait_ge(self.sem, self.n)

    def restart(self):
        self.eng.sem_clear(self.sem)
        self.n = 0


def one(ap, i, pat="p a c -> p (a c)"):
    return ap[:, bass.ds(i, 1)].rearrange(pat)


def two_block_gnn(nc, x, src, dst, g0_W, g0_as, g0_ad, g0_b, f0_W1, f0_b1, f0_Wg, f0_bg, f0_Wd, f0_bd,
                  g1_W, g1_b, f1_Wr, f1_br, f1_W1, f1_b1, f1_g1, f1_be1, f1_m1, f1_v1,
                  f1_W2, f1_b2, f1_g2, f1_be2, f1_m2, f1_v2, f1_Wo, f1_bo, out):
    N, C = x.shape
    E = src.shape[0]
    NT = N // PT
    HID = f0_W1.shape[1]
    NX = f0_Wd.shape[0]
    HEADS, HC = g0_as.shape
    KC = C // 128
    KH = HID // 128
    EC = E // PT
    EPT = EC // NT
    WA = C + 2 * HEADS
    TW = C + HEADS
    GW = TW + 4
    ROW = HID + C + 4
    REG = 26 * 128
    TMAX = 34
    UN = 5
    assert N % PT == 0 and E % PT == 0 and EC % NT == 0 and REG >= N + 128 and NT % UN == 0

    with ExitStack() as ctx:
        def sem(name, n=None):
            if n is None:
                return ctx.enter_context(nc.semaphore(name))
            return [ctx.enter_context(nc.semaphore(f"{name}{i}")) for i in range(n)]

        def allocator(c):
            return lambda name, shape, dt=F32: c.enter_context(nc.sbuf_tensor(name, shape, dt))

        def dram(name, shape, dt=F32):
            return nc.dram_tensor(name, shape, dt, kind="Internal").ap()

        sb = allocator(ctx)
        src_pad = dram("src_pad", (E + WIN,), I32)
        dst_pad = dram("dst_pad", (E + WIN,), I32)
        table0 = dram("table0", (N, TW))
        table1 = dram("table1", (N, 2 * C), F16)
        x2_rows = dram("x2_rows", (N, C))
        rs_rows = dram("rs_rows", (N, 1))
        sorted_rows = dram("sorted_rows", (NX * REG + 128, ROW))

        ps = [ctx.enter_context(nc.psum_tensor(f"bank{i}", [128, 512], F32)) for i in range(8)]

        iota_c = sb("iota_c", [128, 128])
        iota_p = sb("iota_p", [128, 1])
        tile_lo = sb("tile_lo", [128, NT])
        ident = sb("ident", [128, 128])
        eps_ln = sb("eps_ln", [128, 1])
        eps_bn = sb("eps_bn", [128, 1])
        wtab = sb("wtab", [1, 2, NT + 1], I32)
        deg_in = sb("deg_in", [PT, NT])
        src_win = sb("src_win", [128, SLOTS], I32)
        idx = sb("idx", [128, SLOTS], I32)
        dst_win = sb("dst_win", [128, SLOTS], I32)
        dloc = sb("dloc", [128, SLOTS])
        OH = sb("OH", [128, SLOTS, PT])
        G = sb("G", [128, SLOTS, GW])
        st = sb("st", [128, 2, 6])
        mv = sb("mv", [128, 2, 2])
        std = sb("std", [128, 2])
        rstd = sb("rstd", [128, 2])
        xn = [sb(f"xn{i}", [128, C]) for i in range(2)]
        xT = [sb(f"xT{i}", [128, KC, 128]) for i in range(2)]
        cnt = sb("cnt", [128, NX])
        region8 = sb("region8", [128, NX])
        bn_rows = [sb("bn_rowsA", [128, 128]), sb("bn_rowsB", [32, 128])]

        bnT = sb("bnT", [128, 10, NX, KC])

        v_chain = sem("v_chain")
        a_chain = sem("a_chain")
        p_chain = sem("p_chain")
        sink = sem("sink")

        def hold(eng, s, value):
            eng.wait_ge(s, value)
            eng.sem_inc(sink, 1)

        weights2 = ExitStack()
        s2w = allocator(weights2)
        Wd = s2w("Wd", [128, NX, KH, C])
        bdrow = s2w("bdrow", [128, NX, C])
        borrowed = Wd[:, :, :, :].rearrange("p e k c -> p (e k c)")
        weights0 = ExitStack()
        sw = allocator(weights0)
        XH = sw("XH", [PT, NT, WA])
        node = sw("node", [PT, NT, 3, 2 * HEADS], BF16)
        e_self = sw("e_self", [PT, NT, HEADS])
        tile_row = sw("tile_row", [128, NT])
        shi = sw("shi", [PT, EC])
        slo = sw("slo", [PT, EC])
        iota_b = sw("iota_b", [128, 128], BF16)
        before = sw("before", [128, 128], BF16)
        ones_b = sw("ones_b", [128, 128], BF16)
        zeros_b = sw("zeros_b", [128, 128], BF16)
        fW1 = sw("fW1", [128, KC, HID])
        fWg = sw("fWg", [128, KH, NX])
        bias0 = sw("bias0", [128, C])
        b1row = sw("b1row", [128, HID])
        bgrow = sw("bgrow", [128, NX])

        s_const = sem("s_const")
        loaded0 = sem("loaded0")
        edges_in = sem("edges_in")
        weights_in = sem("weights_in")
        padded = sem("padded")
        var_all = sem("var_all")
        std_all = sem("std_all")
        wm_ready = sem("wm_ready")
        wm_all = sem("wm_all")
        gm_ready = sem("gm_ready")
        gm_all = sem("gm_all")
        self_z = sem("self_z")
        self_e = sem("self_e")
        xn0 = sem("xn0")
        xT0_done = sem("xT0_done")
        xT0_copied = sem("xT0_copied")
        xh_done = sem("xh_done")
        xh_copied = sem("xh_copied")
        t0_written = sem("t0_written")

        def free_after(i, j):
            return i * UN + (j + 2 if j == 0 else j + 1)

        with ExitStack() as c0, nc.Block() as block:
            s0 = allocator(c0)
            X = s0("X", [PT, NT, C])
            W0 = s0("W0", [128, KC, WA])
            att = s0("att", [128, 2, C])
            wtmp = s0("wtmp", [128, C])
            iota_d = s0("iota_d", [128, NT])
            edge_no = s0("edge_no", [PT, EC])
            no_edge = s0("no_edge", [1, WIN], I32)
            stA = s0("stA", [PT, NT, 6])
            mvA = s0("mvA", [PT, NT, 2])
            stdA = s0("stdA", [PT, NT])
            rstdA = s0("rstdA", [PT, NT])
            srci = s0("srci", [PT, EC], I32)
            dsti = s0("dsti", [PT, EC], I32)
            tmpe = s0("tmpe", [PT, EC])
            dhi = s0("dhi", [PT, EC])
            other = borrowed[0:PT, 0:NT * EC // 2].bitcast(BF16).rearrange("p (t e) -> p t e", t=NT)
            bound = borrowed[0:PT, NT * EC // 2:NT * EC // 2 + NT * EC].rearrange("p (t e) -> p t e", t=NT)
            wmm = s0("wmm", [PT, 2, NT])
            wall = s0("wall", [PT, 2, NT])
            wa = s0("wa", [PT, NT])
            wb = s0("wb", [PT, NT])
            wc = s0("wc", [PT, NT + 1])
            ones_t = s0("ones_t", [PT, NT])
            gmax = s0("gmax", [PT, HEADS])
            gall = s0("gall", [PT, HEADS])
            sh = s0("sh", [PT, NT, HEADS])
            shift = s0("shift", [PT, NT, HEADS])
            rest = s0("rest", [PT, NT, 2 * HEADS])

            @block.gpsimd
            def _(pool):
                def iota(ap, pattern, cm):
                    pool.iota(ap, pattern, base=0, channel_multiplier=cm,
                              allow_small_or_imprecise_dtypes=True).then_inc(s_const, 1)
                iota(iota_c[:, :], [[1, 128]], 0)
                iota(iota_p[:, :], [[1, 1]], 1)
                iota(iota_d[:, :], [[1, NT]], 0)
                iota(tile_lo[:, :], [[PT, NT]], 0)
                iota(tile_row[:, :], [[PT, NT]], 1)
                iota(region8[:, :], [[REG, NX]], 0)
                iota(edge_no[:, :], [[1, EC]], EC)
                pool.memset(no_edge[:, :], -1).then_inc(s_const, 1)
                pool.wait_ge(wm_ready, 1)
                nc.gpsimd.partition_all_reduce(wall[:, :, :].rearrange("p a t -> p (a t)"),
                                               wmm[:, :, :].rearrange("p a t -> p (a t)"), PT, RMAX).then_inc(wm_all, 1)
                pool.wait_ge(gm_ready, 1)
                nc.gpsimd.partition_all_reduce(gall[:, :], gmax[:, :], PT, RMAX).then_inc(gm_all, 1)

            @block.sync
            def _(sp):
                sp.dma_start(X[:, :, :], x.rearrange("(t p) c -> p t c", p=PT)).then_inc(loaded0, 16)
                sp.dma_start(W0[:, :, 0:C], g0_W.rearrange("(k p) n -> p k n", p=128)).then_inc(loaded0, 16)
                sp.dma_start(att[:, 0, :], g0_as.rearrange("h c -> (h c)").partition_broadcast(128)).then_inc(loaded0, 16)
                sp.dma_start(att[:, 1, :], g0_ad.rearrange("h c -> (h c)").partition_broadcast(128)).then_inc(loaded0, 16)
                sp.dma_start(dsti[:, :], dst.rearrange("(p j) -> p j", p=PT)).then_inc(edges_in, 16)
                sp.dma_start(srci[:, :], src.rearrange("(p j) -> p j", p=PT)).then_inc(edges_in, 16)
                sp.dma_start(src_pad[0:E], src).then_inc(padded, 16)
                sp.dma_start(dst_pad[0:E], dst).then_inc(padded, 16)
                sp.dma_start(src_pad[E:E + WIN], src[0:WIN]).then_inc(padded, 16)
                sp.dma_start(fW1[:, :, :], f0_W1.rearrange("(k p) n -> p k n", p=128)).then_inc(weights_in, 16)
                sp.dma_start(fWg[:, :, :], f0_Wg.rearrange("(k p) n -> p k n", p=128)).then_inc(weights_in, 16)
                for tile, vec in ((bias0[:, :], g0_b), (b1row[:, :], f0_b1), (bgrow[:, :], f0_bg)):
                    sp.dma_start(tile, vec.partition_broadcast(128)).then_inc(weights_in, 16)
                for i, vec in enumerate((f1_b1, f1_g1, f1_be1, f1_m1, f1_v1, f1_b2, f1_g2, f1_be2, f1_m2, f1_v2)):
                    at = i * NX * KC
                    sp.dma_start(bn_rows[at // 128][at % 128:at % 128 + NX * KC, :],
                                 vec.rearrange("e (k p) -> (e k) p", p=128)).then_inc(weights_in, 16)
                sp.wait_ge(s_const, 8)
                sp.dma_start(dst_pad[E:E + WIN].rearrange("(a n) -> a n", a=1), no_edge[:, :]).then_inc(padded, 16)
                with sp.Fori(0, NT) as t:
                    sp.wait_ge(xh_copied, t + 3)
                    sp.dma_start(table0.rearrange("(t p) n -> t p n", p=PT)[bass.ds(t, 1), :, :].rearrange("a p n -> (a p) n"),
                                 XH[:, bass.ds(t, 1), 0:TW].rearrange("p a n -> p (a n)")).then_inc(t0_written, 16)
                sp.wait_ge(t0_written, 16 * NT)
                sp.wait_ge(padded, 64)
                sp.wait_ge(weights_in, 16 * 15)

            @block.scalar
            def _(act):
                act.wait_ge(var_all, 1)
                act.activation(stdA[:, :], mvA[:, :, 1], ACT.Sqrt, bias=eps_ln[0:PT, :]).then_inc(std_all, 1)
                with act.Fori(0, NT // UN) as i:
                    for j in range(UN):
                        act.wait_ge(xT0_done, i * UN + (j + 3))
                        hold(act, xh_done, free_after(i, j))
                        act.activation(xT[j % 2][:, :, 0:PT],
                                       ps[j % 2][:, 0:KC * PT].rearrange("p (k n) -> p k n", k=KC),
                                       ACT.Copy).then_inc(xT0_copied, 1)
                act.wait_ge(self_z, 1)
                act.activation(e_self[:, :, :], sh[:, :, :], ACT.Exp).then_inc(self_e, 1)

            @block.tensor
            def _(pe):
                pe.sem_inc(xT0_done, 2)
                pe.sem_inc(xh_done, 2)
                with pe.Fori(0, NT // UN) as i:
                    for j in range(UN):
                        hold(pe, xn0, i * UN + (j + 1))
                        for k in range(KC):
                            m = pe.transpose(ps[j % 2][:, k * PT:(k + 1) * PT], xn[j % 2][0:PT, k * 128:(k + 1) * 128],
                                             ident[0:PT, 0:PT])
                        m.then_inc(xT0_done, 1)
                        hold(pe, xT0_copied, i * UN + (j + 1))
                        hold(pe, xh_copied, free_after(i, j))
                        for k in range(KC):
                            m = pe.matmul(ps[2 + j % 2][0:PT, 0:WA], xT[j % 2][:, k, 0:PT], W0[:, k, :],
                                          start=(k == 0), stop=(k == KC - 1))
                        m.then_inc(xh_done, 1)

            @block.vector
            def _(v):
                chain = Chain(v, v_chain)
                v.sem_inc(xh_copied, 2)
                v.memset(eps_ln[:, :], EPS_LN)
                v.memset(eps_bn[:, :], EPS_BN)
                v.memset(ones_b[:, :], 1.0)
                v.memset(zeros_b[:, :], 0.0)
                v.memset(ones_t[:, :], 1.0)
                v.memset(G[:, :, TW:GW], 1.0)
                chain(v.memset(cnt[:, :], 0.0))
                v.wait_ge(s_const, 8)
                v.tensor_scalar(ident[:, :], iota_c[:, :], iota_p[:, :], None, ALU.is_equal)
                v.tensor_copy(iota_b[:, :], iota_c[:, :])
                chain(v.tensor_scalar(before[:, :], iota_c[:, :], iota_p[:, :], None, ALU.is_gt))
                v.wait_ge(loaded0, 64)
                for t in range(NT):
                    chain(v.bn_stats(stA[:, t, :], X[:, t, :]))
                for t in range(NT):
                    ins = v.bn_aggr(mvA[:, t, :], stA[:, t, :])
                    if t < NT - 1:
                        chain(ins)
                ins.then_inc(var_all, 1)
                for a in range(2):
                    for k in range(KC):
                        chain(v.tensor_tensor(wtmp[:, :], W0[:, k, 0:C], att[:, a, :], ALU.mult))
                        chain(v.tensor_reduce(W0[:, k, C + a * HEADS:C + (a + 1) * HEADS],
                                              wtmp[:, :].rearrange("p (h c) -> p h c", h=HEADS), AX, ALU.add))
                v.wait_ge(std_all, 1)
                chain(v.reciprocal(rstdA[:, :], stdA[:, :]))
                with v.Fori(0, NT // UN) as i:
                    for j in range(UN):
                        hold(v, xT0_done, free_after(i, j))
                        v.tensor_scalar(xn[j % 2][0:PT, :], one(X, i * UN + j),
                                        one(mvA[:, :, 0:1], i * UN + j), rstdA[:, bass.ds(i * UN + j, 1)],
                                        ALU.subtract, ALU.mult).then_inc(xn0, 1)
                        hold(v, xh_done, i * UN + (j + 3))
                        v.tensor_copy(one(XH, i * UN + j), ps[2 + j % 2][0:PT, 0:WA]).then_inc(xh_copied, 1)
                chain.restart()
                v.wait_ge(xh_copied, NT + 2)
                v.tensor_reduce(gmax[:, :], XH[:, :, C:TW].rearrange("p t h -> p h t"), AX, ALU.max).then_inc(gm_ready, 1)
                v.wait_ge(edges_in, 32)
                for ends, hi in ((dsti, dhi), (srci, shi)):
                    chain(v.tensor_scalar(tmpe[:, :], ends[:, :], 1.0 / PT, -0.5 + 0.5 / PT, ALU.mult, ALU.add))
                    chain(v.tensor_scalar(tmpe[:, :], tmpe[:, :], MAGIC, None, ALU.add))
                    chain(v.tensor_scalar(hi[:, :], tmpe[:, :], -MAGIC, None, ALU.add))
                chain(v.tensor_scalar(tmpe[:, :], shi[:, :], -float(PT), None, ALU.mult))
                chain(v.tensor_tensor(slo[:, :], tmpe[:, :], srci[:, :], ALU.add))
                chain(v.tensor_tensor(other[:, :, :], dhi[:, :].unsqueeze(1).broadcast_to([PT, NT, EC]),
                                      iota_d[0:PT, :].unsqueeze(2).broadcast_to([PT, NT, EC]), ALU.not_equal))
                for side, s in enumerate((BIG, -BIG)):
                    chain(v.scalar_tensor_tensor(bound[:, :, :], other[:, :, :], s,
                                                 edge_no[:, :].unsqueeze(1).broadcast_to([PT, NT, EC]),
                                                 ALU.mult, ALU.add))
                    chain(v.tensor_reduce(wmm[:, side, :], bound[:, :, :], AX, ALU.min if side == 0 else ALU.max))
                v.tensor_scalar(wmm[:, 0, :], wmm[:, 0, :], -1.0, None, ALU.mult).then_inc(wm_ready, 1)
                v.wait_ge(gm_all, 1)
                v.wait_ge(wm_ready, 1)
                chain(v.tensor_copy(rest[:, :, 0:HEADS], XH[:, :, TW:WA]))
                chain(v.tensor_tensor(sh[:, :, :], XH[:, :, TW:WA],
                                      gall[:, :].unsqueeze(1).broadcast_to([PT, NT, HEADS]), ALU.add))
                chain(v.scalar_tensor_tensor(shift[:, :, :], sh[:, :, :], SLOPE, sh[:, :, :], ALU.mult, ALU.max))
                chain(v.tensor_copy(rest[:, :, HEADS:2 * HEADS], shift[:, :, :]))
                for part in range(3):
                    chain(v.tensor_copy(node[:, :, part, :], rest[:, :, :]))
                    if part < 2:
                        chain(v.tensor_tensor(rest[:, :, :], rest[:, :, :], node[:, :, part, :], ALU.subtract))
                chain(v.tensor_tensor(e_self[:, :, :], XH[:, :, C:TW], XH[:, :, TW:WA], ALU.add))
                chain(v.scalar_tensor_tensor(e_self[:, :, :], e_self[:, :, :], SLOPE, e_self[:, :, :],
                                             ALU.mult, ALU.max))
                v.tensor_tensor(sh[:, :, :], e_self[:, :, :], shift[:, :, :], ALU.subtract).then_inc(self_z, 1)
                v.wait_ge(wm_all, 1)
                chain(v.tensor_scalar(wa[:, :], wall[:, 0, :], -1.0, float(E - 1), ALU.mult, ALU.min))
                chain(v.tensor_tensor(wb[:, :], wall[:, 1, :], wa[:, :], ALU.subtract))
                chain(v.tensor_scalar(wb[:, :], wb[:, :], 1.0, 1.0, ALU.add, ALU.max))
                chain(v.tensor_scalar(wb[:, :], wb[:, :], 1.0 / WIN, 0.5 - 0.5 / WIN, ALU.mult, ALU.add))
                chain(v.tensor_scalar(wb[:, :], wb[:, :], MAGIC, None, ALU.add))
                chain(v.tensor_scalar(wb[:, :], wb[:, :], -MAGIC, None, ALU.add))
                chain(v.memset(wc[:, 0:1], 0.0))
                chain(v.tensor_tensor_scan(wc[:, 1:NT + 1], ones_t[:, :], wb[:, :], 0.0, ALU.mult, ALU.add))
                chain(v.tensor_copy(wtab[0:1, 0, 0:NT], wa[0:1, :]))
                chain(v.tensor_copy(wtab[0:1, 1, :], wc[0:1, :]))
                v.wait_ge(self_e, 1)

        def extra_passes(eng, first, last, body):
            with eng.If(first + 1 < last):
                with eng.Fori(first + 1, last) as q:
                    body(q)

        def window_passes(eng, d):
            first = eng.value_load(wtab[0:1, 1, bass.ds(d, 1)], min_val=0, max_val=NT * 23)
            last = eng.value_load(wtab[0:1, 1, bass.ds(d + 1, 1)], min_val=1, max_val=NT * 23)
            return first, last

        def load_windows(sp, taken_src, taken_dst, win_src, win_dst, row=None):
            with sp.Fori(0, NT) as d:
                first, last = window_passes(sp, d)
                start = sp.value_load(wtab[0:1, 0, bass.ds(d, 1)], min_val=0, max_val=E - 1)
                with sp.Fori(first, last) as q:
                    at = nc.s_assert_within((q - first) * WIN + start, 0, E, 
                                            skip_runtime_bounds_check_because="a pass starts inside its window")
                    sp.wait_ge(taken_src, q + 1)
                    sp.dma_start(src_win[:, :], src_pad[bass.ds(at, WIN)].rearrange("(p j) -> p j", p=128))\
                        .then_inc(win_src, 16)
                    sp.wait_ge(taken_dst, q + 1)
                    sp.dma_start(dst_win[:, :], dst_pad[bass.ds(at, WIN)].rearrange("(p j) -> p j", p=128))\
                        .then_inc(win_dst, 16)
                    if row is not None:
                        dst_row, win_row = row
                        sp.dma_start(dst_row[:, :], dst_pad[bass.ds(at, WIN)].partition_broadcast(PT))\
                            .then_inc(win_row, 16)

        def rows16(j):
            return G[:, j, 0:C].bitcast(F16)

        def gather_pass(pool, q, table, rows, win_src, taken_src, seg_done, idx_ready, got, between=None):
            hold(pool, win_src, q * 16 + 16)
            for c, (j0, j1) in enumerate(CHUNKS):
                if between and c == NCH - 1:
                    between()
                hold(pool, seg_done, q * NCH + (c + 1))
                pool.tensor_copy(idx[:, j0:j1], src_win[:, j0:j1]).then_inc(idx_ready, 1)
                hold(pool, idx_ready, q * NCH + (c + 1))
                if c == NCH - 1:
                    pool.sem_inc(taken_src, 1)
                for j in range(j0, j1):
                    pool.indirect_dma_start(rows(j), None, table,
                                            bass.IndirectOffsetOnAxis(idx[:, j:j + 1], 0)).then_inc(got[c], 16)

        def stagger(eng, tile):
            tile(0, True, False, True)
            with eng.Fori(1, NT - 1) as d:
                tile(d, True, True, True)
            tile(NT - 1, True, True, False)
            tile(NT, False, True, False)

        p1 = {n: sem("gat_" + n) for n in (
            "win_src", "win_dst", "win_row", "taken_src", "taken_dst", "idx_ready", "masks_ready", "adm_ready",
            "z_ready", "w_ready", "msgs_ready", "seg_done", "self_ready", "var_ready", "std_ready", "xn_ready",
            "xT_done", "xT_copied", "h_done", "hpre_ready", "gelu_done", "ht_done", "ht_copied", "gate_done",
            "lmax_ready", "lexp_done", "sel_ready", "rank_done", "pos_ready", "scattered", "x_in", "x_used", "x1_ready", "hist_ready", "hist_done",
            "pad_ready")}
        weights2_in = sem("weights2_in")
        got1 = sem("gat_got", NCH)
        with ExitStack() as c1, nc.Block() as block:
            s1 = allocator(c1)
            dst_row = s1("dst_row", [PT, WIN], I32)
            OHT = s1("OHT", [PT, WIN], BF16)
            ads = s1("ads", [128, SLOTS, 2 * HEADS])
            lg4 = s1("lg4", [128, SLOTS, HEADS])
            selfm = s1("selfm", [PT, TW + 1])
            row = s1("row", [128, ROW])
            hpre = s1("hpre", [128, HID])
            HT = s1("HT", [128, KH, PT])
            r4 = s1("r4", [PT, HEADS])
            lg = s1("lg", [PT, NX])
            lex = s1("lex", [PT, NX])
            nmx = s1("nmx", [PT, 1])
            se = s1("se", [PT, 1])
            cand = s1("cand", [PT, NX])
            amin = s1("amin", [PT, 1])
            sel = s1("sel", [PT, NX])
            selb = s1("selb", [PT, NX], BF16)
            pos = s1("pos", [PT, NX])
            pos1 = s1("pos1", [PT, 1])
            posi = s1("posi", [PT, 1], I32)
            xt = s1("xt", [PT, C])
            x1 = s1("x1", [PT, C])
            ohi = s1("ohi", [PT, EPT, NT], BF16)
            olo = s1("olo", [PT, EPT, PT], BF16)
            acc, hist, misc = ps[0], ps[2], ps[3]
            adm = ps[1]
            PW = 3 * 2 * HEADS
            gate_ps = misc[0:PT, 256:256 + NX]
            rank_ps = misc[0:PT, 272:272 + NX]
            all_ps = misc[0:PT, 288:288 + NX]

            @block.sync
            def _(sp):
                sp.dma_start(bdrow[:, :, :].rearrange("p e c -> p (e c)"),
                             f0_bd.rearrange("e c -> (e c)").partition_broadcast(128)).then_inc(weights2_in, 16)
                for e in range(NX):
                    sp.dma_start(Wd[:, e, :, :], f0_Wd[e].rearrange("(k p) n -> p k n", p=128)).then_inc(weights2_in, 16)
                load_windows(sp, p1["taken_src"], p1["taken_dst"], p1["win_src"], p1["win_dst"],
                             (dst_row, p1["win_row"]))
                sp.wait_ge(weights2_in, 16 * (NX + 1))
                sp.wait_ge(p1["scattered"], 16 * (NT + 1))

            @block.gpsimd
            def _(pool):
                pool.sem_inc(p1["taken_src"], 1)
                pool.wait_ge(p1["pad_ready"], 1)
                pool.dma_start(sorted_rows[NX * REG:NX * REG + 128, :], row[:, :]).then_inc(p1["scattered"], 16)

                def scatter(d):
                    hold(pool, p1["gelu_done"], d * 2 + 2)
                    hold(pool, p1["pos_ready"], d + 1)
                    pool.indirect_dma_start(sorted_rows, bass.IndirectOffsetOnAxis(posi[:, :], 0),
                                            row[0:PT, :], None).then_inc(p1["scattered"], 16)

                def gathers(d, between=None):
                    def one_pass(q, between=None):
                        gather_pass(pool, q, table0, lambda j: G[:, j, 0:TW], p1["win_src"], p1["taken_src"], p1["seg_done"],
                                    p1["idx_ready"], got1, between)
                    first, last = window_passes(pool, d)
                    one_pass(first, between)
                    extra_passes(pool, first, last, one_pass)
                gathers(0)
                gathers(1)
                with pool.Fori(2, NT) as d:
                    gathers(d, lambda: scatter(d - 2))
                scatter(NT - 2)
                scatter(NT - 1)

            @block.scalar
            def _(act):
                xv = x.rearrange("(t p) c -> t p c", p=PT)

                def weights(q, c):
                    j0, j1 = CHUNKS[c]
                    act.wait_ge(p1["z_ready"], q * NCH + (c + 1))
                    act.activation(G[:, j0:j1, C:TW], lg4[:, j0:j1, :], ACT.Exp).then_inc(p1["w_ready"], 1)

                def tile(d, sums, finish, ahead):
                    p = d - 1
                    if sums:
                        first, last = window_passes(act, d)
                    if finish:
                        act.wait_ge(p1["var_ready"], p + 1)
                        act.activation(std[0:PT, 0:1], mv[0:PT, 0, 1:2], ACT.Sqrt, bias=eps_ln[0:PT, :])\
                            .then_inc(p1["std_ready"], 1)
                    if sums:
                        act.dma_start(xt[:, :], xv[bass.ds(d, 1), :, :].rearrange("a p c -> (a p) c"))\
                            .then_inc(p1["x_in"], 16)
                        weights(first, 0)
                    if finish:
                        act.wait_ge(p1["xT_done"], p + 1)
                        act.activation(xT[0][:, :, 0:PT], misc[:, 0:KC * PT].rearrange("p (k n) -> p k n", k=KC),
                                       ACT.Copy).then_inc(p1["xT_copied"], 1)
                    if sums:
                        weights(first, 1)
                    if finish:
                        hold(act, p1["scattered"], p * 16 + 16)
                        act.activation(row[0:PT, HID:HID + C], x1[:, :], ACT.Copy)
                        for half in range(2):
                            act.wait_ge(p1["hpre_ready"], p * 2 + (half + 1))
                            s = slice(half * 512, (half + 1) * 512)
                            act.activation(row[0:PT, s], hpre[0:PT, s], ACT.Gelu).then_inc(p1["gelu_done"], 1)
                        for half in range(2):
                            act.wait_ge(p1["ht_done"], p * 2 + (half + 1))
                            act.activation(HT[:, half * (KH // 2):(half + 1) * (KH // 2), :],
                                           ps[6 + half][:, 0:KH // 2 * PT].rearrange("p (k n) -> p k n", n=PT),
                                           ACT.Copy).then_inc(p1["ht_copied"], 1)
                    if sums:
                        weights(first, 2)
                    if finish:
                        act.wait_ge(p1["lmax_ready"], p + 1)
                        act.activation(lex[:, :], lg[:, :], ACT.Exp, bias=nmx[:, :], accum_out=se[:, :])\
                            .then_inc(p1["lexp_done"], 1)
                    if sums:
                        extra_passes(act, first, last, lambda q: [weights(q, c) for c in range(NCH)])
                stagger(act, tile)

            @block.tensor
            def _(pe):
                pe.matmul(hist[0:PT, 0:NT], zeros_b[0:PT, 0:PT], zeros_b[0:PT, 0:NT], start=True, stop=False,
                          skip_group_check=True)

                def to_edges(q, d):
                    hold(pe, p1["masks_ready"], q + 1)
                    for j in range(SLOTS):
                        m = pe.matmul(adm[:, j * PW:(j + 1) * PW], OHT[:, j * 128:(j + 1) * 128],
                                      one(node, d, "p a s n -> p (a s n)"), start=True, stop=True)
                    m.then_inc(p1["adm_ready"], 1)

                def sums_of(q, c):
                    j0, j1 = CHUNKS[c]
                    hold(pe, p1["msgs_ready"], q * NCH + (c + 1))
                    for j in range(j0, j1):
                        m = pe.matmul(acc[0:PT, 0:TW + 1], OH[:, j, :], G[:, j, 0:TW + 1], start=False,
                                      stop=False, skip_group_check=True)
                    m.then_inc(p1["seg_done"], 1)

                def tile(d, sums, finish, ahead):
                    p = d - 1
                    if sums:
                        first, last = window_passes(pe, d)
                        hold(pe, p1["self_ready"], d + 1)
                        pe.matmul(acc[0:PT, 0:TW + 1], ident[0:PT, 0:PT], selfm[:, :], start=True, stop=False,
                                  skip_group_check=True)
                    if finish:
                        hold(pe, p1["xn_ready"], p + 1)
                        for k in range(KC):
                            m = pe.transpose(misc[:, k * PT:(k + 1) * PT], xn[0][0:PT, k * 128:(k + 1) * 128],
                                             ident[0:PT, 0:PT])
                        m.then_inc(p1["xT_done"], 1)
                    if sums:
                        sums_of(first, 0)
                    if finish:
                        hold(pe, p1["xT_copied"], p + 1)
                        for half in range(2):
                            for k in range(KC):
                                m = pe.matmul(ps[4 + half][0:PT, :], xT[0][:, k, 0:PT],
                                              fW1[:, k, half * 512:(half + 1) * 512],
                                              start=(k == 0), stop=(k == KC - 1))
                            m.then_inc(p1["h_done"], 1)
                    if sums:
                        sums_of(first, 1)
                        hold(pe, p1["hist_ready"], d + 1)
                        for j in range(EPT):
                            m = pe.matmul(hist[0:PT, 0:NT], olo[:, j, :], ohi[:, j, :], start=False, stop=False,
                                          skip_group_check=True)
                        m.then_inc(p1["hist_done"], 1)
                    if finish:
                        for half in range(2):
                            hold(pe, p1["gelu_done"], p * 2 + (half + 1))
                            for k in range(KH // 2):
                                kk = half * (KH // 2) + k
                                m = pe.transpose(ps[6 + half][:, k * PT:(k + 1) * PT],
                                                 row[0:PT, kk * 128:(kk + 1) * 128], ident[0:PT, 0:PT])
                            m.then_inc(p1["ht_done"], 1)
                        for k in range(KH):
                            if k % (KH // 2) == 0:
                                hold(pe, p1["ht_copied"], p * 2 + (k // (KH // 2) + 1))
                            m = pe.matmul(gate_ps, HT[:, k, :], fWg[:, k, :], start=(k == 0), stop=(k == KH - 1))
                        m.then_inc(p1["gate_done"], 1)
                    if sums:
                        sums_of(first, 2)
                    if finish:
                        hold(pe, p1["sel_ready"], p + 1)
                        pe.matmul(rank_ps, before[0:PT, 0:PT], selb[:, :], start=True, stop=True)
                        pe.matmul(all_ps, ones_b[0:PT, 0:PT], selb[:, :], start=True, stop=True)\
                            .then_inc(p1["rank_done"], 1)
                    if sums:
                        def again(q):
                            to_edges(q, d)
                            for c in range(NCH):
                                sums_of(q, c)
                        extra_passes(pe, first, last, again)
                    if ahead:
                        to_edges(last, d + 1)
                to_edges(0, 0)
                stagger(pe, tile)

            @block.vector
            def _(v):
                chain = Chain(v, v_chain)
                chain.restart()
                chain(v.memset(row[:, :], 0.0))
                v.memset(row[:, HID + C + 1:HID + C + 2].bitcast(I32), NO_NODE).then_inc(p1["pad_ready"], 1)
                v.sem_inc(p1["taken_dst"], 1)
                v.sem_inc(p1["seg_done"], NCH)

                def local_targets(q, d):
                    hold(v, p1["win_dst"], q * 16 + 16)
                    chain(v.tensor_scalar(dloc[:, :], dst_win[:, :], tile_lo[:, bass.ds(d, 1)], None, ALU.subtract))
                    hold(v, p1["win_row"], q * 16 + 16)

                def node_masks(q, d):
                    chain(v.tensor_scalar(
                        OHT[:, :].rearrange("p (j e) -> p j e", e=128),
                        dst_row[:, :].rearrange("p (e j) -> p j e", j=SLOTS),
                        tile_row[0:PT, bass.ds(d, 1)], None, ALU.is_equal))
                    v.sem_inc(p1["masks_ready"], 1)
                    v.sem_inc(p1["taken_dst"], 1)

                def edge_masks(q, c):
                    j0, j1 = CHUNKS[c]
                    hold(v, p1["seg_done"], q * NCH + (c + 1))
                    chain(v.tensor_tensor(OH[:, j0:j1, :],
                                          iota_c[:, 0:PT].unsqueeze(1).broadcast_to([128, j1 - j0, PT]),
                                          dloc[:, j0:j1].unsqueeze(2).broadcast_to([128, j1 - j0, PT]), ALU.is_equal))

                def node_values(q):
                    hold(v, p1["adm_ready"], q + 1)
                    chain(v.tensor_reduce(ads[:, :, :],
                                          adm[:, 0:SLOTS * PW].rearrange("p (j s n) -> p j n s", s=3, n=2 * HEADS),
                                          AX, ALU.add))

                def logits(q, c):
                    j0, j1 = CHUNKS[c]
                    a = ads[:, j0:j1, :]
                    hold(v, got1[c], (q + 1) * (16 * (j1 - j0)))
                    z = lg4[:, j0:j1, :]
                    chain(v.tensor_tensor(z, G[:, j0:j1, C:TW], a[:, :, 0:HEADS], ALU.add))
                    chain(v.scalar_tensor_tensor(z, z, SLOPE, z, ALU.mult, ALU.max))
                    chain(v.tensor_tensor(z, z, a[:, :, HEADS:2 * HEADS], ALU.subtract))
                    v.tensor_scalar(z, z, 0.0, None, ALU.min).then_inc(p1["z_ready"], 1)

                def messages(q, c):
                    j0, j1 = CHUNKS[c]
                    hold(v, p1["w_ready"], q * NCH + (c + 1))
                    g4 = G[:, j0:j1, 0:C].rearrange("p j (h c) -> p j h c", h=HEADS)
                    v.tensor_tensor(g4, g4, G[:, j0:j1, C:TW].unsqueeze(3).broadcast_to([128, j1 - j0, HEADS, HC]),
                                    ALU.mult).then_inc(p1["msgs_ready"], 1)

                def tile(d, sums, finish, ahead):
                    p = d - 1
                    chain.restart()
                    if sums:
                        first, last = window_passes(v, d)
                        chain(v.tensor_tensor(selfm[:, 0:C].rearrange("p (h c) -> p h c", h=HEADS),
                                              XH[:, bass.ds(d, 1), 0:C].rearrange("p a (h c) -> p (a h) c", h=HEADS),
                                              one(e_self, d).unsqueeze(2).broadcast_to([PT, HEADS, HC]), ALU.mult))
                        chain(v.tensor_copy(selfm[:, C:TW], one(e_self, d)))
                        v.memset(selfm[:, TW:TW + 1], 0.0).then_inc(p1["self_ready"], 1)
                        node_values(first)
                        logits(first, 0)
                    if finish:
                        hold(v, p1["std_ready"], p + 1)
                        chain(v.reciprocal(rstd[0:PT, 0:1], std[0:PT, 0:1]))
                        v.tensor_scalar(xn[0][0:PT, :], x1[:, :], mv[0:PT, 0, 0:1], rstd[0:PT, 0:1], ALU.subtract,
                                        ALU.mult).then_inc(p1["xn_ready"], 1)
                    if sums:
                        messages(first, 0)
                        edge_masks(first, 2)
                        chain(v.tensor_tensor(olo[:, :, :], iota_b[0:PT, 0:PT].unsqueeze(1).broadcast_to([PT, EPT, PT]),
                                              slo[:, bass.ds(d * EPT, EPT)].unsqueeze(2).broadcast_to([PT, EPT, PT]),
                                              ALU.is_equal))
                        v.tensor_tensor(ohi[:, :, :], iota_b[0:PT, 0:NT].unsqueeze(1).broadcast_to([PT, EPT, NT]),
                                        shi[:, bass.ds(d * EPT, EPT)].unsqueeze(2).broadcast_to([PT, EPT, NT]),
                                        ALU.is_equal).then_inc(p1["hist_ready"], 1)
                        logits(first, 1)
                        messages(first, 1)
                    if finish:
                        for half in range(2):
                            hold(v, p1["h_done"], p * 2 + (half + 1))
                            s = slice(half * 512, (half + 1) * 512)
                            v.tensor_tensor(hpre[0:PT, s], ps[4 + half][0:PT, :], b1row[0:PT, s], ALU.add)\
                                .then_inc(p1["hpre_ready"], 1)
                    if sums:
                        logits(first, 2)
                        messages(first, 2)
                    if finish:
                        hold(v, p1["gate_done"], p + 1)
                        chain(v.tensor_tensor(lg[:, :], gate_ps, bgrow[0:PT, :], ALU.add))
                        chain(v.tensor_reduce(amin[:, :], lg[:, :], AX, ALU.max))
                        v.tensor_scalar(nmx[:, :], amin[:, :], -1.0, None, ALU.mult).then_inc(p1["lmax_ready"], 1)
                        chain(v.tensor_scalar(cand[:, :], lg[:, :], amin[:, :], BIG, ALU.is_lt, ALU.mult))
                        chain(v.tensor_tensor(cand[:, :], cand[:, :], iota_c[0:PT, 0:NX], ALU.add))
                        chain(v.tensor_reduce(amin[:, :], cand[:, :], AX, ALU.min))
                        chain(v.tensor_scalar(sel[:, :], iota_c[0:PT, 0:NX], amin[:, :], None, ALU.is_equal))
                        v.tensor_copy(selb[:, :], sel[:, :]).then_inc(p1["sel_ready"], 1)
                        hold(v, p1["lexp_done"], p + 1)
                        hold(v, p1["scattered"], p * 16 + 16)
                        chain(v.reciprocal(row[0:PT, HID + C:HID + C + 1], se[:, :]))
                        chain(v.tensor_copy(row[0:PT, HID + C + 1:HID + C + 2].bitcast(I32),
                                            tile_row[0:PT, bass.ds(p, 1)]))
                        hold(v, p1["rank_done"], p + 1)
                        chain(v.tensor_tensor(pos[:, :], rank_ps, cnt[0:PT, :], ALU.add))
                        chain(v.tensor_tensor(pos[:, :], pos[:, :], region8[0:PT, :], ALU.add))
                        chain(v.tensor_tensor(pos[:, :], pos[:, :], sel[:, :], ALU.mult))
                        chain(v.tensor_reduce(pos1[:, :], pos[:, :], AX, ALU.add))
                        chain(v.tensor_tensor(cnt[0:PT, :], cnt[0:PT, :], all_ps, ALU.add))
                        v.tensor_copy(posi[:, :], pos1[:, :]).then_inc(p1["pos_ready"], 1)
                    if sums:
                        def again(q):
                            chain.restart()
                            local_targets(q, d)
                            node_masks(q, d)
                            for c in range(NCH):
                                edge_masks(q, c)
                            node_values(q)
                            for c in range(NCH):
                                logits(q, c)
                                messages(q, c)
                        extra_passes(v, first, last, again)
                        chain.restart()
                        if ahead:
                            local_targets(last, d + 1)
                            node_masks(last, d + 1)
                            edge_masks(last, 0)
                            edge_masks(last, 1)
                        hold(v, p1["seg_done"], last * NCH + NCH)
                        hold(v, p1["hist_done"], d + 1)
                        if finish:
                            hold(v, p1["gelu_done"], p * 2 + 2)
                        chain(v.reciprocal(r4[:, :], acc[0:PT, C:TW]))
                        chain(v.tensor_tensor(x1[:, :].rearrange("p (h c) -> p h c", h=HEADS),
                                              acc[0:PT, 0:C].rearrange("p (h c) -> p h c", h=HEADS),
                                              r4[:, :].unsqueeze(2).broadcast_to([PT, HEADS, HC]), ALU.mult))
                        chain(v.tensor_copy(deg_in[:, bass.ds(d, 1)], acc[0:PT, TW:TW + 1]))
                        chain(v.tensor_tensor(x1[:, :], x1[:, :], bias0[0:PT, :], ALU.add))
                        hold(v, p1["x_in"], d * 16 + 16)
                        chain(v.tensor_tensor(x1[:, :], x1[:, :], xt[:, :], ALU.add))
                        chain(v.bn_stats(st[0:PT, 0, :], x1[:, :]))
                        v.bn_aggr(mv[0:PT, 0, :], st[0:PT, 0, :]).then_inc(p1["var_ready"], 1)
                local_targets(0, 0)
                node_masks(0, 0)
                edge_masks(0, 0)
                edge_masks(0, 1)
                stagger(v, tile)

        hist = ps[2]
        p2 = {n: sem("moe_" + n) for n in (
            "deg_ready", "sq_ready", "rs_ready", "tab_ready", "filled", "pads", "ht_done",
            "ht_copied", "y_done", "var_ready", "std_ready", "ids_ready", "rs_got", "x2_ready", "h_ready",
            "bnt_done", "row_used", "x1_kept")}
        rin = sem("rin", 2)
        sent = sem("sent", 2)
        weights0.close()
        with ExitStack() as c2, nc.Block() as block:
            s2 = allocator(c2)
            rbuf = [s2(f"rbuf{i}", [128, ROW]) for i in range(2)]
            HT = [s2(f"HTb{i}", [128, KH, 128]) for i in range(2)]
            pads = s2("pads", [128, ROW])
            degs = s2("degs", [PT, 2, NT])
            sqs = s2("sqs", [PT, 2, NT])
            rsq = s2("rsq", [PT, 2, NT])
            nt8 = s2("nt8", [128, NX])
            ct8 = s2("ct8", [128, NX])
            one8 = s2("one8", [128, NX])
            ge = s2("ge", [128, TMAX, NX])
            gn = s2("gn", [128, TMAX, NX])
            te = s2("te", [128, TMAX])
            ts_ = s2("ts_", [128, TMAX])
            tr = s2("tr", [128, TMAX])
            ttab = s2("ttab", [1, 2, TMAX], I32)
            ptab = s2("ptab", [1, NX + 1], I32)
            pf = s2("pf", [128, NX + 1])
            ids = [s2(f"ids{i}", [128, 1], I32) for i in range(2)]
            rsg = [s2(f"rsg{i}", [128, 1]) for i in range(2)]
            x1p = [s2(f"x1p{i}", [128, C + 1]) for i in range(2)]
            x2 = [s2(f"x2_{i}", [128, C]) for i in range(2)]
            hx = [s2(f"hx{i}", [128, C]) for i in range(2)]
            hparts = [s2(f"hparts{i}", [128, 2, C], F16) for i in range(2)]

            def last_pair(eng):
                eng.wait_ge(p2["tab_ready"], 2)
                return eng.value_load(ptab[0:1, NX:NX + 1], min_val=1, max_val=TMAX // 2 - 1)

            def by_pairs(eng, turn, finish):
                last = last_pair(eng)
                turn(0, 0)
                with eng.Fori(0, last) as u:
                    turn(u, 1)
                    finish(u, 0)
                    turn(u + 1, 0)
                    finish(u, 1)
                turn(last, 1)
                finish(last, 0)
                finish(last, 1)

            @block.sync
            def _(sp):
                sp.wait_ge(p2["tab_ready"], 2)
                for e in range(NX):
                    at = sp.value_load(ptab[0:1, e:e + 1], min_val=0, max_val=NX * REG)
                    sp.dma_start(sorted_rows[bass.ds(at, 128), :], pads[:, :]).then_inc(p2["pads"], 16)
                sp.wait_ge(p2["pads"], 16 * NX)
                last = last_pair(sp)
                with sp.Fori(0, last + 1) as u:
                    for b in range(2):
                        at = sp.value_load(ttab[0:1, 1, bass.ds(u * 2 + b, 1)], min_val=0, max_val=NX * REG)
                        sp.wait_ge(p2["row_used"], u * 2 + (b + 1))
                        sp.dma_start(rbuf[b][:, :], sorted_rows[bass.ds(at, 128), :]).then_inc(rin[b], 16)
                for b in range(2):
                    hold(sp, sent[b], last * 32 + 48)

            @block.gpsimd
            def _(pool):
                pool.wait_ge(p2["rs_ready"], 1)
                half = NT // 2
                with nc.allow_non_contiguous_dma(reason="one value a node, once"):
                    for b, (t0, t1) in enumerate(((0, half), (half, NT))):
                        pool.dma_start(rs_rows[t0 * PT:t1 * PT, :].rearrange("(t p) a -> p (t a)", p=PT),
                                       rsq[:, 0, t0:t1]).then_inc(sent[b], 16)
                for b in range(2):
                    pool.wait_ge(sent[b], 16)
                last = last_pair(pool)
                with pool.Fori(0, last + 1) as u:
                    for b in range(2):
                        hold(pool, p2["ids_ready"], u * 2 + (b + 1))
                        pool.indirect_dma_start(rsg[b][:, :], None, rs_rows, bass.IndirectOffsetOnAxis(ids[b][:, :], 0),
                                                bounds_check=N - 1, oob_is_err=False).then_inc(p2["rs_got"], 16)
                        hold(pool, p2["h_ready"], u * 2 + (b + 1))
                        pool.indirect_dma_start(x2_rows, bass.IndirectOffsetOnAxis(ids[b][:, :], 0), x2[b][:, :], None,
                                                bounds_check=N - 1, oob_is_err=False).then_inc(sent[b], 16)
                        pool.indirect_dma_start(table1, bass.IndirectOffsetOnAxis(ids[b][:, :], 0), hparts[b][:, :, :].rearrange("p s c -> p (s c)"), None,
                                                bounds_check=N - 1, oob_is_err=False).then_inc(sent[b], 16)

            @block.scalar
            def _(act):
                act.wait_ge(p2["deg_ready"], 1)
                act.activation(sqs[:, :, :], degs[:, :, :], ACT.Sqrt).then_inc(p2["sq_ready"], 1)

                def turn(u, b):
                    hold(act, p2["y_done"], u * 2 + (b + 1))
                    for half in range(2):
                        act.wait_ge(p2["ht_done"], u * 4 + (2 * b + half + 1))
                        act.activation(HT[b][:, half * (KH // 2):(half + 1) * (KH // 2), :],
                                       ps[2 * b + half][:, :].rearrange("p (k n) -> p k n", n=128),
                                       ACT.Copy).then_inc(p2["ht_copied"], 1)

                def finish(u, b):
                    act.wait_ge(p2["var_ready"], u * 2 + (b + 1))
                    act.activation(std[:, b:b + 1], mv[:, b, 1:2], ACT.Sqrt, bias=eps_ln[:, :])\
                        .then_inc(p2["std_ready"], 1)
                by_pairs(act, turn, finish)

            @block.tensor
            def _(pe):
                pe.transpose(ps[7][:, 0:128], bn_rows[0][:, :], ident[:, :])
                pe.transpose(ps[7][:, 128:160], bn_rows[1][:, :], ident[0:32, 0:32]).then_inc(p2["bnt_done"], 1)
                pe.sem_inc(p2["y_done"], 2)

                def turn(u, b):
                    hold(pe, rin[b], u * 16 + 16)
                    hold(pe, p2["ht_copied"], u * 4 + (2 * b + 2))
                    for half in range(2):
                        for k in range(KH // 2):
                            kk = half * (KH // 2) + k
                            m = pe.transpose(ps[2 * b + half][:, k * 128:(k + 1) * 128],
                                             rbuf[b][:, kk * 128:(kk + 1) * 128], ident[:, :])
                        m.then_inc(p2["ht_done"], 1)

                def finish(u, b):
                    e = pe.value_load(ttab[0:1, 0, bass.ds(u * 2 + b, 1)], min_val=0, max_val=NX - 1)
                    for k in range(KH):
                        if k % (KH // 2) == 0:
                            hold(pe, p2["ht_copied"], u * 4 + (2 * b + k // (KH // 2) + 5))
                        m = pe.matmul(ps[4 + b][:, 0:C], HT[b][:, k, :],
                                      Wd[:, bass.ds(e, 1), k, :].rearrange("p a c -> p (a c)"),
                                      start=(k == 0), stop=(k == KH - 1))
                    m.then_inc(p2["y_done"], 1)
                pe.sem_inc(p2["ht_copied"], 4)
                by_pairs(pe, turn, finish)

            @block.vector
            def _(v):
                chain = Chain(v, v_chain)
                chain.restart()
                v.sem_inc(p2["row_used"], 2)
                v.wait_ge(p2["bnt_done"], 1)
                chain(v.tensor_copy(bnT[:, :, :, :].rearrange("p i e k -> p (i e k)"), ps[7][:, 0:160]))
                chain(v.tensor_scalar(degs[:, 0, :], hist[0:PT, 0:NT], 1.0, None, ALU.max))
                v.tensor_scalar(degs[:, 1, :], deg_in[:, :], 1.0, None, ALU.max).then_inc(p2["deg_ready"], 1)
                v.wait_ge(p2["sq_ready"], 1)
                v.reciprocal(rsq[:, :, :], sqs[:, :, :]).then_inc(p2["rs_ready"], 1)
                v.wait_ge(p2["rs_ready"], 1)
                chain(v.tensor_copy(deg_in[:, :], rsq[:, 1, :]))
                v.memset(one8[:, :], 1.0)
                v.memset(rsg[0][:, :], 0.0)
                chain(v.memset(rsg[1][:, :], 0.0))
                chain(v.tensor_scalar(nt8[0:PT, :], cnt[0:PT, :], 1.0 / 128, 0.5 - 1.0 / 512, ALU.mult, ALU.add))
                chain(v.tensor_scalar(nt8[0:PT, :], nt8[0:PT, :], MAGIC, None, ALU.add))
                chain(v.tensor_scalar(nt8[0:PT, :], nt8[0:PT, :], -MAGIC, None, ALU.add))
                chain(v.tensor_tensor_scan(ct8[0:PT, :], one8[0:PT, :], nt8[0:PT, :], 0.0, ALU.mult, ALU.add))
                chain(v.tensor_tensor(ge[0:PT, :, :], iota_c[0:PT, 0:TMAX].unsqueeze(2).broadcast_to([PT, TMAX, NX]),
                                      ct8[0:PT, :].unsqueeze(1).broadcast_to([PT, TMAX, NX]), ALU.is_ge))
                chain(v.tensor_tensor(gn[0:PT, :, :], ge[0:PT, :, :],
                                      nt8[0:PT, :].unsqueeze(1).broadcast_to([PT, TMAX, NX]), ALU.mult))
                chain(v.tensor_reduce(te[0:PT, :], ge[0:PT, :, :], AX, ALU.add))
                chain(v.tensor_reduce(ts_[0:PT, :], gn[0:PT, :, :], AX, ALU.add))
                chain(v.tensor_tensor(tr[0:PT, :], iota_c[0:PT, 0:TMAX], ts_[0:PT, :], ALU.subtract))
                chain(v.tensor_scalar(ts_[0:PT, :], te[0:PT, :], REG / 128.0, None, ALU.mult))
                chain(v.tensor_tensor(tr[0:PT, :], tr[0:PT, :], ts_[0:PT, :], ALU.add))
                chain(v.tensor_scalar(tr[0:PT, :], tr[0:PT, :], 128.0, float(NX * REG), ALU.mult, ALU.min))
                chain(v.tensor_scalar(te[0:PT, :], te[0:PT, :], float(NX - 1), None, ALU.min))
                chain(v.tensor_tensor(pf[0:PT, 0:NX], region8[0:PT, :], cnt[0:PT, :], ALU.add))
                chain(v.tensor_scalar(pf[0:PT, NX:NX + 1], ct8[0:PT, NX - 1:NX], 0.5, -0.75, ALU.mult, ALU.add))
                chain(v.tensor_scalar(pf[0:PT, NX:NX + 1], pf[0:PT, NX:NX + 1], MAGIC, None, ALU.add))
                chain(v.tensor_scalar(pf[0:PT, NX:NX + 1], pf[0:PT, NX:NX + 1], -MAGIC, None, ALU.add))
                chain(v.tensor_copy(ttab[0:1, 0, :], te[0:1, :]))
                chain(v.tensor_copy(ttab[0:1, 1, :], tr[0:1, :]))
                v.tensor_copy(ptab[0:1, :], pf[0:1, :]).then_inc(p2["tab_ready"], 1)
                chain(v.memset(pads[:, :], 0.0))
                v.memset(pads[:, HID + C + 1:HID + C + 2].bitcast(I32), NO_NODE).then_inc(p2["tab_ready"], 1)

                def turn(u, b):
                    hold(v, rin[b], u * 16 + 16)
                    hold(v, sent[b], u * 32 + 16)
                    v.tensor_copy(ids[b][:, :], rbuf[b][:, HID + C + 1:HID + C + 2].bitcast(I32))\
                        .then_inc(p2["ids_ready"], 1)
                    v.tensor_copy(x1p[b][:, :], rbuf[b][:, HID:HID + C + 1]).then_inc(p2["x1_kept"], 1)
                    hold(v, p2["x1_kept"], u * 2 + (b + 1))
                    hold(v, p2["ht_done"], u * 4 + (2 * b + 2))
                    v.sem_inc(p2["row_used"], 1)

                def finish(u, b):
                    chain.restart()
                    e = v.value_load(ttab[0:1, 0, bass.ds(u * 2 + b, 1)], min_val=0, max_val=NX - 1)
                    hold(v, p2["y_done"], u * 2 + (b + 3))
                    chain(v.tensor_tensor(x2[b][:, :], ps[4 + b][:, 0:C], one(bdrow, e), ALU.add))
                    chain(v.scalar_tensor_tensor(x2[b][:, :], x2[b][:, :], x1p[b][:, C:C + 1],
                                                 x1p[b][:, 0:C], ALU.mult, ALU.add))
                    chain(v.bn_stats(st[:, b, :], x2[b][:, :]))
                    v.bn_aggr(mv[:, b, :], st[:, b, :]).then_inc(p2["var_ready"], 1)
                    hold(v, p2["std_ready"], u * 2 + (b + 1))
                    chain(v.reciprocal(rstd[:, b:b + 1], std[:, b:b + 1]))
                    hold(v, p2["rs_got"], u * 32 + (16 * b + 16))
                    chain(v.tensor_tensor(rstd[:, b:b + 1], rstd[:, b:b + 1], rsg[b][:, :], ALU.mult))
                    chain(v.tensor_scalar(hx[b][:, :], x2[b][:, :], mv[:, b, 0:1], rstd[:, b:b + 1], ALU.subtract,
                                          ALU.mult))
                    chain(v.tensor_copy(hparts[b][:, 0, :], hx[b][:, :]))
                    chain(v.tensor_tensor(hx[b][:, :], hx[b][:, :], hparts[b][:, 0, :], ALU.subtract))
                    v.tensor_scalar(hparts[b][:, 1, :], hx[b][:, :], LOW, None, ALU.mult).then_inc(p2["h_ready"], 1)
                by_pairs(v, turn, finish)

        weights2.close()

        p3 = {n: sem("gcn_" + n) for n in (
            "weights", "win_src", "win_dst", "taken_src", "taken_dst", "idx_ready", "masks_ready", "seg_done",
            "ag_ready", "agT_done", "agT_copied", "hw_done", "ss_ready", "nrm_ready", "var_ready", "std_ready",
            "xn_ready", "xT_done", "xT_copied", "gate_done", "lmax_ready", "lexp_done", "w_ready", "wT_done",
            "wT_copied", "bo_done", "h1_done", "h1_act", "h2_done", "h2_act", "y_done", "y_taken", "x2_in", "out_ready",
            "written", "sq_in", "sq_out", "zero_done", "experts", "xF_copied", "bns_ready")}
        got3 = sem("gcn_got", NCH)
        with ExitStack() as c3, nc.Block() as block:
            s3 = allocator(c3)
            L1 = s3("L1", [128, NX, KC, C])
            L2 = s3("L2", [128, NX, KC, C])
            L3 = s3("L3", [128, NX, KC, C])
            W1g = s3("W1g", [128, KC, C])
            b1g = s3("b1g", [128, C])
            Wr = s3("Wr", [128, KC, NX])
            brrow = s3("brrow", [128, NX])
            bo = s3("bo", [NX, C])
            bns = s3("bns", [128, 4, NX, KC])
            bsq = s3("bsq", [128, 2, NX, KC])
            x2t = s3("x2t", [PT, C])
            ag = s3("ag", [PT, C])
            agT = s3("agT", [128, KC, PT])
            hh = s3("hh", [PT, C])
            hsq = s3("hsq", [PT, C])
            ss = s3("ss", [PT, 1])
            nrm = s3("nrm", [PT, 1])
            x3 = s3("x3", [PT, C])
            lg = s3("lg3", [PT, NX])
            lex = s3("lex3", [PT, NX])
            lmx = s3("lmx", [PT, 1])
            nmx = s3("nmx3", [PT, 1])
            se = s3("se3", [PT, 1])
            rse = s3("rse", [PT, 1])
            wgt = s3("wgt", [PT, NX])
            wT = s3("wT", [NX, PT])
            h1 = [s3(f"h1_{i}", [128, KC, PT]) for i in range(2)]
            h2 = [s3(f"h2_{i}", [128, KC, PT]) for i in range(2)]
            ot = s3("ot", [PT, C])
            xF = s3("xF", [128, KC, PT])
            wgtF = s3("wgtF", [PT, NX])
            base = s3("base", [PT, C])
            zeros_h = s3("zeros_h", [128, 2 * C], F16)
            iota_h = s3("iota_h", [128, PT], F16)
            dloc_h = s3("dloc_h", [128, SLOTS], F16)
            OH16 = s3("OH16", [128, SLOTS, PT], F16)
            acc, misc = ps[0], ps[1]
            agT_ps = misc[:, 0:KC * PT].rearrange("p (k n) -> p k n", k=KC)
            hw_ps = ps[2][0:PT, 0:C]
            gate_ps = ps[2][0:PT, C:C + NX]
            y_ps = ps[7][0:PT, 0:C]
            wT_ps = ps[2][0:NX, C + 16:C + 16 + PT]

            def pipeline(eng, tile, experts=None):
                tile(0, True, False, False)
                tile(1, True, True, False)
                if experts:
                    experts()
                with eng.Fori(2, NT) as k:
                    tile(k, True, True, True)
                tile(NT, False, True, True)
                tile(NT + 1, False, False, True)

            @block.sync
            def _(sp):
                sp.dma_start(W1g[:, :, :], g1_W.rearrange("(k p) n -> p k n", p=128)).then_inc(p3["weights"], 16)
                sp.dma_start(b1g[:, :], g1_b.partition_broadcast(128)).then_inc(p3["weights"], 16)
                sp.dma_start(Wr[:, :, :], f1_Wr.rearrange("(k p) n -> p k n", p=128)).then_inc(p3["weights"], 16)
                sp.dma_start(brrow[:, :], f1_br.partition_broadcast(128)).then_inc(p3["weights"], 16)
                sp.dma_start(bo[:, :], f1_bo).then_inc(p3["weights"], 16)
                load_windows(sp, p3["taken_src"], p3["taken_dst"], p3["win_src"], p3["win_dst"])

            @block.gpsimd
            def _(pool):
                pool.sem_inc(p3["taken_src"], 1)
                with pool.Fori(0, NT) as d:
                    first, last = window_passes(pool, d)
                    with pool.Fori(first, last) as q:
                        gather_pass(pool, q, table1, rows16, p3["win_src"], p3["taken_src"], p3["seg_done"],
                                    p3["idx_ready"], got3)

            @block.scalar
            def _(act):
                x2v = x2_rows.rearrange("(t p) c -> t p c", p=PT)
                ov = out.rearrange("(t p) c -> t p c", p=PT)
                for tile, w in ((L1, f1_W1), (L2, f1_W2), (L3, f1_Wo)):
                    for e in range(NX):
                        act.dma_start(tile[:, e, :, :], w[e].rearrange("(k p) n -> p k n", p=128)).then_inc(p3["experts"], 16)
                act.wait_ge(p3["sq_in"], 1)
                act.activation(bsq[:, :, :, :], bsq[:, :, :, :], ACT.Sqrt, bias=eps_bn[:, :]).then_inc(p3["sq_out"], 1)

                def hidden1(f, e):
                    act.wait_ge(p3["h1_done"], f * NX + (e + 1))
                    for k in range(KC):
                        m = act.activation(h1[e % 2][:, k, :], ps[3 + e % 2][:, k * PT:(k + 1) * PT], ACT.Relu,
                                           bias=bns[:, 1, e, k:k + 1], scale=bns[:, 0, e, k:k + 1])
                    m.then_inc(p3["h1_act"], 1)

                def hidden2(f, e):
                    act.wait_ge(p3["h2_done"], f * NX + (e + 1))
                    for k in range(KC):
                        m = act.activation(h2[e % 2][:, k, :], ps[5 + e % 2][:, k * PT:(k + 1) * PT], ACT.Relu,
                                           bias=bns[:, 3, e, k:k + 1], scale=bns[:, 2, e, k:k + 1])
                    m.then_inc(p3["h2_act"], 1)

                def store(f):
                    hold(act, p3["out_ready"], f + 1)
                    act.dma_start(ov[bass.ds(f, 1), :, :].rearrange("a p c -> (a p) c"), ot[:, :]).then_inc(p3["written"], 16)

                def tile(k, sums, layer, mix):
                    t, f = k - 1, k - 2
                    for i in range(NX + 1):
                        if mix and i < NX:
                            hidden1(f, i)
                        if layer and i == 0:
                            act.wait_ge(p3["agT_done"], t + 1)
                            act.activation(agT[:, :, :], agT_ps, ACT.Copy).then_inc(p3["agT_copied"], 1)
                        if layer and i == 2:
                            act.wait_ge(p3["ss_ready"], t + 1)
                            act.activation(nrm[:, :], ss[:, :], ACT.Sqrt).then_inc(p3["nrm_ready"], 1)
                        if mix and i >= 1:
                            hidden2(f, i - 1)
                        if layer and i == 2:
                            act.wait_ge(p3["var_ready"], t + 1)
                            act.activation(std[0:PT, 0:1], mv[0:PT, 0, 1:2], ACT.Sqrt, bias=eps_ln[0:PT, :])\
                                .then_inc(p3["std_ready"], 1)
                        if layer and i == 3:
                            act.wait_ge(p3["xT_done"], t + 1)
                            act.activation(xT[0][:, :, 0:PT], agT_ps, ACT.Copy).then_inc(p3["xT_copied"], 1)
                        if sums and i == 3:
                            act.dma_start(x2t[:, :], x2v[bass.ds(k, 1), :, :].rearrange("a p c -> (a p) c"))\
                                .then_inc(p3["x2_in"], 16)
                        if layer and i == 4:
                            act.wait_ge(p3["lmax_ready"], t + 1)
                            act.activation(lex[:, :], lg[:, :], ACT.Exp, bias=nmx[:, :], accum_out=se[:, :])\
                                .then_inc(p3["lexp_done"], 1)
                    if layer:
                        act.activation(xF[:, :, :], xT[0][:, :, 0:PT], ACT.Copy).then_inc(p3["xF_copied"], 1)
                    if mix:
                        store(f)
                pipeline(act, tile, lambda: act.wait_ge(p3["bns_ready"], 1))
                act.wait_ge(p3["written"], 16 * NT)

            @block.tensor
            def _(pe):
                def opened():
                    pe.matmul(acc[0:PT, :], zeros_h[:, 0:PT], zeros_h[:, :], start=True, stop=False,
                              skip_group_check=True)

                def sums_of(q, c):
                    j0, j1 = CHUNKS[c]
                    hold(pe, p3["masks_ready"], q * NCH + (c + 1))
                    hold(pe, got3[c], (q + 1) * (16 * (j1 - j0)))
                    for j in range(j0, j1):
                        m = pe.matmul(acc[0:PT, :], OH16[:, j, :], rows16(j), start=False, stop=False,
                                      skip_group_check=True)
                    m.then_inc(p3["seg_done"], 1)

                def product1(f, e):
                    if e == 0:
                        hold(pe, p3["xF_copied"], f + 1)
                    else:
                        hold(pe, p3["h1_act"], f * NX + e)
                    for k in range(KC):
                        for kk in range(KC):
                            m = pe.matmul(ps[3 + e % 2][:, k * PT:(k + 1) * PT],
                                          L1[:, e, kk, k * 128:(k + 1) * 128], xF[:, kk, :],
                                          start=(kk == 0), stop=(kk == KC - 1))
                    m.then_inc(p3["h1_done"], 1)

                def product2(f, e):
                    hold(pe, p3["h1_act"], f * NX + (e + 1))
                    if e >= 2:
                        hold(pe, p3["h2_act"], f * NX + (e - 1))
                    for k in range(KC):
                        for kk in range(KC):
                            m = pe.matmul(ps[5 + e % 2][:, k * PT:(k + 1) * PT],
                                          L2[:, e, kk, k * 128:(k + 1) * 128], h1[e % 2][:, kk, :],
                                          start=(kk == 0), stop=(kk == KC - 1))
                    m.then_inc(p3["h2_done"], 1)

                def product3(f, e):
                    hold(pe, p3["h2_act"], f * NX + (e + 1))
                    hold(pe, p3["y_taken"], f * NX + (e + 1))
                    for kk in range(KC):
                        m = pe.matmul(y_ps, h2[e % 2][:, kk, :], L3[:, e, kk, :], start=(kk == 0), stop=(kk == KC - 1))
                    m.then_inc(p3["y_done"], 1)

                def tile(k, sums, layer, mix):
                    t, f = k - 1, k - 2
                    if sums:
                        first, last = window_passes(pe, k)
                    for i in range(NX + 2):
                        if mix and i < NX:
                            product1(f, i)
                        if mix and 1 <= i <= NX:
                            product2(f, i - 1)
                        if mix and i >= 2:
                            product3(f, i - 2)
                        if layer and i == 0:
                            hold(pe, p3["ag_ready"], t + 1)
                            for kk in range(KC):
                                m = pe.transpose(misc[:, kk * PT:(kk + 1) * PT], ag[:, kk * 128:(kk + 1) * 128],
                                                 ident[0:PT, 0:PT])
                            m.then_inc(p3["agT_done"], 1)
                        if layer and i == 1:
                            hold(pe, p3["agT_copied"], t + 1)
                            for kk in range(KC):
                                m = pe.matmul(hw_ps, agT[:, kk, :], W1g[:, kk, :], start=(kk == 0), stop=(kk == KC - 1))
                            m.then_inc(p3["hw_done"], 1)
                        if layer and i == 3:
                            hold(pe, p3["xn_ready"], t + 1)
                            for kk in range(KC):
                                m = pe.transpose(misc[:, kk * PT:(kk + 1) * PT], xn[0][0:PT, kk * 128:(kk + 1) * 128],
                                                 ident[0:PT, 0:PT])
                            m.then_inc(p3["xT_done"], 1)
                        if layer and i == 4:
                            hold(pe, p3["xT_copied"], t + 1)
                            for kk in range(KC):
                                m = pe.matmul(gate_ps, xT[0][:, kk, 0:PT], Wr[:, kk, :], start=(kk == 0),
                                              stop=(kk == KC - 1))
                            m.then_inc(p3["gate_done"], 1)
                        if layer and i == 6:
                            hold(pe, p3["w_ready"], t + 1)
                            pe.transpose(wT_ps, wgt[:, :], ident[0:PT, 0:PT]).then_inc(p3["wT_done"], 1)
                        if layer and i == 7:
                            hold(pe, p3["wT_copied"], t + 1)
                            pe.matmul(hw_ps, wT[:, :], bo[:, :], start=True, stop=True).then_inc(p3["bo_done"], 1)
                        if sums and i == 4:
                            opened()
                        if sums and i in (4, 6, 8):
                            sums_of(first, i // 2 - 2)
                    if sums:
                        extra_passes(pe, first, last, lambda q: [sums_of(q, c) for c in range(NCH)])
                pe.wait_ge(p3["weights"], 16 * 5)
                pe.wait_ge(p3["zero_done"], 1)
                pipeline(pe, tile, lambda: pe.wait_ge(p3["experts"], 16 * 3 * NX))

            @block.vector
            def _(v):
                chain = Chain(v, v_chain)
                chain.restart()
                v.sem_inc(p3["taken_dst"], 1)
                v.sem_inc(p3["seg_done"], NCH)
                v.sem_inc(p3["y_taken"], 1)
                v.tensor_copy(iota_h[:, :], iota_c[:, 0:PT])
                chain(v.memset(zeros_h[:, :], 0.0))
                v.sem_inc(p3["zero_done"], 1)
                for i in range(2):
                    ins = v.tensor_copy(bsq[:, i, :, :], bnT[:, 5 * i + 4, :, :])
                    if i == 0:
                        chain(ins)
                ins.then_inc(p3["sq_in"], 1)
                v.wait_ge(p3["sq_out"], 1)
                chain(v.reciprocal(bsq[:, :, :, :], bsq[:, :, :, :]))
                for i in range(2):
                    chain(v.tensor_tensor(bns[:, 2 * i, :, :], bsq[:, i, :, :], bnT[:, 5 * i + 1, :, :], ALU.mult))
                    chain(v.tensor_tensor(bns[:, 2 * i + 1, :, :], bnT[:, 5 * i, :, :], bnT[:, 5 * i + 3, :, :],
                                          ALU.subtract))
                    chain(v.tensor_tensor(bns[:, 2 * i + 1, :, :], bns[:, 2 * i + 1, :, :], bns[:, 2 * i, :, :], ALU.mult))
                    chain(v.tensor_tensor(bns[:, 2 * i + 1, :, :], bns[:, 2 * i + 1, :, :], bnT[:, 5 * i + 2, :, :],
                                          ALU.add))
                v.sem_inc(p3["bns_ready"], 1)
                v.wait_ge(p3["weights"], 16 * 5)

                def masks(q, d):
                    hold(v, p3["win_dst"], q * 16 + 16)
                    chain(v.tensor_scalar(dloc_h[:, :], dst_win[:, :], tile_lo[:, bass.ds(d, 1)], None, ALU.subtract))
                    v.sem_inc(p3["taken_dst"], 1)
                    for c, (j0, j1) in enumerate(CHUNKS):
                        hold(v, p3["seg_done"], q * NCH + (c + 1))
                        v.tensor_tensor(OH16[:, j0:j1, :],
                                        iota_h[:, :].unsqueeze(1).broadcast_to([128, j1 - j0, PT]),
                                        dloc_h[:, j0:j1].unsqueeze(2).broadcast_to([128, j1 - j0, PT]),
                                        ALU.is_equal).then_inc(p3["masks_ready"], 1)

                def mixed(f, e):
                    hold(v, p3["y_done"], f * NX + (e + 1))
                    if e == 0:
                        if type(f) is not int or f:
                            hold(v, p3["written"], f * 16)
                        before_it = base
                    else:
                        before_it = ot
                    v.scalar_tensor_tensor(ot[:, :], y_ps, wgtF[:, e:e + 1], before_it[:, :], ALU.mult,
                                           ALU.add).then_inc(p3["y_taken"], 1)
                    hold(v, p3["y_taken"], f * NX + (e + 2))

                def tile(k, sums, layer, mix):
                    t, f = k - 1, k - 2
                    chain.restart()
                    if sums:
                        first, last = window_passes(v, k)
                    if mix:
                        chain(v.tensor_copy(wgtF[:, :], wgt[:, :]))
                    if sums:
                        masks(first, k)
                    if layer:
                        hold(v, p3["hw_done"], t + 1)
                        chain(v.tensor_tensor(hh[:, :], hw_ps, b1g[0:PT, :], ALU.add))
                        chain(v.tensor_scalar(hh[:, :], hh[:, :], 0.0, None, ALU.max))
                        v.tensor_tensor_reduce(hsq[:, :], hh[:, :], hh[:, :], 1.0, 0.0, ALU.mult, ALU.add, ss[:, :])\
                            .then_inc(p3["ss_ready"], 1)
                        hold(v, p3["nrm_ready"], t + 1)
                        chain(v.tensor_scalar(nrm[:, :], nrm[:, :], EPS_NORM, None, ALU.max))
                        chain(v.reciprocal(nrm[:, :], nrm[:, :]))
                        hold(v, p3["x2_in"], t * 16 + 16)
                        chain(v.scalar_tensor_tensor(x3[:, :], hh[:, :], nrm[:, :], x2t[:, :], ALU.mult, ALU.add))
                        chain(v.bn_stats(st[0:PT, 0, :], x3[:, :]))
                        v.bn_aggr(mv[0:PT, 0, :], st[0:PT, 0, :]).then_inc(p3["var_ready"], 1)
                    if mix:
                        mixed(f, 0)
                    if layer:
                        hold(v, p3["std_ready"], t + 1)
                        chain(v.reciprocal(rstd[0:PT, 0:1], std[0:PT, 0:1]))
                        v.tensor_scalar(xn[0][0:PT, :], x3[:, :], mv[0:PT, 0, 0:1], rstd[0:PT, 0:1], ALU.subtract,
                                        ALU.mult).then_inc(p3["xn_ready"], 1)
                    if mix:
                        mixed(f, 1)
                        mixed(f, 2)
                    if layer:
                        hold(v, p3["gate_done"], t + 1)
                        chain(v.tensor_tensor(lg[:, :], gate_ps, brrow[0:PT, :], ALU.add))
                        chain(v.tensor_reduce(lmx[:, :], lg[:, :], AX, ALU.max))
                        v.tensor_scalar(nmx[:, :], lmx[:, :], -1.0, None, ALU.mult).then_inc(p3["lmax_ready"], 1)
                    if mix:
                        mixed(f, 3)
                    if layer:
                        hold(v, p3["lexp_done"], t + 1)
                        chain(v.reciprocal(rse[:, :], se[:, :]))
                        v.tensor_scalar(wgt[:, :], lex[:, :], rse[:, :], None, ALU.mult).then_inc(p3["w_ready"], 1)
                    if mix:
                        mixed(f, 4)
                    if layer:
                        hold(v, p3["wT_done"], t + 1)
                        v.tensor_copy(wT[:, :], wT_ps).then_inc(p3["wT_copied"], 1)
                    if mix:
                        mixed(f, 5)
                        mixed(f, 6)
                    if layer:
                        hold(v, p3["bo_done"], t + 1)
                        chain(v.tensor_tensor(base[:, :], x3[:, :], hw_ps, ALU.add))
                    if mix:
                        mixed(f, 7)
                        v.sem_inc(p3["out_ready"], 1)
                    if sums:
                        extra_passes(v, first, last, lambda q: masks(q, k))
                        chain.restart()
                        hold(v, p3["seg_done"], last * NCH + NCH)
                        chain(v.tensor_copy(ag[:, :], acc[0:PT, 0:C]))
                        chain(v.scalar_tensor_tensor(ag[:, :], acc[0:PT, C:2 * C], 1.0 / LOW, ag[:, :], ALU.mult,
                                                     ALU.add))
                        v.tensor_scalar(ag[:, :], ag[:, :], deg_in[:, bass.ds(k, 1)], None, ALU.mult)\
                            .then_inc(p3["ag_ready"], 1)
                pipeline(v, tile)


_INS = ['x', 'src', 'dst', 'L0_gnn_W', 'L0_gnn_att_src', 'L0_gnn_att_dst', 'L0_gnn_bias', 'L0_ffn_W1', 'L0_ffn_b1',
        'L0_ffn_Wg', 'L0_ffn_bg', 'L0_ffn_Wd', 'L0_ffn_bd', 'L1_gnn_W', 'L1_gnn_b', 'L1_ffn_Wr', 'L1_ffn_br',
        'L1_ffn_W1', 'L1_ffn_b1', 'L1_ffn_g1', 'L1_ffn_be1', 'L1_ffn_m1', 'L1_ffn_v1', 'L1_ffn_W2', 'L1_ffn_b2',
        'L1_ffn_g2', 'L1_ffn_be2', 'L1_ffn_m2', 'L1_ffn_v2', 'L1_ffn_Wo', 'L1_ffn_bo']
_OUTS = [((3125, 256), 'float32')]


def kernel(**inputs):
    import numpy as _np
    import concourse.bacc as _bacc
    from concourse import mybir as _mybir
    from concourse.bass_utils import run_bass_kernel_spmd as _run

    nc = _bacc.Bacc("TRN2", target_bir_lowering=False, num_devices=1)
    arrays, args = {}, []
    for name in _INS:
        a = _np.ascontiguousarray(inputs[name])
        arrays[f"in_{name}_dram"] = a
        args.append(nc.dram_tensor(f"in_{name}_dram", a.shape, _mybir.dt.from_np(a.dtype), kind="ExternalInput").ap())
    for i, (shape, dtype) in enumerate(_OUTS):
        dt = _mybir.dt.from_np(_np.dtype(dtype))
        args.append(nc.dram_tensor(f"out_{i}_dram", shape, dt, kind="ExternalOutput").ap())
    two_block_gnn(nc, *args)
    r = _run(nc, [arrays], core_ids=[0])
    got = tuple(r.results[0][f"out_{i}_dram"] for i in range(len(_OUTS)))
    return got[0]
```

```python
from contextlib import ExitStack

import concourse.bass as bass
from concourse import mybir

F32 = mybir.dt.float32
BF16 = mybir.dt.bfloat16
F16 = mybir.dt.float16
I32 = mybir.dt.int32
ALU = mybir.AluOpType
ACT = mybir.ActivationFunctionType
AX = mybir.AxisListType.X
RMAX = bass.bass_isa.ReduceOp.max

PT = 125
SLOTS = 17
CHUNKS = ((0, 5), (5, 10), (10, 17))
NCH = len(CHUNKS)
WIN = SLOTS * 128
BIG = 65536.0
MAGIC = 12582912.0
EPS_LN = 1e-5
EPS_BN = 1e-3
EPS_NORM = 1e-12
SLOPE = 0.2
SPREAD = 60.0
FAR = -1.0e30
NO_NODE = 1 << 20
LOW = 4096.0


class Chain:

    def __init__(self, eng, sem):
        self.eng, self.sem, self.n = eng, sem, 0

    def __call__(self, ins):
        self.n += 1
        ins.then_inc(self.sem, 1)
        self.eng.wait_ge(self.sem, self.n)

    def restart(self):
        self.eng.sem_clear(self.sem)
        self.n = 0


def one(ap, i, pat="p a c -> p (a c)"):
    return ap[:, bass.ds(i, 1)].rearrange(pat)


def two_block_gnn(nc, x, src, dst, g0_W, g0_as, g0_ad, g0_b, f0_W1, f0_b1, f0_Wg, f0_bg, f0_Wd, f0_bd,
                  g1_W, g1_b, f1_Wr, f1_br, f1_W1, f1_b1, f1_g1, f1_be1, f1_m1, f1_v1,
                  f1_W2, f1_b2, f1_g2, f1_be2, f1_m2, f1_v2, f1_Wo, f1_bo, out):
    N, C = x.shape
    E = src.shape[0]
    NT = N // PT
    HID = f0_W1.shape[1]
    NX = f0_Wd.shape[0]
    HEADS, HC = g0_as.shape
    KC = C // 128
    KH = HID // 128
    EC = E // PT
    EPT = EC // NT
    WA = C + 2 * HEADS
    TW = C + HEADS
    GW = TW + 4
    ROW = HID + C + 4
    REG = 26 * 128
    TMAX = 34
    UN = 5
    assert N % PT == 0 and E % PT == 0 and EC % NT == 0 and REG >= N + 128 and NT % UN == 0

    with ExitStack() as ctx:
        def sem(name, n=None):
            if n is None:
                return ctx.enter_context(nc.semaphore(name))
            return [ctx.enter_context(nc.semaphore(f"{name}{i}")) for i in range(n)]

        def allocator(c):
            return lambda name, shape, dt=F32: c.enter_context(nc.sbuf_tensor(name, shape, dt))

        def dram(name, shape, dt=F32):
            return nc.dram_tensor(name, shape, dt, kind="Internal").ap()

        sb = allocator(ctx)
        src_pad = dram("src_pad", (E + WIN,), I32)
        dst_pad = dram("dst_pad", (E + WIN,), I32)
        table0 = dram("table0", (N, TW))
        table1 = dram("table1", (N, 2 * C), F16)
        x2_rows = dram("x2_rows", (N, C))
        rs_rows = dram("rs_rows", (N, 1))
        sorted_rows = dram("sorted_rows", (NX * REG + 128, ROW))

        ps = [ctx.enter_context(nc.psum_tensor(f"bank{i}", [128, 512], F32)) for i in range(8)]

        iota_c = sb("iota_c", [128, 128])
        iota_p = sb("iota_p", [128, 1])
        tile_lo = sb("tile_lo", [128, NT])
        ident = sb("ident", [128, 128])
        eps_ln = sb("eps_ln", [128, 1])
        eps_bn = sb("eps_bn", [128, 1])
        wtab = sb("wtab", [1, 2, NT + 1], I32)
        deg_in = sb("deg_in", [PT, NT])
        src_win = sb("src_win", [128, SLOTS], I32)
        idx = sb("idx", [128, SLOTS], I32)
        dst_win = sb("dst_win", [128, SLOTS], I32)
        dloc = sb("dloc", [128, SLOTS])
        OH = sb("OH", [128, SLOTS, PT])
        G = sb("G", [128, SLOTS, GW])
        st = sb("st", [128, 2, 6])
        mv = sb("mv", [128, 2, 2])
        std = sb("std", [128, 2])
        rstd = sb("rstd", [128, 2])
        xn = [sb(f"xn{i}", [128, C]) for i in range(2)]
        xT = [sb(f"xT{i}", [128, KC, 128]) for i in range(2)]
        cnt = sb("cnt", [128, NX])
        region8 = sb("region8", [128, NX])
        bn_rows = [sb("bn_rowsA", [128, 128]), sb("bn_rowsB", [32, 128])]

        bnT = sb("bnT", [128, 10, NX, KC])

        v_chain = sem("v_chain")
        p_chain = sem("p_chain")
        sink = sem("sink")

        def hold(eng, s, value):
            eng.wait_ge(s, value)
            eng.sem_inc(sink, 1)

        weights2 = ExitStack()
        s2w = allocator(weights2)
        Wd = s2w("Wd", [128, NX, KH, C])
        bdrow = s2w("bdrow", [128, NX, C])
        weights0 = ExitStack()
        sw = allocator(weights0)
        XH = sw("XH", [PT, NT, WA])
        node = sw("node", [PT, NT, 3, 2 * HEADS], BF16)
        e_self = sw("e_self", [PT, NT, HEADS])
        gall = sw("gall", [PT, 2, HEADS])
        far_apart = sw("far_apart", [1, 1], I32)
        tile_row = sw("tile_row", [128, NT])
        shi = sw("shi", [PT, EC])
        slo = sw("slo", [PT, EC])
        iota_b = sw("iota_b", [128, 128], BF16)
        before = sw("before", [128, 128], BF16)
        ones_b = sw("ones_b", [128, 128], BF16)
        zeros_b = sw("zeros_b", [128, 128], BF16)
        fW1 = sw("fW1", [128, KC, HID])
        fWg = sw("fWg", [128, KH, NX])
        bias0 = sw("bias0", [128, C])
        b1row = sw("b1row", [1, HID])
        ones_row = sw("ones_row", [1, PT])
        bgrow = sw("bgrow", [128, NX])

        s_const = sem("s_const")
        loaded0 = sem("loaded0")
        x_in = sem("x_in", NT // UN)
        edges_in = sem("edges_in")
        weights_in = sem("weights_in")
        padded = sem("padded")
        var_all = sem("var_all")
        std_all = sem("std_all")
        seen_ready = sem("seen_ready")
        found_ready = sem("found_ready")
        wm_ready = sem("wm_ready")
        wm_all = sem("wm_all")
        gm_ready = sem("gm_ready")
        gm_all = sem("gm_all")
        self_z = sem("self_z")
        self_e = sem("self_e")
        xn0 = sem("xn0")
        xT0_done = sem("xT0_done")
        xT0_copied = sem("xT0_copied")
        xh_done = sem("xh_done")
        xh_copied = sem("xh_copied")
        t0_written = sem("t0_written")

        def free_after(i, j):
            return i * UN + (j + 2 if j == 0 else j + 1)

        with ExitStack() as c0, nc.Block() as block:
            s0 = allocator(c0)
            X = s0("X", [PT, NT, C])
            W0 = s0("W0", [128, KC, WA])
            att = s0("att", [128, 2, C])
            wtmp = s0("wtmp", [128, C])
            iota_d = s0("iota_d", [128, NT])
            edge_no = s0("edge_no", [PT, EC])
            no_edge = s0("no_edge", [1, WIN], I32)
            stA = s0("stA", [PT, NT, 6])
            mvA = s0("mvA", [PT, NT, 2])
            stdA = s0("stdA", [PT, NT])
            rstdA = s0("rstdA", [PT, NT])
            srci = s0("srci", [PT, EC], I32)
            dsti = s0("dsti", [PT, EC], I32)
            tmpe = s0("tmpe", [PT, EC])
            dhi = s0("dhi", [PT, EC])
            ends_at = s0("ends_at", [PT, 2, EC])
            seen0 = s0("seen0", [PT, 2, EC])
            wmm = s0("wmm", [PT, 2, NT])
            wall = s0("wall", [PT, 2, NT])
            wa = s0("wa", [PT, NT])
            wb = s0("wb", [PT, NT])
            wc = s0("wc", [PT, NT + 1])
            ones_t = s0("ones_t", [PT, NT])
            gmax = s0("gmax", [PT, 2, HEADS])
            spread = s0("spread", [PT, HEADS + 1])

            @block.gpsimd
            def _(pool):
                def iota(ap, pattern, cm):
                    pool.iota(ap, pattern, base=0, channel_multiplier=cm,
                              allow_small_or_imprecise_dtypes=True).then_inc(s_const, 1)
                iota(iota_c[:, :], [[1, 128]], 0)
                iota(iota_p[:, :], [[1, 1]], 1)
                iota(iota_d[:, :], [[1, NT]], 0)
                iota(tile_lo[:, :], [[PT, NT]], 0)
                iota(tile_row[:, :], [[PT, NT]], 1)
                iota(region8[:, :], [[REG, NX]], 0)
                iota(edge_no[:, :], [[1, EC]], EC)
                pool.memset(no_edge[:, :], -1).then_inc(s_const, 1)
                pool.wait_ge(wm_ready, 1)
                nc.gpsimd.partition_all_reduce(wall[:, :, :].rearrange("p a t -> p (a t)"),
                                               wmm[:, :, :].rearrange("p a t -> p (a t)"), PT, RMAX).then_inc(wm_all, 1)
                pool.wait_ge(gm_ready, 1)
                nc.gpsimd.partition_all_reduce(gall[:, :, :].rearrange("p a h -> p (a h)"),
                                               gmax[:, :, :].rearrange("p a h -> p (a h)"), PT, RMAX).then_inc(gm_all, 1)

            @block.sync
            def _(sp):
                sp.dma_start(dsti[:, :], dst.rearrange("(p j) -> p j", p=PT)).then_inc(edges_in, 16)
                sp.dma_start(srci[:, :], src.rearrange("(p j) -> p j", p=PT)).then_inc(edges_in, 16)
                for i in range(NT // UN):
                    sp.dma_start(X[:, i * UN:(i + 1) * UN, :],
                                 x[i * UN * PT:(i + 1) * UN * PT, :].rearrange("(t p) c -> p t c", p=PT))\
                        .then_inc(x_in[i], 16)
                sp.dma_start(src_pad[0:E], src).then_inc(padded, 16)
                sp.dma_start(dst_pad[0:E], dst).then_inc(padded, 16)
                sp.dma_start(src_pad[E:E + WIN], src[0:WIN]).then_inc(padded, 16)
                sp.dma_start(fW1[:, :, :], f0_W1.rearrange("(k p) n -> p k n", p=128)).then_inc(weights_in, 16)
                sp.dma_start(fWg[:, :, :], f0_Wg.rearrange("(k p) n -> p k n", p=128)).then_inc(weights_in, 16)
                for tile, vec in ((bias0[:, :], g0_b), (bgrow[:, :], f0_bg)):
                    sp.dma_start(tile, vec.partition_broadcast(128)).then_inc(weights_in, 16)
                sp.dma_start(b1row[:, :], f0_b1.rearrange("(a n) -> a n", a=1)).then_inc(weights_in, 16)
                for i, vec in enumerate((f1_b1, f1_g1, f1_be1, f1_m1, f1_v1, f1_b2, f1_g2, f1_be2, f1_m2, f1_v2)):
                    at = i * NX * KC
                    sp.dma_start(bn_rows[at // 128][at % 128:at % 128 + NX * KC, :],
                                 vec.rearrange("e (k p) -> (e k) p", p=128)).then_inc(weights_in, 16)
                sp.wait_ge(s_const, 8)
                sp.dma_start(dst_pad[E:E + WIN].rearrange("(a n) -> a n", a=1), no_edge[:, :]).then_inc(padded, 16)
                table0_tiles = table0.rearrange("(t p) n -> t p n", p=PT)
                with sp.Fori(0, NT) as t:
                    sp.wait_ge(xh_copied, t + 3)
                    sp.dma_start(table0_tiles[bass.ds(t, 1), :, :].rearrange("a p n -> (a p) n"),
                                 XH[:, bass.ds(t, 1), 0:TW].rearrange("p a n -> p (a n)")).then_inc(t0_written, 16)
                sp.wait_ge(t0_written, 16 * NT)
                sp.wait_ge(padded, 64)
                sp.wait_ge(weights_in, 16 * 15)

            @block.scalar
            def _(act):
                act.dma_start(W0[:, :, 0:C], g0_W.rearrange("(k p) n -> p k n", p=128)).then_inc(loaded0, 16)
                for i, vec in enumerate((g0_as, g0_ad)):
                    act.dma_start(att[:, i, :], vec.rearrange("h c -> (h c)").partition_broadcast(128))\
                        .then_inc(loaded0, 16)
                act.wait_ge(var_all, 1)
                act.activation(stdA[:, :], mvA[:, :, 1], ACT.Sqrt, bias=eps_ln[0:PT, :]).then_inc(std_all, 1)
                with act.Fori(0, NT // UN) as i:
                    for jj in range(UN + 1):
                        if jj < UN:
                            act.wait_ge(xT0_done, i * UN + (jj + 3))
                            hold(act, xh_done, free_after(i, jj))
                            act.activation(xT[jj % 2][:, :, 0:PT],
                                           ps[jj % 2][:, 0:KC * PT].rearrange("p (k n) -> p k n", k=KC),
                                           ACT.Copy).then_inc(xT0_copied, 1)
                        if jj >= 1:
                            j = jj - 1
                            hold(act, xh_done, i * UN + (j + 3))
                            act.activation(one(XH, i * UN + j), ps[2 + j % 2][0:PT, 0:WA],
                                           ACT.Copy).then_inc(xh_copied, 1)

            @block.tensor
            def _(pe):
                pe.sem_inc(xT0_done, 2)
                pe.sem_inc(xh_done, 2)
                with pe.Fori(0, NT // UN) as i:
                    for jj in range(UN + 1):
                        if jj < UN:
                            hold(pe, xn0, i * UN + (jj + 1))
                            for k in range(KC):
                                m = pe.transpose(ps[jj % 2][:, k * PT:(k + 1) * PT],
                                                 xn[jj % 2][0:PT, k * 128:(k + 1) * 128], ident[0:PT, 0:PT])
                            m.then_inc(xT0_done, 1)
                        if jj == 0:
                            continue
                        j = jj - 1
                        hold(pe, xT0_copied, i * UN + (j + 1))
                        hold(pe, xh_copied, free_after(i, j))
                        for k in range(KC):
                            m = pe.matmul(ps[2 + j % 2][0:PT, 0:WA], xT[j % 2][:, k, 0:PT], W0[:, k, :],
                                          start=(k == 0), stop=(k == KC - 1))
                        m.then_inc(xh_done, 1)

            @block.vector
            def _(v):
                chain = Chain(v, v_chain)
                v.sem_inc(xh_copied, 2)
                v.memset(eps_ln[:, :], EPS_LN)
                v.memset(eps_bn[:, :], EPS_BN)
                v.memset(ones_b[:, :], 1.0)
                v.memset(zeros_b[:, :], 0.0)
                v.memset(ones_t[:, :], 1.0)
                v.memset(ones_row[:, :], 1.0)
                v.memset(G[:, :, TW:GW], 1.0)
                chain(v.memset(cnt[:, :], 0.0))
                v.wait_ge(s_const, 8)
                v.tensor_scalar(ident[:, :], iota_c[:, :], iota_p[:, :], None, ALU.is_equal)
                v.tensor_copy(iota_b[:, :], iota_c[:, :])
                chain(v.tensor_scalar(before[:, :], iota_c[:, :], iota_p[:, :], None, ALU.is_gt))
                v.wait_ge(edges_in, 32)
                for ends, hi in ((dsti, dhi), (srci, shi)):
                    chain(v.tensor_scalar(tmpe[:, :], ends[:, :], 1.0 / PT, -0.5 + 0.5 / PT, ALU.mult, ALU.add))
                    chain(v.tensor_scalar(tmpe[:, :], tmpe[:, :], MAGIC, None, ALU.add))
                    chain(v.tensor_scalar(hi[:, :], tmpe[:, :], -MAGIC, None, ALU.add))
                chain(v.tensor_scalar(tmpe[:, :], shi[:, :], -float(PT), None, ALU.mult))
                chain(v.tensor_tensor(slo[:, :], tmpe[:, :], srci[:, :], ALU.add))
                chain(v.tensor_scalar(ends_at[:, 0, :], edge_no[:, :], -1.0, float(E), ALU.mult, ALU.add))
                chain(v.tensor_scalar(ends_at[:, 1, :], edge_no[:, :], 1.0, None, ALU.add))
                v.wait_ge(loaded0, 48)
                for a in range(2):
                    for k in range(KC):
                        chain(v.tensor_tensor(wtmp[:, :], W0[:, k, 0:C], att[:, a, :], ALU.mult))
                        chain(v.tensor_reduce(W0[:, k, C + a * HEADS:C + (a + 1) * HEADS],
                                              wtmp[:, :].rearrange("p (h c) -> p h c", h=HEADS), AX, ALU.add))
                for i in range(NT // UN):
                    v.wait_ge(x_in[i], 16)
                    for t in range(i * UN, (i + 1) * UN):
                        ins = v.bn_stats(stA[:, t, :], X[:, t, :])
                    chain(ins)
                for t in range(NT):
                    ins = v.bn_aggr(mvA[:, t, :], stA[:, t, :])
                ins.then_inc(var_all, 1)
                v.wait_ge(std_all, 1)
                chain(v.reciprocal(rstdA[:, :], stdA[:, :]))
                with v.Fori(0, NT // UN) as i:
                    for jj in range(UN):
                        t = i * UN + jj
                        hold(v, xT0_done, free_after(i, jj))
                        v.tensor_scalar(xn[jj % 2][0:PT, :], one(X, t), one(mvA[:, :, 0:1], t),
                                        rstdA[:, bass.ds(t, 1)], ALU.subtract, ALU.mult).then_inc(xn0, 1)
                        for side in range(2):
                            m = v.scalar_tensor_tensor(seen0[:, side, :], dhi[:, :], iota_d[0:PT, bass.ds(t, 1)],
                                                       ends_at[:, side, :], ALU.is_equal, ALU.mult)
                        m.then_inc(seen_ready, 1)
                        hold(v, seen_ready, t + 1)
                        v.tensor_reduce(wmm[:, :, bass.ds(t, 1)].rearrange("p s a -> p (s a)"), seen0[:, :, :],
                                        AX, ALU.max).then_inc(found_ready, 1)
                        hold(v, found_ready, t + 1)
                chain.restart()
                v.wait_ge(xh_copied, NT + 2)
                a_src = XH[:, :, C:TW].rearrange("p t h -> p h t")
                chain(v.tensor_reduce(gmax[:, 0, :], a_src, AX, ALU.max))
                chain(v.tensor_reduce(gmax[:, 1, :], a_src, AX, ALU.min))
                v.tensor_scalar(gmax[:, 1, :], gmax[:, 1, :], -1.0, None, ALU.mult).then_inc(gm_ready, 1)
                v.sem_inc(wm_ready, 1)
                v.wait_ge(gm_all, 1)
                chain(v.tensor_tensor(spread[:, 0:HEADS], gall[:, 0, :], gall[:, 1, :], ALU.add))
                chain(v.tensor_reduce(spread[:, HEADS:HEADS + 1], spread[:, 0:HEADS], AX, ALU.max))
                chain(v.tensor_scalar(spread[:, HEADS:HEADS + 1], spread[:, HEADS:HEADS + 1], SPREAD, None, ALU.is_gt))
                chain(v.tensor_copy(far_apart[:, :], spread[0:1, HEADS:HEADS + 1]))
                v.wait_ge(wm_all, 1)
                chain(v.tensor_scalar(wa[:, :], wall[:, 0, :], -1.0, float(E), ALU.mult, ALU.add))
                chain(v.tensor_scalar(wa[:, :], wa[:, :], float(E - 1), None, ALU.min))
                chain(v.tensor_tensor(wb[:, :], wall[:, 1, :], wa[:, :], ALU.subtract))
                chain(v.tensor_scalar(wb[:, :], wb[:, :], 1.0, None, ALU.max))
                chain(v.tensor_scalar(wb[:, :], wb[:, :], 1.0 / WIN, 0.5 - 0.5 / WIN, ALU.mult, ALU.add))
                chain(v.tensor_scalar(wb[:, :], wb[:, :], MAGIC, None, ALU.add))
                chain(v.tensor_scalar(wb[:, :], wb[:, :], -MAGIC, None, ALU.add))
                chain(v.memset(wc[:, 0:1], 0.0))
                chain(v.tensor_tensor_scan(wc[:, 1:NT + 1], ones_t[:, :], wb[:, :], 0.0, ALU.mult, ALU.add))
                chain(v.tensor_copy(wtab[0:1, 0, 0:NT], wa[0:1, :]))
                chain(v.tensor_copy(wtab[0:1, 1, :], wc[0:1, :]))

        def extra_passes(eng, first, last, body, then=None):
            with eng.If(first + 1 < last):
                with eng.Fori(first + 1, last) as q:
                    body(q)
                if then:
                    then()

        def if_one_pass(eng, first, last, body):
            with eng.If(last < first + 2):
                body()

        def window_passes(eng, d):
            first = eng.value_load(wtab[0:1, 1, bass.ds(d, 1)], min_val=0, max_val=NT * 23)
            last = eng.value_load(wtab[0:1, 1, bass.ds(d + 1, 1)], min_val=1, max_val=NT * 23)
            return first, last

        def load_windows(sp, taken_src, taken_dst, win_src, win_dst, row=None, tiles=(0, NT), also=None):
            with sp.Fori(*tiles) as d:
                first, last = window_passes(sp, d)
                start = sp.value_load(wtab[0:1, 0, bass.ds(d, 1)], min_val=0, max_val=E - 1)
                with sp.Fori(first, last) as q:
                    at = nc.s_assert_within((q - first) * WIN + start, 0, E,
                                            skip_runtime_bounds_check_because="a pass starts inside its window")
                    sp.wait_ge(taken_src, q + 1)
                    sp.dma_start(src_win[:, :], src_pad[bass.ds(at, WIN)].rearrange("(p j) -> p j", p=128))\
                        .then_inc(win_src, 16)
                    sp.wait_ge(taken_dst, q + 1)
                    sp.dma_start(dst_win[:, :], dst_pad[bass.ds(at, WIN)].rearrange("(p j) -> p j", p=128))\
                        .then_inc(win_dst, 16)
                    if row is not None:
                        dst_row, win_row = row
                        sp.dma_start(dst_row[:, :], dst_pad[bass.ds(at, WIN)].partition_broadcast(PT))\
                            .then_inc(win_row, 16)
                if also:
                    also(d)

        def rows16(j):
            return G[:, j, 0:C].bitcast(F16)

        def gather_pass(pool, q, table, rows, win_src, taken_src, seg_done, idx_ready, got, between=None):
            hold(pool, win_src, q * 16 + 16)
            for c, (j0, j1) in enumerate(CHUNKS):
                if between and c == NCH - 1:
                    between()
                hold(pool, seg_done, q * NCH + (c + 1))
                pool.tensor_copy(idx[:, j0:j1], src_win[:, j0:j1]).then_inc(idx_ready, 1)
                hold(pool, idx_ready, q * NCH + (c + 1))
                if c == NCH - 1:
                    pool.sem_inc(taken_src, 1)
                for j in range(j0, j1):
                    pool.indirect_dma_start(rows(j), None, table,
                                            bass.IndirectOffsetOnAxis(idx[:, j:j + 1], 0)).then_inc(got[c], 16)

        def stagger(eng, tile):
            tile(0, True, False, True)
            with eng.Fori(1, NT - 1) as d:
                tile(d, True, True, True)
            tile(NT - 1, True, True, False)
            tile(NT, False, True, False)

        pm = {n: sem("max_" + n) for n in ("win_src", "win_dst", "win_row", "taken_src", "taken_dst", "idx_ready",
                                           "got", "diag_ready", "spread_done", "rows_used")}
        with ExitStack() as cm, nc.Block() as block:
            sm = allocator(cm)
            dst_row = sm("dst_row_m", [PT, WIN], I32)
            away = sm("away", [PT, WIN])
            diag = sm("diag", [128, HEADS, 128])
            ones_f = sm("ones_f", [128, PT])
            seen = sm("seen", [PT, HEADS, 128])
            found = sm("found", [PT, HEADS])
            high = sm("high", [PT, HEADS])
            m_src = sm("m_src", [PT, NT, HEADS])
            sh = sm("sh", [PT, NT, HEADS])
            shift = sm("shift", [PT, NT, HEADS])
            rest = sm("rest", [PT, NT, 2 * HEADS])

            def if_far_apart(eng):
                return eng.If(eng.value_load(far_apart[0:1, 0:1], min_val=0, max_val=1) > 0)

            def all_passes(eng, body):
                with eng.Fori(0, NT) as d:
                    first, last = window_passes(eng, d)
                    with eng.Fori(first, last) as q:
                        body(d, q)

            @block.sync
            def _(sp):
                with if_far_apart(sp):
                    load_windows(sp, pm["taken_src"], pm["taken_dst"], pm["win_src"], pm["win_dst"],
                                 (dst_row, pm["win_row"]))

            @block.gpsimd
            def _(pool):
                def gathers(d, q):
                    hold(pool, pm["win_src"], q * 16 + 16)
                    hold(pool, pm["rows_used"], q + 1)
                    pool.tensor_copy(idx[:, :], src_win[:, :]).then_inc(pm["idx_ready"], 1)
                    hold(pool, pm["idx_ready"], q + 1)
                    pool.sem_inc(pm["taken_src"], 1)
                    for j in range(SLOTS):
                        pool.indirect_dma_start(G[:, j, 0:TW], None, table0,
                                                bass.IndirectOffsetOnAxis(idx[:, j:j + 1], 0)).then_inc(pm["got"], 16)
                with if_far_apart(pool):
                    pool.sem_inc(pm["taken_src"], 1)
                    all_passes(pool, gathers)

            @block.tensor
            def _(pe):
                def to_all_nodes(d, q):
                    for j in range(SLOTS):
                        hold(pe, pm["diag_ready"], q * SLOTS + (j + 1))
                        pe.matmul(ps[0][0:PT, :], ones_f[:, :], diag[:, :, :].rearrange("p h e -> p (h e)"),
                                  start=True, stop=True).then_inc(pm["spread_done"], 1)
                with if_far_apart(pe):
                    all_passes(pe, to_all_nodes)

            @block.scalar
            def _(act):
                act.wait_ge(self_z, 1)
                act.activation(e_self[:, :, :], sh[:, :, :], ACT.Exp).then_inc(self_e, 1)

            @block.vector
            def _(v):
                chain = Chain(v, v_chain)
                chain.restart()
                chain(v.tensor_copy(m_src[:, :, :], gall[:, 0, :].unsqueeze(1).broadcast_to([PT, NT, HEADS])))

                def maxima(d, q):
                    chain.restart()
                    hold(v, pm["win_row"], q * 16 + 16)
                    chain(v.tensor_scalar(away[:, :], dst_row[:, :], tile_row[0:PT, bass.ds(d, 1)], FAR,
                                          ALU.not_equal, ALU.mult))
                    hold(v, pm["win_dst"], q * 16 + 16)
                    v.sem_inc(pm["taken_dst"], 1)
                    hold(v, pm["got"], q * (16 * SLOTS) + 16 * SLOTS)
                    for j in range(SLOTS):
                        v.tensor_tensor(diag[:, :, :], ident[:, :].unsqueeze(1).broadcast_to([128, HEADS, 128]),
                                        G[:, j, C:TW].unsqueeze(2).broadcast_to([128, HEADS, 128]),
                                        ALU.mult).then_inc(pm["diag_ready"], 1)
                        hold(v, pm["spread_done"], q * SLOTS + (j + 1))
                        chain(v.tensor_tensor(seen[:, :, :], ps[0][0:PT, :].rearrange("p (h e) -> p h e", h=HEADS),
                                              away[:, :].rearrange("p (e j) -> p j e", j=SLOTS)[:, j, :]
                                              .unsqueeze(1).broadcast_to([PT, HEADS, 128]), ALU.add))
                        chain(v.tensor_reduce(found[:, :], seen[:, :, :], AX, ALU.max))
                        chain(v.tensor_tensor(high[:, :], high[:, :], found[:, :], ALU.max))
                    v.sem_inc(pm["rows_used"], 1)

                with if_far_apart(v):
                    v.sem_inc(pm["taken_dst"], 1)
                    v.sem_inc(pm["rows_used"], 1)
                    chain(v.memset(ones_f[:, :], 1.0))
                    with v.Fori(0, NT) as d:
                        chain.restart()
                        chain(v.tensor_copy(high[:, :], one(XH[:, :, C:TW], d)))
                        first, last = window_passes(v, d)
                        with v.Fori(first, last) as q:
                            maxima(d, q)
                        chain.restart()
                        chain(v.tensor_copy(one(m_src, d), high[:, :]))
                chain.restart()
                chain(v.tensor_copy(rest[:, :, 0:HEADS], XH[:, :, TW:WA]))
                chain(v.tensor_tensor(sh[:, :, :], XH[:, :, TW:WA], m_src[:, :, :], ALU.add))
                chain(v.scalar_tensor_tensor(shift[:, :, :], sh[:, :, :], SLOPE, sh[:, :, :], ALU.mult, ALU.max))
                chain(v.tensor_copy(rest[:, :, HEADS:2 * HEADS], shift[:, :, :]))
                for part in range(3):
                    chain(v.tensor_copy(node[:, :, part, :], rest[:, :, :]))
                    if part < 2:
                        chain(v.tensor_tensor(rest[:, :, :], rest[:, :, :], node[:, :, part, :], ALU.subtract))
                chain(v.tensor_tensor(e_self[:, :, :], XH[:, :, C:TW], XH[:, :, TW:WA], ALU.add))
                chain(v.scalar_tensor_tensor(e_self[:, :, :], e_self[:, :, :], SLOPE, e_self[:, :, :],
                                             ALU.mult, ALU.max))
                v.tensor_tensor(sh[:, :, :], e_self[:, :, :], shift[:, :, :], ALU.subtract).then_inc(self_z, 1)
                v.wait_ge(self_e, 1)

        p1 = {n: sem("gat_" + n) for n in (
            "win_src", "win_dst", "win_row", "taken_src", "taken_dst", "idx_ready", "masks_ready", "adm_ready",
            "z_ready", "w_ready", "msgs_ready", "seg_done", "var_ready", "std_ready", "xn_ready",
            "xT_done", "xT_copied", "h_done", "gelu_done", "ht_done", "ht_copied", "gate_done",
            "lmax_ready", "lexp_done", "sel_ready", "rank_done", "ranks_in", "row_ready",
            "scattered", "x_in", "own_ready", "hist_ready", "hist_done",
            "pad_ready", "acc_read")}
        weights2_in = sem("weights2_in")
        got1 = sem("gat_got", NCH)
        with ExitStack() as c1, nc.Block() as block:
            s1 = allocator(c1)
            dst_row = s1("dst_row", [PT, WIN], I32)
            OHT = s1("OHT", [PT, WIN], BF16)
            ads = s1("ads", [128, SLOTS, 2 * HEADS])
            lg4 = s1("lg4", [128, SLOTS, HEADS])
            row = s1("row", [128, ROW])
            HT = s1("HT", [128, KH, PT])
            r4 = s1("r4", [PT, HEADS])
            lg = s1("lg", [PT, NX])
            lex = s1("lex", [PT, NX])
            nmx = s1("nmx", [PT, 1])
            se = s1("se", [PT, 1])
            cand = s1("cand", [PT, NX])
            amin = s1("amin", [PT, 1])
            sel = s1("sel", [PT, NX])
            selb = s1("selb", [PT, NX], BF16)
            pos = s1("pos", [PT, NX])
            pos1 = s1("pos1", [PT, 1])
            lmax = s1("lmax", [PT, 1])
            ranks = s1("ranks", [PT, 2 * NX])
            posi = s1("posi", [PT, 1], I32)
            xt = s1("xt", [PT, C])
            x1 = s1("x1", [PT, C])
            ohi = s1("ohi", [PT, EPT, NT], BF16)
            olo = s1("olo", [PT, EPT, PT], BF16)
            acc, hist, misc = ps[0], ps[2], ps[3]
            adm = ps[1]
            PW = 3 * 2 * HEADS
            gate_ps = misc[0:PT, 256:256 + NX]
            rank_ps = misc[0:PT, 272:272 + NX]
            all_ps = misc[0:PT, 272 + NX:272 + 2 * NX]

            @block.sync
            def _(sp):
                def load_expert(e):
                    sp.dma_start(Wd[:, bass.ds(e, 1), :, :].rearrange("p a k n -> p (a k) n"),
                                 f0_Wd[bass.ds(e, 1), :, :].rearrange("a (k p) n -> p (a k) n", p=128))\
                        .then_inc(weights2_in, 16)
                for tiles, also in (((0, NX), load_expert), ((NX, NT), None)):
                    load_windows(sp, p1["taken_src"], p1["taken_dst"], p1["win_src"], p1["win_dst"],
                                 (dst_row, p1["win_row"]), tiles, also)
                    if also:
                        sp.dma_start(bdrow[:, :, :].rearrange("p e c -> p (e c)"),
                                     f0_bd.rearrange("e c -> (e c)").partition_broadcast(128))\
                            .then_inc(weights2_in, 16)
                sp.wait_ge(weights2_in, 16 * (NX + 1))
                sp.wait_ge(p1["scattered"], 16 * (NT + 1))

            @block.gpsimd
            def _(pool):
                pool.sem_inc(p1["taken_src"], 1)
                pool.wait_ge(p1["pad_ready"], 1)
                pool.dma_start(sorted_rows[NX * REG:NX * REG + 128, :], row[:, :]).then_inc(p1["scattered"], 16)

                chain = Chain(pool, p_chain)

                def fold(result, values, op):
                    n = NX // 2
                    while n > 1:
                        chain(pool.tensor_tensor(values[:, 0:n], values[:, 0:n], values[:, n:2 * n], op))
                        n //= 2
                    chain(pool.tensor_tensor(result[:, :], values[:, 0:1], values[:, 1:2], op))

                def scatter(d):
                    chain.restart()
                    hold(pool, p1["ranks_in"], d + 1)
                    chain(pool.tensor_tensor(pos[:, :], ranks[:, 0:NX], cnt[0:PT, :], ALU.add))
                    chain(pool.tensor_tensor(pos[:, :], pos[:, :], region8[0:PT, :], ALU.add))
                    chain(pool.tensor_tensor(pos[:, :], pos[:, :], sel[:, :], ALU.mult))
                    fold(pos1, pos, ALU.add)
                    chain(pool.tensor_tensor(cnt[0:PT, :], cnt[0:PT, :], ranks[:, NX:2 * NX], ALU.add))
                    chain(pool.tensor_copy(posi[:, :], pos1[:, :]))
                    hold(pool, p1["gelu_done"], d * 2 + 2)
                    hold(pool, p1["row_ready"], d + 1)
                    pool.indirect_dma_start(sorted_rows, bass.IndirectOffsetOnAxis(posi[:, :], 0),
                                            row[0:PT, :], None).then_inc(p1["scattered"], 16)

                def one_pass(q, between=None):
                    gather_pass(pool, q, table0, lambda j: G[:, j, 0:TW], p1["win_src"], p1["taken_src"],
                                p1["seg_done"], p1["idx_ready"], got1, between)

                def gathers(d, scatters):
                    first, last = window_passes(pool, d)

                    def between():
                        before_it = pool.value_load(wtab[0:1, 1, bass.ds(d - 1, 1)], min_val=0, max_val=NT * 23)
                        if_one_pass(pool, before_it, first, lambda: scatter(d - 2))
                    one_pass(first, between if scatters > 1 else None)
                    with pool.If(first + 1 < last):
                        if scatters:
                            scatter(d - 1)
                        with pool.Fori(first + 1, last) as q:
                            one_pass(q)
                    return first, last
                gathers(0, 0)
                gathers(1, 1)
                with pool.Fori(2, NT) as d:
                    gathers(d, 2)
                first, last = window_passes(pool, NT - 1)
                if_one_pass(pool, first, last, lambda: scatter(NT - 2))
                scatter(NT - 1)

            @block.scalar
            def _(act):
                xv = x.rearrange("(t p) c -> t p c", p=PT)

                def weights(q, c):
                    j0, j1 = CHUNKS[c]
                    act.wait_ge(p1["z_ready"], q * NCH + (c + 1))
                    act.activation(G[:, j0:j1, C:TW], lg4[:, j0:j1, :], ACT.Exp).then_inc(p1["w_ready"], 1)

                def tile(d, sums, finish, ahead):
                    p = d - 1
                    if sums:
                        first, last = window_passes(act, d)
                    if finish:
                        act.wait_ge(p1["var_ready"], p + 1)
                        act.activation(std[0:PT, 0:1], mv[0:PT, 0, 1:2], ACT.Sqrt, bias=eps_ln[0:PT, :])\
                            .then_inc(p1["std_ready"], 1)
                    if sums:
                        act.dma_start(xt[:, :], xv[bass.ds(d, 1), :, :].rearrange("a p c -> (a p) c"))\
                            .then_inc(p1["x_in"], 16)
                    if finish:
                        act.wait_ge(p1["xT_done"], p + 1)
                        act.activation(xT[0][:, :, 0:PT], misc[:, 0:KC * PT].rearrange("p (k n) -> p k n", k=KC),
                                       ACT.Copy).then_inc(p1["xT_copied"], 1)
                    if sums:
                        weights(first, 1)
                    if finish:
                        hold(act, p1["scattered"], p * 16 + 16)
                        act.activation(row[0:PT, HID:HID + C], x1[:, :], ACT.Copy)
                        for half in range(2):
                            act.wait_ge(p1["h_done"], p * 2 + (half + 1))
                            act.activation(row[0:PT, half * 512:(half + 1) * 512], ps[4 + half][0:PT, :],
                                           ACT.Gelu).then_inc(p1["gelu_done"], 1)
                    if sums:
                        weights(first, 2)
                    if finish:
                        for half in range(2):
                            act.wait_ge(p1["ht_done"], p * 2 + (half + 1))
                            act.activation(HT[:, half * (KH // 2):(half + 1) * (KH // 2), :],
                                           ps[6 + half][:, 0:KH // 2 * PT].rearrange("p (k n) -> p k n", n=PT),
                                           ACT.Copy).then_inc(p1["ht_copied"], 1)
                    if ahead:
                        if_one_pass(act, first, last, lambda: weights(last, 0))
                    if finish:
                        act.wait_ge(p1["lmax_ready"], p + 1)
                        act.activation(lex[:, :], lg[:, :], ACT.Exp, bias=nmx[:, :], accum_out=se[:, :])\
                            .then_inc(p1["lexp_done"], 1)
                        act.wait_ge(p1["rank_done"], p + 1)
                        act.activation(ranks[:, :], misc[0:PT, 272:272 + 2 * NX], ACT.Copy).then_inc(p1["ranks_in"], 1)
                    if sums:
                        extra_passes(act, first, last, lambda q: [weights(q, c) for c in range(NCH)],
                                     (lambda: weights(last, 0)) if ahead else None)
                weights(0, 0)
                stagger(act, tile)

            @block.tensor
            def _(pe):
                pe.matmul(hist[0:PT, 0:NT], zeros_b[0:PT, 0:PT], zeros_b[0:PT, 0:NT], start=True, stop=False,
                          skip_group_check=True)

                def to_edges(q, d):
                    hold(pe, p1["masks_ready"], q + 1)
                    for j in range(SLOTS):
                        m = pe.matmul(adm[:, j * PW:(j + 1) * PW],
                                      OHT[:, :].rearrange("p (e j) -> p j e", j=SLOTS)[:, j, :], one(node, d, "p a s n -> p (a s n)"), start=True, stop=True)
                    m.then_inc(p1["adm_ready"], 1)

                def sums_of(q, c):
                    j0, j1 = CHUNKS[c]
                    hold(pe, p1["msgs_ready"], q * NCH + (c + 1))
                    for j in range(j0, j1):
                        m = pe.matmul(acc[0:PT, 0:TW + 1], OH[:, j, :], G[:, j, 0:TW + 1], start=False,
                                      stop=False, skip_group_check=True)
                    m.then_inc(p1["seg_done"], 1)

                def tile(d, sums, finish, ahead):
                    p = d - 1
                    if sums:
                        first, last = window_passes(pe, d)
                        if finish:
                            hold(pe, p1["acc_read"], p + 1)
                        pe.matmul(acc[0:PT, 0:TW + 1], ident[0:PT, 0:PT], one(XH[:, :, 0:TW + 1], d), start=True,
                                  stop=False, skip_group_check=True)
                    if sums:
                        sums_of(first, 0)
                    if finish:
                        hold(pe, p1["xn_ready"], p + 1)
                        for k in range(KC):
                            m = pe.transpose(misc[:, k * PT:(k + 1) * PT], xn[0][0:PT, k * 128:(k + 1) * 128],
                                             ident[0:PT, 0:PT])
                        m.then_inc(p1["xT_done"], 1)
                        hold(pe, p1["xT_copied"], p + 1)
                        for half in range(2):
                            for k in range(KC):
                                pe.matmul(ps[4 + half][0:PT, :], xT[0][:, k, 0:PT],
                                          fW1[:, k, half * 512:(half + 1) * 512], start=(k == 0), stop=False)
                            m = pe.matmul(ps[4 + half][0:PT, :], ones_row[:, :],
                                          b1row[:, half * 512:(half + 1) * 512], start=False, stop=True)
                            m.then_inc(p1["h_done"], 1)
                    if sums:
                        sums_of(first, 1)
                        hold(pe, p1["hist_ready"], d + 1)
                        for j in range(EPT):
                            m = pe.matmul(hist[0:PT, 0:NT], olo[:, j, :], ohi[:, j, :], start=False, stop=False,
                                          skip_group_check=True)
                        m.then_inc(p1["hist_done"], 1)
                    if finish:
                        for half in range(2):
                            hold(pe, p1["gelu_done"], p * 2 + (half + 1))
                            for k in range(KH // 2):
                                kk = half * (KH // 2) + k
                                m = pe.transpose(ps[6 + half][:, k * PT:(k + 1) * PT],
                                                 row[0:PT, kk * 128:(kk + 1) * 128], ident[0:PT, 0:PT])
                            m.then_inc(p1["ht_done"], 1)
                        for k in range(KH):
                            if k % (KH // 2) == 0:
                                hold(pe, p1["ht_copied"], p * 2 + (k // (KH // 2) + 1))
                            m = pe.matmul(gate_ps, HT[:, k, :], fWg[:, k, :], start=(k == 0), stop=(k == KH - 1))
                        m.then_inc(p1["gate_done"], 1)
                    if ahead:
                        if_one_pass(pe, first, last, lambda: to_edges(last, d + 1))
                    if sums:
                        sums_of(first, 2)
                    if finish:
                        hold(pe, p1["sel_ready"], p + 1)
                        pe.matmul(rank_ps, before[0:PT, 0:PT], selb[:, :], start=True, stop=True)
                        pe.matmul(all_ps, ones_b[0:PT, 0:PT], selb[:, :], start=True, stop=True)\
                            .then_inc(p1["rank_done"], 1)
                    if sums:
                        def again(q):
                            to_edges(q, d)
                            for c in range(NCH):
                                sums_of(q, c)
                        extra_passes(pe, first, last, again, (lambda: to_edges(last, d + 1)) if ahead else None)
                to_edges(0, 0)
                pe.wait_ge(p1["own_ready"], 1)
                stagger(pe, tile)

            @block.vector
            def _(v):
                chain = Chain(v, v_chain)
                chain.restart()
                chain(v.memset(row[:, :], 0.0))
                v.memset(row[:, HID + C + 1:HID + C + 2].bitcast(I32), NO_NODE).then_inc(p1["pad_ready"], 1)
                v.sem_inc(p1["taken_dst"], 1)
                v.sem_inc(p1["seg_done"], NCH)
                chain(v.tensor_tensor(XH[:, :, 0:C].rearrange("p t (h c) -> p t h c", h=HEADS),
                                      XH[:, :, 0:C].rearrange("p t (h c) -> p t h c", h=HEADS),
                                      e_self[:, :, :].unsqueeze(3).broadcast_to([PT, NT, HEADS, HC]), ALU.mult))
                chain(v.tensor_copy(XH[:, :, C:TW], e_self[:, :, :]))
                v.memset(XH[:, :, TW:TW + 1], 0.0).then_inc(p1["own_ready"], 1)

                def local_targets(q, d):
                    hold(v, p1["win_dst"], q * 16 + 16)
                    chain(v.tensor_scalar(dloc[:, :], dst_win[:, :], tile_lo[:, bass.ds(d, 1)], None, ALU.subtract))
                    hold(v, p1["win_row"], q * 16 + 16)

                def node_masks(q, d):
                    chain(v.tensor_scalar(OHT[:, :], dst_row[:, :], tile_row[0:PT, bass.ds(d, 1)], None,
                                          ALU.is_equal))
                    v.sem_inc(p1["masks_ready"], 1)
                    v.sem_inc(p1["taken_dst"], 1)

                def edge_masks(q, c):
                    j0, j1 = CHUNKS[c]
                    hold(v, p1["seg_done"], q * NCH + (c + 1))
                    chain(v.tensor_tensor(OH[:, j0:j1, :],
                                          iota_c[:, 0:PT].unsqueeze(1).broadcast_to([128, j1 - j0, PT]),
                                          dloc[:, j0:j1].unsqueeze(2).broadcast_to([128, j1 - j0, PT]), ALU.is_equal))

                def node_values(q):
                    hold(v, p1["adm_ready"], q + 1)
                    chain(v.tensor_reduce(ads[:, :, :],
                                          adm[:, 0:SLOTS * PW].rearrange("p (j s n) -> p j n s", s=3, n=2 * HEADS),
                                          AX, ALU.add))

                def logits(q, c):
                    j0, j1 = CHUNKS[c]
                    a = ads[:, j0:j1, :]
                    hold(v, got1[c], (q + 1) * (16 * (j1 - j0)))
                    z = lg4[:, j0:j1, :]
                    chain(v.tensor_tensor(z, G[:, j0:j1, C:TW], a[:, :, 0:HEADS], ALU.add))
                    chain(v.scalar_tensor_tensor(z, z, SLOPE, z, ALU.mult, ALU.max))
                    chain(v.tensor_tensor(z, z, a[:, :, HEADS:2 * HEADS], ALU.subtract))
                    v.tensor_scalar(z, z, 1.0, None, ALU.min).then_inc(p1["z_ready"], 1)

                def messages(q, c):
                    j0, j1 = CHUNKS[c]
                    hold(v, p1["w_ready"], q * NCH + (c + 1))
                    g4 = G[:, j0:j1, 0:C].rearrange("p j (h c) -> p j h c", h=HEADS)
                    v.tensor_tensor(g4, g4, G[:, j0:j1, C:TW].unsqueeze(3).broadcast_to([128, j1 - j0, HEADS, HC]),
                                    ALU.mult).then_inc(p1["msgs_ready"], 1)

                def targets_of(q, d):
                    local_targets(q, d)
                    node_masks(q, d)
                    edge_masks(q, 0)

                def first_messages(q, d):
                    node_values(q)
                    logits(q, 0)
                    edge_masks(q, 1)
                    messages(q, 0)

                def tile(d, sums, finish, ahead):
                    p = d - 1
                    chain.restart()
                    if sums:
                        first, last = window_passes(v, d)
                    if finish:
                        hold(v, p1["std_ready"], p + 1)
                        chain(v.reciprocal(rstd[0:PT, 0:1], std[0:PT, 0:1]))
                        v.tensor_scalar(xn[0][0:PT, :], x1[:, :], mv[0:PT, 0, 0:1], rstd[0:PT, 0:1], ALU.subtract,
                                        ALU.mult).then_inc(p1["xn_ready"], 1)
                    if sums:
                        logits(first, 1)
                        chain(v.tensor_tensor(olo[:, :, :],
                                              iota_b[0:PT, 0:PT].unsqueeze(1).broadcast_to([PT, EPT, PT]),
                                              slo[:, bass.ds(d * EPT, EPT)].unsqueeze(2).broadcast_to([PT, EPT, PT]),
                                              ALU.is_equal))
                        messages(first, 1)
                        edge_masks(first, 2)
                        v.tensor_tensor(ohi[:, :, :], iota_b[0:PT, 0:NT].unsqueeze(1).broadcast_to([PT, EPT, NT]),
                                        shi[:, bass.ds(d * EPT, EPT)].unsqueeze(2).broadcast_to([PT, EPT, NT]),
                                        ALU.is_equal).then_inc(p1["hist_ready"], 1)
                        logits(first, 2)
                    if ahead:
                        if_one_pass(v, first, last, lambda: targets_of(last, d + 1))
                        chain.restart()
                    if sums:
                        messages(first, 2)
                        hold(v, p1["x_in"], d * 16 + 16)
                        chain(v.tensor_tensor(xt[:, :], xt[:, :], bias0[0:PT, :], ALU.add))
                    if finish:
                        hold(v, p1["gate_done"], p + 1)
                        hold(v, p1["scattered"], p * 16 + 16)
                        chain(v.tensor_tensor(lg[:, :], gate_ps, bgrow[0:PT, :], ALU.add))
                        chain(v.tensor_reduce(lmax[:, :], lg[:, :], AX, ALU.max))
                        v.tensor_scalar(nmx[:, :], lmax[:, :], -1.0, None, ALU.mult).then_inc(p1["lmax_ready"], 1)
                        chain(v.tensor_scalar(cand[:, :], lg[:, :], lmax[:, :], BIG, ALU.is_lt, ALU.mult))
                        chain(v.tensor_tensor(cand[:, :], cand[:, :], iota_c[0:PT, 0:NX], ALU.add))
                        chain(v.tensor_reduce(amin[:, :], cand[:, :], AX, ALU.min))
                        chain(v.tensor_scalar(sel[:, :], iota_c[0:PT, 0:NX], amin[:, :], None, ALU.is_equal))
                        v.tensor_copy(selb[:, :], sel[:, :]).then_inc(p1["sel_ready"], 1)
                    if ahead:
                        if_one_pass(v, first, last, lambda: first_messages(last, d + 1))
                        chain.restart()
                    if finish:
                        hold(v, p1["lexp_done"], p + 1)
                        chain(v.reciprocal(row[0:PT, HID + C:HID + C + 1], se[:, :]))
                        v.tensor_copy(row[0:PT, HID + C + 1:HID + C + 2].bitcast(I32),
                                      tile_row[0:PT, bass.ds(p, 1)]).then_inc(p1["row_ready"], 1)
                    if sums:
                        def again(q):
                            chain.restart()
                            local_targets(q, d)
                            node_masks(q, d)
                            for c in range(NCH):
                                edge_masks(q, c)
                            node_values(q)
                            for c in range(NCH):
                                logits(q, c)
                                messages(q, c)
                        def prepare():
                            targets_of(last, d + 1)
                            first_messages(last, d + 1)
                        extra_passes(v, first, last, again, prepare if ahead else None)
                        chain.restart()
                        hold(v, p1["seg_done"], last * NCH + NCH)
                        hold(v, p1["hist_done"], d + 1)
                        if finish:
                            hold(v, p1["gelu_done"], p * 2 + 2)
                        chain(v.reciprocal(r4[:, :], acc[0:PT, C:TW]))
                        chain(v.tensor_tensor(x1[:, :].rearrange("p (h c) -> p h c", h=HEADS),
                                              acc[0:PT, 0:C].rearrange("p (h c) -> p h c", h=HEADS),
                                              r4[:, :].unsqueeze(2).broadcast_to([PT, HEADS, HC]), ALU.mult))
                        chain(v.tensor_copy(deg_in[:, bass.ds(d, 1)], acc[0:PT, TW:TW + 1]))
                        v.sem_inc(p1["acc_read"], 1)
                        chain(v.tensor_tensor(x1[:, :], x1[:, :], xt[:, :], ALU.add))
                        chain(v.bn_stats(st[0:PT, 0, :], x1[:, :]))
                        v.bn_aggr(mv[0:PT, 0, :], st[0:PT, 0, :]).then_inc(p1["var_ready"], 1)
                targets_of(0, 0)
                first_messages(0, 0)
                stagger(v, tile)

        hist = ps[2]
        p2 = {n: sem("moe_" + n) for n in (
            "deg_ready", "sq_ready", "rs_ready", "tab_ready", "pads", "ht_done",
            "ht_copied", "y_done", "var_ready", "std_ready", "ids_ready", "rs_got", "h_ready",
            "bnt_done", "row_used", "x1_kept")}
        rin = sem("rin", 2)
        sent = sem("sent", 2)
        weights0.close()
        w3 = ExitStack()
        s3w = allocator(w3)
        L1 = s3w("L1", [128, NX, KC, C])
        L2 = s3w("L2", [128, NX, KC, C])
        L3 = s3w("L3", [128, NX, KC, C])
        experts_in = sem("experts_in")
        with ExitStack() as c2, nc.Block() as block:
            s2 = allocator(c2)
            rbuf = [s2(f"rbuf{i}", [128, ROW]) for i in range(2)]
            HT = [s2(f"HTb{i}", [128, KH, 128]) for i in range(2)]
            pads = s2("pads", [128, ROW])
            degs = s2("degs", [PT, 2, NT])
            sqs = s2("sqs", [PT, 2, NT])
            rsq = s2("rsq", [PT, 2, NT])
            nt8 = s2("nt8", [128, NX])
            ct8 = s2("ct8", [128, NX])
            one8 = s2("one8", [128, NX])
            ge = s2("ge", [128, TMAX, NX])
            gn = s2("gn", [128, TMAX, NX])
            te = s2("te", [128, TMAX])
            ts_ = s2("ts_", [128, TMAX])
            tr = s2("tr", [128, TMAX])
            ttab = s2("ttab", [1, 2, TMAX], I32)
            ptab = s2("ptab", [1, NX + 1], I32)
            pf = s2("pf", [128, NX + 1])
            ids_in = [s2(f"ids_in{i}", [128, 1], I32) for i in range(2)]
            ids = [s2(f"ids{i}", [128, 1], I32) for i in range(2)]
            rsg = [s2(f"rsg{i}", [128, 1]) for i in range(2)]
            x1p = [s2(f"x1p{i}", [128, C + 1]) for i in range(2)]
            x2 = [s2(f"x2_{i}", [128, C]) for i in range(2)]
            hx = [s2(f"hx{i}", [128, C]) for i in range(2)]
            hparts = [s2(f"hparts{i}", [128, 2, C], F16) for i in range(2)]

            def last_pair(eng):
                eng.wait_ge(p2["tab_ready"], 2)
                return eng.value_load(ptab[0:1, NX:NX + 1], min_val=(NT - 1) // 2, max_val=TMAX // 2 - 1)

            def by_pairs(eng, turn, finish, also=None):
                last = last_pair(eng)
                turn(0, 0)

                def pair(u):
                    turn(u, 1)
                    finish(u, 0)
                    turn(u + 1, 0)
                    finish(u, 1)
                if also:
                    with eng.Fori(0, NX) as u:
                        pair(u)
                        also(u)
                with eng.Fori(NX if also else 0, last) as u:
                    pair(u)
                turn(last, 1)
                finish(last, 0)
                finish(last, 1)

            @block.sync
            def _(sp):
                sp.wait_ge(p2["tab_ready"], 2)
                for e in range(NX):
                    at = sp.value_load(ptab[0:1, e:e + 1], min_val=0, max_val=NX * REG)
                    sp.dma_start(sorted_rows[bass.ds(at, 128), :], pads[:, :]).then_inc(p2["pads"], 16)
                sp.wait_ge(p2["pads"], 16 * NX)
                last = last_pair(sp)
                with sp.Fori(0, last + 1) as u:
                    for b in range(2):
                        at = sp.value_load(ttab[0:1, 1, bass.ds(u * 2 + b, 1)], min_val=0, max_val=NX * REG)
                        sp.wait_ge(p2["row_used"], u * 2 + (b + 1))
                        sp.dma_start(rbuf[b][:, :], sorted_rows[bass.ds(at, 128), :]).then_inc(rin[b], 16)
                for b in range(2):
                    hold(sp, sent[b], last * 32 + 48)

            @block.gpsimd
            def _(pool):
                pool.wait_ge(p2["rs_ready"], 1)
                half = NT // 2
                with nc.allow_non_contiguous_dma(reason="one value a node, once"):
                    for b, (t0, t1) in enumerate(((0, half), (half, NT))):
                        pool.dma_start(rs_rows[t0 * PT:t1 * PT, :].rearrange("(t p) a -> p (t a)", p=PT),
                                       rsq[:, 0, t0:t1]).then_inc(sent[b], 16)
                for b in range(2):
                    pool.wait_ge(sent[b], 16)
                last = last_pair(pool)
                with pool.Fori(0, last + 1) as u:
                    for b in range(2):
                        hold(pool, p2["ids_ready"], u * 2 + (b + 1))
                        pool.indirect_dma_start(rsg[b][:, :], None, rs_rows,
                                                bass.IndirectOffsetOnAxis(ids_in[b][:, :], 0),
                                                bounds_check=N - 1, oob_is_err=False).then_inc(p2["rs_got"], 16)
                        hold(pool, p2["h_ready"], u * 2 + (b + 1))
                        pool.indirect_dma_start(x2_rows, bass.IndirectOffsetOnAxis(ids[b][:, :], 0), x2[b][:, :], None,
                                                bounds_check=N - 1, oob_is_err=False).then_inc(sent[b], 16)
                        pool.indirect_dma_start(table1, bass.IndirectOffsetOnAxis(ids[b][:, :], 0),
                                                hparts[b][:, :, :].rearrange("p s c -> p (s c)"), None,
                                                bounds_check=N - 1, oob_is_err=False).then_inc(sent[b], 16)

            @block.scalar
            def _(act):
                act.wait_ge(p2["deg_ready"], 1)
                act.activation(sqs[:, :, :], degs[:, :, :], ACT.Sqrt).then_inc(p2["sq_ready"], 1)

                def turn(u, b):
                    hold(act, p2["y_done"], u * 2 + (b + 1))
                    for half in range(2):
                        act.wait_ge(p2["ht_done"], u * 4 + (2 * b + half + 1))
                        act.activation(HT[b][:, half * (KH // 2):(half + 1) * (KH // 2), :],
                                       ps[2 * b + half][:, :].rearrange("p (k n) -> p k n", n=128),
                                       ACT.Copy).then_inc(p2["ht_copied"], 1)

                def finish(u, b):
                    act.wait_ge(p2["var_ready"], u * 2 + (b + 1))
                    act.activation(std[:, b:b + 1], mv[:, b, 1:2], ACT.Sqrt, bias=eps_ln[:, :])\
                        .then_inc(p2["std_ready"], 1)

                def load_expert(e):
                    for tile, w in ((L1, f1_W1), (L2, f1_W2), (L3, f1_Wo)):
                        act.dma_start(tile[:, bass.ds(e, 1), :, :].rearrange("p a k n -> p (a k) n"),
                                      w[bass.ds(e, 1), :, :].rearrange("a (k p) n -> p (a k) n", p=128))\
                            .then_inc(experts_in, 16)
                by_pairs(act, turn, finish, load_expert)

            @block.tensor
            def _(pe):
                pe.transpose(ps[7][:, 0:128], bn_rows[0][:, :], ident[:, :])
                pe.transpose(ps[7][:, 128:160], bn_rows[1][:, :], ident[0:32, 0:32]).then_inc(p2["bnt_done"], 1)
                pe.sem_inc(p2["y_done"], 2)

                def turn(u, b):
                    hold(pe, rin[b], u * 16 + 16)
                    hold(pe, p2["ht_copied"], u * 4 + (2 * b + 2))
                    for half in range(2):
                        for k in range(KH // 2):
                            kk = half * (KH // 2) + k
                            m = pe.transpose(ps[2 * b + half][:, k * 128:(k + 1) * 128],
                                             rbuf[b][:, kk * 128:(kk + 1) * 128], ident[:, :])
                        m.then_inc(p2["ht_done"], 1)

                def finish(u, b):
                    e = pe.value_load(ttab[0:1, 0, bass.ds(u * 2 + b, 1)], min_val=0, max_val=NX - 1)
                    for k in range(KH):
                        if k % (KH // 2) == 0:
                            hold(pe, p2["ht_copied"], u * 4 + (2 * b + k // (KH // 2) + 5))
                        m = pe.matmul(ps[4 + b][:, 0:C], HT[b][:, k, :],
                                      Wd[:, bass.ds(e, 1), k, :].rearrange("p a c -> p (a c)"),
                                      start=(k == 0), stop=(k == KH - 1))
                    m.then_inc(p2["y_done"], 1)
                pe.sem_inc(p2["ht_copied"], 4)
                by_pairs(pe, turn, finish)

            @block.vector
            def _(v):
                chain = Chain(v, v_chain)
                chain.restart()
                v.sem_inc(p2["row_used"], 2)
                v.wait_ge(p2["bnt_done"], 1)
                chain(v.tensor_copy(bnT[:, :, :, :].rearrange("p i e k -> p (i e k)"), ps[7][:, 0:160]))
                chain(v.tensor_scalar(degs[:, 0, :], hist[0:PT, 0:NT], 1.0, None, ALU.max))
                v.tensor_scalar(degs[:, 1, :], deg_in[:, :], 1.0, None, ALU.max).then_inc(p2["deg_ready"], 1)
                v.wait_ge(p2["sq_ready"], 1)
                v.reciprocal(rsq[:, :, :], sqs[:, :, :]).then_inc(p2["rs_ready"], 1)
                v.wait_ge(p2["rs_ready"], 1)
                chain(v.tensor_copy(deg_in[:, :], rsq[:, 1, :]))
                v.memset(one8[:, :], 1.0)
                v.memset(rsg[0][:, :], 0.0)
                chain(v.memset(rsg[1][:, :], 0.0))
                chain(v.tensor_scalar(nt8[0:PT, :], cnt[0:PT, :], 1.0 / 128, 0.5 - 1.0 / 512, ALU.mult, ALU.add))
                chain(v.tensor_scalar(nt8[0:PT, :], nt8[0:PT, :], MAGIC, None, ALU.add))
                chain(v.tensor_scalar(nt8[0:PT, :], nt8[0:PT, :], -MAGIC, None, ALU.add))
                chain(v.tensor_tensor_scan(ct8[0:PT, :], one8[0:PT, :], nt8[0:PT, :], 0.0, ALU.mult, ALU.add))
                chain(v.tensor_tensor(ge[0:PT, :, :], iota_c[0:PT, 0:TMAX].unsqueeze(2).broadcast_to([PT, TMAX, NX]),
                                      ct8[0:PT, :].unsqueeze(1).broadcast_to([PT, TMAX, NX]), ALU.is_ge))
                chain(v.tensor_tensor(gn[0:PT, :, :], ge[0:PT, :, :],
                                      nt8[0:PT, :].unsqueeze(1).broadcast_to([PT, TMAX, NX]), ALU.mult))
                chain(v.tensor_reduce(te[0:PT, :], ge[0:PT, :, :], AX, ALU.add))
                chain(v.tensor_reduce(ts_[0:PT, :], gn[0:PT, :, :], AX, ALU.add))
                chain(v.tensor_tensor(tr[0:PT, :], iota_c[0:PT, 0:TMAX], ts_[0:PT, :], ALU.subtract))
                chain(v.tensor_scalar(ts_[0:PT, :], te[0:PT, :], REG / 128.0, None, ALU.mult))
                chain(v.tensor_tensor(tr[0:PT, :], tr[0:PT, :], ts_[0:PT, :], ALU.add))
                chain(v.tensor_scalar(tr[0:PT, :], tr[0:PT, :], 128.0, float(NX * REG), ALU.mult, ALU.min))
                chain(v.tensor_scalar(te[0:PT, :], te[0:PT, :], float(NX - 1), None, ALU.min))
                chain(v.tensor_tensor(pf[0:PT, 0:NX], region8[0:PT, :], cnt[0:PT, :], ALU.add))
                chain(v.tensor_scalar(pf[0:PT, NX:NX + 1], ct8[0:PT, NX - 1:NX], 0.5, -0.75, ALU.mult, ALU.add))
                chain(v.tensor_scalar(pf[0:PT, NX:NX + 1], pf[0:PT, NX:NX + 1], MAGIC, None, ALU.add))
                chain(v.tensor_scalar(pf[0:PT, NX:NX + 1], pf[0:PT, NX:NX + 1], -MAGIC, None, ALU.add))
                chain(v.tensor_copy(ttab[0:1, 0, :], te[0:1, :]))
                chain(v.tensor_copy(ttab[0:1, 1, :], tr[0:1, :]))
                v.tensor_copy(ptab[0:1, :], pf[0:1, :]).then_inc(p2["tab_ready"], 1)
                chain(v.memset(pads[:, :], 0.0))
                v.memset(pads[:, HID + C + 1:HID + C + 2].bitcast(I32), NO_NODE).then_inc(p2["tab_ready"], 1)

                def turn(u, b):
                    hold(v, rin[b], u * 16 + 16)
                    v.tensor_copy(ids_in[b][:, :], rbuf[b][:, HID + C + 1:HID + C + 2].bitcast(I32))\
                        .then_inc(p2["ids_ready"], 1)
                    v.tensor_copy(x1p[b][:, :], rbuf[b][:, HID:HID + C + 1]).then_inc(p2["x1_kept"], 1)
                    hold(v, p2["x1_kept"], u * 2 + (b + 1))
                    hold(v, p2["ht_done"], u * 4 + (2 * b + 2))
                    v.sem_inc(p2["row_used"], 1)

                def finish(u, b):
                    chain.restart()
                    e = v.value_load(ttab[0:1, 0, bass.ds(u * 2 + b, 1)], min_val=0, max_val=NX - 1)
                    hold(v, p2["y_done"], u * 2 + (b + 3))
                    hold(v, sent[b], u * 32 + 16)
                    chain(v.tensor_copy(ids[b][:, :], ids_in[b][:, :]))
                    chain(v.tensor_tensor(x2[b][:, :], ps[4 + b][:, 0:C], one(bdrow, e), ALU.add))
                    chain(v.scalar_tensor_tensor(x2[b][:, :], x2[b][:, :], x1p[b][:, C:C + 1],
                                                 x1p[b][:, 0:C], ALU.mult, ALU.add))
                    chain(v.bn_stats(st[:, b, :], x2[b][:, :]))
                    v.bn_aggr(mv[:, b, :], st[:, b, :]).then_inc(p2["var_ready"], 1)
                    hold(v, p2["std_ready"], u * 2 + (b + 1))
                    chain(v.reciprocal(rstd[:, b:b + 1], std[:, b:b + 1]))
                    hold(v, p2["rs_got"], u * 32 + (16 * b + 16))
                    chain(v.tensor_tensor(rstd[:, b:b + 1], rstd[:, b:b + 1], rsg[b][:, :], ALU.mult))
                    chain(v.tensor_scalar(hx[b][:, :], x2[b][:, :], mv[:, b, 0:1], rstd[:, b:b + 1], ALU.subtract,
                                          ALU.mult))
                    chain(v.tensor_copy(hparts[b][:, 0, :], hx[b][:, :]))
                    chain(v.tensor_tensor(hx[b][:, :], hx[b][:, :], hparts[b][:, 0, :], ALU.subtract))
                    v.tensor_scalar(hparts[b][:, 1, :], hx[b][:, :], LOW, None, ALU.mult).then_inc(p2["h_ready"], 1)
                by_pairs(v, turn, finish)


        p3 = {n: sem("gcn_" + n) for n in (
            "weights", "win_src", "win_dst", "taken_src", "taken_dst", "idx_ready", "masks_ready", "seg_done",
            "ag_ready", "agT_done", "agT_copied", "hw_done", "ss_ready", "nrm_ready", "var_ready", "std_ready",
            "xn_ready", "xT_done", "xT_copied", "gate_done", "lmax_ready", "lexp_done", "w_ready", "wT_done",
            "wT_copied", "bo_done", "h1_done", "h1_act", "h2_done", "h2_act", "y_done", "y_taken", "x2_in", "out_ready",
            "written", "sq_in", "sq_out", "zero_done", "xF_copied", "bns_ready")}
        got3 = sem("gcn_got", NCH)
        with ExitStack() as c3, nc.Block() as block:
            s3 = allocator(c3)
            W1g = s3("W1g", [128, KC, C])
            b1g = s3("b1g", [128, C])
            Wr = s3("Wr", [128, KC, NX])
            brrow = s3("brrow", [128, NX])
            bo = s3("bo", [NX, C])
            bns = s3("bns", [128, 4, NX, KC])
            bsq = s3("bsq", [128, 2, NX, KC])
            x2t = s3("x2t", [PT, C])
            ag = s3("ag", [PT, C])
            agT = s3("agT", [128, KC, PT])
            hh = s3("hh", [PT, C])
            hsq = s3("hsq", [PT, C])
            ss = s3("ss", [PT, 1])
            nrm = s3("nrm", [PT, 1])
            x3 = s3("x3", [PT, C])
            lg = s3("lg3", [PT, NX])
            lex = s3("lex3", [PT, NX])
            lmx = s3("lmx", [PT, 1])
            nmx = s3("nmx3", [PT, 1])
            se = s3("se3", [PT, 1])
            rse = s3("rse", [PT, 1])
            wgt = s3("wgt", [PT, NX])
            wT = s3("wT", [NX, PT])
            h1 = [s3(f"h1_{i}", [128, KC, PT]) for i in range(2)]
            h2 = [s3(f"h2_{i}", [128, KC, PT]) for i in range(2)]
            ot = s3("ot", [PT, C])
            xF = s3("xF", [128, KC, PT])
            wgtF = s3("wgtF", [PT, NX])
            base = s3("base", [PT, C])
            zeros_h = s3("zeros_h", [128, 2 * C], F16)
            iota_h = s3("iota_h", [128, PT], F16)
            dloc_h = s3("dloc_h", [128, SLOTS], F16)
            OH16 = s3("OH16", [128, SLOTS, PT], F16)
            acc, misc = ps[0], ps[1]
            agT_ps = misc[:, 0:KC * PT].rearrange("p (k n) -> p k n", k=KC)
            hw_ps = ps[2][0:PT, 0:C]
            gate_ps = ps[2][0:PT, C:C + NX]
            y_ps = ps[7][0:PT, 0:C]
            wT_ps = ps[2][0:NX, C + 16:C + 16 + PT]

            def pipeline(eng, tile, experts=None):
                tile(0, True, False, False)
                tile(1, True, True, False)
                if experts:
                    experts()
                with eng.Fori(0, (NT - 2) // 2) as i:
                    tile(i * 2 + 2, True, True, True)
                    tile(i * 2 + 3, True, True, True)
                if NT % 2:
                    tile(NT - 1, True, True, True)
                tile(NT, False, True, True)
                tile(NT + 1, False, False, True)

            @block.sync
            def _(sp):
                sp.dma_start(W1g[:, :, :], g1_W.rearrange("(k p) n -> p k n", p=128)).then_inc(p3["weights"], 16)
                sp.dma_start(b1g[:, :], g1_b.partition_broadcast(128)).then_inc(p3["weights"], 16)
                sp.dma_start(Wr[:, :, :], f1_Wr.rearrange("(k p) n -> p k n", p=128)).then_inc(p3["weights"], 16)
                sp.dma_start(brrow[:, :], f1_br.partition_broadcast(128)).then_inc(p3["weights"], 16)
                sp.dma_start(bo[:, :], f1_bo).then_inc(p3["weights"], 16)
                load_windows(sp, p3["taken_src"], p3["taken_dst"], p3["win_src"], p3["win_dst"])

            @block.gpsimd
            def _(pool):
                pool.sem_inc(p3["taken_src"], 1)
                with pool.Fori(0, NT) as d:
                    first, last = window_passes(pool, d)
                    with pool.Fori(first, last) as q:
                        gather_pass(pool, q, table1, rows16, p3["win_src"], p3["taken_src"], p3["seg_done"],
                                    p3["idx_ready"], got3)

            @block.scalar
            def _(act):
                x2v = x2_rows.rearrange("(t p) c -> t p c", p=PT)
                ov = out.rearrange("(t p) c -> t p c", p=PT)
                act.wait_ge(p3["sq_in"], 1)
                act.activation(bsq[:, :, :, :], bsq[:, :, :, :], ACT.Sqrt, bias=eps_bn[:, :]).then_inc(p3["sq_out"], 1)

                def hidden1(f, e):
                    act.wait_ge(p3["h1_done"], f * NX + (e + 1))
                    for k in range(KC):
                        m = act.activation(h1[e % 2][:, k, :], ps[3 + e % 2][:, k * PT:(k + 1) * PT], ACT.Relu,
                                           bias=bns[:, 1, e, k:k + 1], scale=bns[:, 0, e, k:k + 1])
                    m.then_inc(p3["h1_act"], 1)

                def hidden2(f, e):
                    act.wait_ge(p3["h2_done"], f * NX + (e + 1))
                    for k in range(KC):
                        m = act.activation(h2[e % 2][:, k, :], ps[5 + e % 2][:, k * PT:(k + 1) * PT], ACT.Relu,
                                           bias=bns[:, 3, e, k:k + 1], scale=bns[:, 2, e, k:k + 1])
                    m.then_inc(p3["h2_act"], 1)

                def store(f):
                    hold(act, p3["out_ready"], f + 1)
                    act.dma_start(ov[bass.ds(f, 1), :, :].rearrange("a p c -> (a p) c"), ot[:, :])\
                        .then_inc(p3["written"], 16)

                def tile(k, sums, layer, mix):
                    t, f = k - 1, k - 2
                    for i in range(NX + 1):
                        if mix and i < NX:
                            hidden1(f, i)
                        if layer and i == 0:
                            act.wait_ge(p3["agT_done"], t + 1)
                            act.activation(agT[:, :, :], agT_ps, ACT.Copy).then_inc(p3["agT_copied"], 1)
                        if layer and i == 2:
                            act.wait_ge(p3["ss_ready"], t + 1)
                            act.activation(nrm[:, :], ss[:, :], ACT.Sqrt).then_inc(p3["nrm_ready"], 1)
                        if layer and i == 3:
                            act.wait_ge(p3["var_ready"], t + 1)
                            act.activation(std[0:PT, 0:1], mv[0:PT, 0, 1:2], ACT.Sqrt, bias=eps_ln[0:PT, :])\
                                .then_inc(p3["std_ready"], 1)
                        if layer and i == 6:
                            act.wait_ge(p3["lmax_ready"], t + 1)
                            act.activation(lex[:, :], lg[:, :], ACT.Exp, bias=nmx[:, :], accum_out=se[:, :])\
                                .then_inc(p3["lexp_done"], 1)
                        if mix and i >= 1:
                            hidden2(f, i - 1)
                        if layer and i == 4:
                            act.wait_ge(p3["xT_done"], t + 1)
                            act.activation(xT[0][:, :, 0:PT], agT_ps, ACT.Copy).then_inc(p3["xT_copied"], 1)
                        if sums and i == 4:
                            act.dma_start(x2t[:, :], x2v[bass.ds(k, 1), :, :].rearrange("a p c -> (a p) c"))\
                                .then_inc(p3["x2_in"], 16)
                    if layer:
                        act.activation(xF[:, :, :], xT[0][:, :, 0:PT], ACT.Copy).then_inc(p3["xF_copied"], 1)
                    if mix:
                        store(f)
                pipeline(act, tile, lambda: act.wait_ge(p3["bns_ready"], 1))
                act.wait_ge(p3["written"], 16 * NT)

            @block.tensor
            def _(pe):
                def opened():
                    pe.matmul(acc[0:PT, :], zeros_h[:, 0:PT], zeros_h[:, :], start=True, stop=False,
                              skip_group_check=True)

                def sums_of(q, c):
                    j0, j1 = CHUNKS[c]
                    hold(pe, p3["masks_ready"], q * NCH + (c + 1))
                    hold(pe, got3[c], (q + 1) * (16 * (j1 - j0)))
                    for j in range(j0, j1):
                        m = pe.matmul(acc[0:PT, :], OH16[:, j, :], rows16(j), start=False, stop=False,
                                      skip_group_check=True)
                    m.then_inc(p3["seg_done"], 1)

                def product1(f, e):
                    if e == 0:
                        hold(pe, p3["xF_copied"], f + 1)
                    if e >= 2:
                        hold(pe, p3["h1_act"], f * NX + (e - 1))
                    for k in range(KC):
                        for kk in range(KC):
                            m = pe.matmul(ps[3 + e % 2][:, k * PT:(k + 1) * PT],
                                          L1[:, e, kk, k * 128:(k + 1) * 128], xF[:, kk, :],
                                          start=(kk == 0), stop=(kk == KC - 1))
                    m.then_inc(p3["h1_done"], 1)

                def product2(f, e):
                    hold(pe, p3["h1_act"], f * NX + (e + 1))
                    if e >= 2:
                        hold(pe, p3["h2_act"], f * NX + (e - 1))
                    for k in range(KC):
                        for kk in range(KC):
                            m = pe.matmul(ps[5 + e % 2][:, k * PT:(k + 1) * PT],
                                          L2[:, e, kk, k * 128:(k + 1) * 128], h1[e % 2][:, kk, :],
                                          start=(kk == 0), stop=(kk == KC - 1))
                    m.then_inc(p3["h2_done"], 1)

                def product3(f, e):
                    hold(pe, p3["h2_act"], f * NX + (e + 1))
                    hold(pe, p3["y_taken"], f * NX + (e + 1))
                    for kk in range(KC):
                        m = pe.matmul(y_ps, h2[e % 2][:, kk, :], L3[:, e, kk, :], start=(kk == 0), stop=(kk == KC - 1))
                    m.then_inc(p3["y_done"], 1)

                def tile(k, sums, layer, mix):
                    t, f = k - 1, k - 2
                    if sums:
                        first, last = window_passes(pe, k)
                    for i in range(NX + 2):
                        if sums and i in (7, 8):
                            sums_of(first, i - 6)
                        if mix and i < NX:
                            product1(f, i)
                        if mix and 1 <= i <= NX:
                            product2(f, i - 1)
                        if mix and i >= 2:
                            product3(f, i - 2)
                        if layer and i == 0:
                            hold(pe, p3["ag_ready"], t + 1)
                            for kk in range(KC):
                                m = pe.transpose(misc[:, kk * PT:(kk + 1) * PT], ag[:, kk * 128:(kk + 1) * 128],
                                                 ident[0:PT, 0:PT])
                            m.then_inc(p3["agT_done"], 1)
                        if layer and i == 1:
                            hold(pe, p3["agT_copied"], t + 1)
                            for kk in range(KC):
                                m = pe.matmul(hw_ps, agT[:, kk, :], W1g[:, kk, :], start=(kk == 0), stop=(kk == KC - 1))
                            m.then_inc(p3["hw_done"], 1)
                        if layer and i == 4:
                            hold(pe, p3["xn_ready"], t + 1)
                            for kk in range(KC):
                                m = pe.transpose(misc[:, kk * PT:(kk + 1) * PT], xn[0][0:PT, kk * 128:(kk + 1) * 128],
                                                 ident[0:PT, 0:PT])
                            m.then_inc(p3["xT_done"], 1)
                        if layer and i == 5:
                            hold(pe, p3["xT_copied"], t + 1)
                            for kk in range(KC):
                                m = pe.matmul(gate_ps, xT[0][:, kk, 0:PT], Wr[:, kk, :], start=(kk == 0),
                                              stop=(kk == KC - 1))
                            m.then_inc(p3["gate_done"], 1)
                        if layer and i == 7:
                            hold(pe, p3["w_ready"], t + 1)
                            pe.transpose(wT_ps, wgt[:, :], ident[0:PT, 0:PT]).then_inc(p3["wT_done"], 1)
                        if layer and i == 8:
                            hold(pe, p3["wT_copied"], t + 1)
                            pe.matmul(hw_ps, wT[:, :], bo[:, :], start=True, stop=True).then_inc(p3["bo_done"], 1)
                        if sums and i == 5:
                            opened()
                            sums_of(first, 0)
                    if sums:
                        extra_passes(pe, first, last, lambda q: [sums_of(q, c) for c in range(NCH)])
                pe.wait_ge(p3["weights"], 16 * 5)
                pe.wait_ge(p3["zero_done"], 1)
                pipeline(pe, tile, lambda: pe.wait_ge(experts_in, 16 * 3 * NX))

            @block.vector
            def _(v):
                chain = Chain(v, v_chain)
                chain.restart()
                v.sem_inc(p3["taken_dst"], 1)
                v.sem_inc(p3["seg_done"], NCH)
                v.sem_inc(p3["y_taken"], 1)
                v.tensor_copy(iota_h[:, :], iota_c[:, 0:PT])
                chain(v.memset(zeros_h[:, :], 0.0))
                v.sem_inc(p3["zero_done"], 1)
                for i in range(2):
                    ins = v.tensor_copy(bsq[:, i, :, :], bnT[:, 5 * i + 4, :, :])
                    if i == 0:
                        chain(ins)
                ins.then_inc(p3["sq_in"], 1)
                v.wait_ge(p3["sq_out"], 1)
                chain(v.reciprocal(bsq[:, :, :, :], bsq[:, :, :, :]))
                for i in range(2):
                    chain(v.tensor_tensor(bns[:, 2 * i, :, :], bsq[:, i, :, :], bnT[:, 5 * i + 1, :, :], ALU.mult))
                    chain(v.tensor_tensor(bns[:, 2 * i + 1, :, :], bnT[:, 5 * i, :, :], bnT[:, 5 * i + 3, :, :],
                                          ALU.subtract))
                    chain(v.tensor_tensor(bns[:, 2 * i + 1, :, :], bns[:, 2 * i + 1, :, :], bns[:, 2 * i, :, :], ALU.mult))
                    chain(v.tensor_tensor(bns[:, 2 * i + 1, :, :], bns[:, 2 * i + 1, :, :], bnT[:, 5 * i + 2, :, :],
                                          ALU.add))
                v.sem_inc(p3["bns_ready"], 1)
                v.wait_ge(p3["weights"], 16 * 5)

                def local_targets(q, d):
                    hold(v, p3["win_dst"], q * 16 + 16)
                    chain(v.tensor_scalar(dloc_h[:, :], dst_win[:, :], tile_lo[:, bass.ds(d, 1)], None, ALU.subtract))
                    v.sem_inc(p3["taken_dst"], 1)

                def masks(q, c):
                    j0, j1 = CHUNKS[c]
                    hold(v, p3["seg_done"], q * NCH + (c + 1))
                    v.tensor_tensor(OH16[:, j0:j1, :],
                                    iota_h[:, :].unsqueeze(1).broadcast_to([128, j1 - j0, PT]),
                                    dloc_h[:, j0:j1].unsqueeze(2).broadcast_to([128, j1 - j0, PT]),
                                    ALU.is_equal).then_inc(p3["masks_ready"], 1)
                    if c == NCH - 1:
                        hold(v, p3["masks_ready"], q * NCH + NCH)

                def mixed(f, e):
                    hold(v, p3["y_done"], f * NX + (e + 1))
                    if e == 0:
                        if not isinstance(f, int) or f > 0:
                            hold(v, p3["written"], f * 16)
                        before_it = base
                    else:
                        before_it = ot
                    v.scalar_tensor_tensor(ot[:, :], y_ps, wgtF[:, e:e + 1], before_it[:, :], ALU.mult,
                                           ALU.add).then_inc(p3["y_taken"], 1)
                    hold(v, p3["y_taken"], f * NX + (e + 2))

                def tile(k, sums, layer, mix):
                    t, f = k - 1, k - 2
                    chain.restart()
                    if sums:
                        first, last = window_passes(v, k)
                    if mix:
                        chain(v.tensor_copy(wgtF[:, :], wgt[:, :]))
                    if layer:
                        hold(v, p3["hw_done"], t + 1)
                        chain(v.tensor_tensor(hh[:, :], hw_ps, b1g[0:PT, :], ALU.add))
                        chain(v.tensor_scalar(hh[:, :], hh[:, :], 0.0, None, ALU.max))
                        v.tensor_tensor_reduce(hsq[:, :], hh[:, :], hh[:, :], 1.0, 0.0, ALU.mult, ALU.add, ss[:, :])\
                            .then_inc(p3["ss_ready"], 1)
                    if mix:
                        mixed(f, 0)
                    if layer:
                        hold(v, p3["nrm_ready"], t + 1)
                        chain(v.tensor_scalar(nrm[:, :], nrm[:, :], EPS_NORM, None, ALU.max))
                        chain(v.reciprocal(nrm[:, :], nrm[:, :]))
                        hold(v, p3["x2_in"], t * 16 + 16)
                        chain(v.scalar_tensor_tensor(x3[:, :], hh[:, :], nrm[:, :], x2t[:, :], ALU.mult, ALU.add))
                        chain(v.bn_stats(st[0:PT, 0, :], x3[:, :]))
                        v.bn_aggr(mv[0:PT, 0, :], st[0:PT, 0, :]).then_inc(p3["var_ready"], 1)
                    if layer:
                        hold(v, p3["std_ready"], t + 1)
                        chain(v.reciprocal(rstd[0:PT, 0:1], std[0:PT, 0:1]))
                        v.tensor_scalar(xn[0][0:PT, :], x3[:, :], mv[0:PT, 0, 0:1], rstd[0:PT, 0:1], ALU.subtract,
                                        ALU.mult).then_inc(p3["xn_ready"], 1)
                    if mix:
                        mixed(f, 1)
                    if sums:
                        local_targets(first, k)
                        masks(first, 0)
                    if mix:
                        mixed(f, 2)
                        mixed(f, 3)
                    if layer:
                        hold(v, p3["gate_done"], t + 1)
                        chain(v.tensor_tensor(lg[:, :], gate_ps, brrow[0:PT, :], ALU.add))
                        chain(v.tensor_reduce(lmx[:, :], lg[:, :], AX, ALU.max))
                        v.tensor_scalar(nmx[:, :], lmx[:, :], -1.0, None, ALU.mult).then_inc(p3["lmax_ready"], 1)
                    if sums:
                        masks(first, 1)
                    if mix:
                        mixed(f, 4)
                    if layer:
                        hold(v, p3["lexp_done"], t + 1)
                        chain(v.reciprocal(rse[:, :], se[:, :]))
                        v.tensor_scalar(wgt[:, :], lex[:, :], rse[:, :], None, ALU.mult).then_inc(p3["w_ready"], 1)
                    if sums:
                        masks(first, 2)
                    if mix:
                        mixed(f, 5)
                    if layer:
                        hold(v, p3["wT_done"], t + 1)
                        v.tensor_copy(wT[:, :], wT_ps).then_inc(p3["wT_copied"], 1)
                    if mix:
                        mixed(f, 6)
                    if layer:
                        hold(v, p3["bo_done"], t + 1)
                        chain(v.tensor_tensor(base[:, :], x3[:, :], hw_ps, ALU.add))
                    if sums:
                        def again(q):
                            chain.restart()
                            local_targets(q, k)
                            for c in range(NCH):
                                masks(q, c)
                        extra_passes(v, first, last, again)
                        chain.restart()
                        hold(v, p3["seg_done"], last * NCH + NCH)
                        chain(v.tensor_copy(ag[:, :], acc[0:PT, 0:C]))
                        chain(v.scalar_tensor_tensor(ag[:, :], acc[0:PT, C:2 * C], 1.0 / LOW, ag[:, :], ALU.mult,
                                                     ALU.add))
                        v.tensor_scalar(ag[:, :], ag[:, :], deg_in[:, bass.ds(k, 1)], None, ALU.mult)\
                            .then_inc(p3["ag_ready"], 1)
                    if mix:
                        mixed(f, 7)
                        v.sem_inc(p3["out_ready"], 1)
                pipeline(v, tile)
        w3.close()
        weights2.close()


_INS = ['x', 'src', 'dst', 'L0_gnn_W', 'L0_gnn_att_src', 'L0_gnn_att_dst', 'L0_gnn_bias', 'L0_ffn_W1', 'L0_ffn_b1',
        'L0_ffn_Wg', 'L0_ffn_bg', 'L0_ffn_Wd', 'L0_ffn_bd', 'L1_gnn_W', 'L1_gnn_b', 'L1_ffn_Wr', 'L1_ffn_br',
        'L1_ffn_W1', 'L1_ffn_b1', 'L1_ffn_g1', 'L1_ffn_be1', 'L1_ffn_m1', 'L1_ffn_v1', 'L1_ffn_W2', 'L1_ffn_b2',
        'L1_ffn_g2', 'L1_ffn_be2', 'L1_ffn_m2', 'L1_ffn_v2', 'L1_ffn_Wo', 'L1_ffn_bo']
_OUTS = [((3125, 256), 'float32')]


def kernel(**inputs):
    import numpy as _np
    import concourse.bacc as _bacc
    from concourse import mybir as _mybir
    from concourse.bass_utils import run_bass_kernel_spmd as _run

    nc = _bacc.Bacc("TRN2", target_bir_lowering=False, num_devices=1)
    arrays, args = {}, []
    for name in _INS:
        a = _np.ascontiguousarray(inputs[name])
        arrays[f"in_{name}_dram"] = a
        args.append(nc.dram_tensor(f"in_{name}_dram", a.shape, _mybir.dt.from_np(a.dtype), kind="ExternalInput").ap())
    for i, (shape, dtype) in enumerate(_OUTS):
        dt = _mybir.dt.from_np(_np.dtype(dtype))
        args.append(nc.dram_tensor(f"out_{i}_dram", shape, dt, kind="ExternalOutput").ap())
    two_block_gnn(nc, *args)
    r = _run(nc, [arrays], core_ids=[0])
    got = tuple(r.results[0][f"out_{i}_dram"] for i in range(len(_OUTS)))
    return got[0]
```
